# Optimizing a Trainium2 kernel written in Bass

```python
import numpy as np
import jax
import jax.numpy as jnp

def _softmax(x, axis=-1):
    return jax.nn.softmax(x, axis=axis)

def _gelu(x):
    return jax.nn.gelu(x, approximate=True)

def _silu(x):
    return jax.nn.silu(x)

def _sigmoid(x):
    return jax.nn.sigmoid(x)

def _layernorm(x, axis=-1, eps=1e-05):
    m = jnp.mean(x, axis=axis, keepdims=True)
    v = jnp.var(x, axis=axis, keepdims=True)
    return (x - m) / jnp.sqrt(v + eps)

def _scatter_add(tgt, idx, src, axis=0):
    return tgt.at[idx].add(src)

def _segment_sum(src, seg, n):
    return jax.ops.segment_sum(src, seg, n)
kernel_name = 'mk_gnn_ffn_d2_gnn_r8_d5473c'

def setup_inputs(seed: int=0):
    np.random.seed(seed)
    _w = jnp.asarray

    def _rec_inputs():
        import jax
        import jax.numpy as jnp
        _gk = jax.random.key(seed)
        x = -6.415e-05 + 1 * jax.random.normal(jax.random.fold_in(_gk, 1), (1250, 1024), jnp.float32)
        src = jax.random.randint(jax.random.fold_in(_gk, 2), (20000,), 0, 1250, jnp.int32)
        dst = jax.random.randint(jax.random.fold_in(_gk, 3), (20000,), 0, 1250, jnp.int32)
        _o = jnp.argsort(dst, stable=True)
        src = src[_o]
        dst = dst[_o]
        return (x, src, dst)
    x, src, dst = _rec_inputs()

    def _L0_gnn_setup():
        import jax, jax.numpy as jnp
        import numpy as np
        NEG_SLOPE = 0.1
        EPS = 1e-05
        key = jax.random.key(seed)
        k1, k2, k3, k4, k5 = jax.random.split(key, 5)
        N, E, DIN, DOUT = (1250, 20000, 1024, 1024)
        x = jax.random.normal(k1, (N, DIN), dtype=jnp.float32)
        W = jax.random.normal(k2, (DIN, DOUT), dtype=jnp.float32) * 0.02
        a = jax.random.normal(k3, (1, 2 * DOUT), dtype=jnp.float32) * 0.02
        src = jax.random.randint(k4, (E,), 0, N, dtype=jnp.int64)
        dst = jax.random.randint(k5, (E,), 0, N, dtype=jnp.int64)
        return {'x': x, 'W': W, 'a': a, 'src': src, 'dst': dst}
    _L0_gnn_all = _L0_gnn_setup()
    _L0_gnn_in = {k: v for k, v in _L0_gnn_all.items() if k in ('W', 'a')}
    del _L0_gnn_all

    def _L0_ffn_setup():
        import jax, jax.numpy as jnp
        import numpy as np
        QMAX = 127.0

        def _ste_round(v):
            return v + jax.lax.stop_gradient(jnp.round(v) - v)

        def _act_fake_quant(x, clip_factor):
            scale = jax.nn.sigmoid(clip_factor) * jnp.max(jnp.abs(x)) / QMAX
            return jnp.clip(_ste_round(x / scale), -QMAX - 1.0, QMAX) * scale

        def _weight_fake_quant(w):
            scale = jnp.max(jnp.abs(w), axis=1, keepdims=True) / QMAX
            return jnp.clip(_ste_round(w / scale), -QMAX - 1.0, QMAX) * scale
        key = jax.random.key(seed)
        k1, k2, k3, k4 = jax.random.split(key, 4)
        B, S, H, I = (8, 1024, 1024, 352)
        return {'x': jax.random.normal(k1, (B, S, H), dtype=jnp.float32), 'clip_x': jnp.full((1,), 4.0, dtype=jnp.float32), 'clip_down': jnp.full((1,), 4.0, dtype=jnp.float32), 'w_gate': jax.random.normal(k2, (I, H), dtype=jnp.float32) * 0.02, 'w_up': jax.random.normal(k3, (I, H), dtype=jnp.float32) * 0.02, 'w_down': jax.random.normal(k4, (H, I), dtype=jnp.float32) * 0.02}
    _L0_ffn_all = _L0_ffn_setup()
    _L0_ffn_in = {k: v for k, v in _L0_ffn_all.items() if k in ('clip_x', 'clip_down', 'w_gate', 'w_up', 'w_down')}
    del _L0_ffn_all

    def _L1_gnn_setup():
        import jax, jax.numpy as jnp
        import numpy as np
        N_DIAS = 64
        L = 60
        N = N_DIAS * L
        E = N_DIAS * L * (L - 1)
        D = 1024
        H = 512
        K = 4

        def _build_edges():
            idx = np.arange(L)
            src = np.repeat(idx, L)
            dst = np.tile(idx, L)
            m = src != dst
            src, dst = (src[m], dst[m])
            offs = (np.arange(N_DIAS) * L)[:, None]
            row = (src[None, :] + offs).reshape(-1)
            col = (dst[None, :] + offs).reshape(-1)
            return (row.astype(np.int32), col.astype(np.int32))
        key = jax.random.key(seed)
        k0, k1, k2 = jax.random.split(key, 3)
        row, col = _build_edges()
        return {'emotions_feat': jax.random.normal(k0, (N, D), jnp.float32), 'W1': jax.random.normal(k1, (D, H), jnp.float32) * 0.02, 'b1': jnp.zeros((H,), jnp.float32), 'Wg': jax.random.normal(k2, (K, 2 * H, 1), jnp.float32) * 0.02, 'bg': jnp.zeros((K, 1), jnp.float32), 'row': jnp.asarray(row), 'col': jnp.asarray(col)}
    _L1_gnn_all = _L1_gnn_setup()
    _L1_gnn_in = {k: v for k, v in _L1_gnn_all.items() if k in ('W1', 'b1', 'Wg', 'bg')}
    del _L1_gnn_all

    def _L1_ffn_setup():
        import jax, jax.numpy as jnp
        import numpy as np
        import math
        D_MODEL = 1024
        N_EXPERTS = 16
        D_FF = 512
        CAP_FACTOR = 1.25
        MIN_CAPACITY = 4

        def _capacity(num_tokens, num_experts):
            cap = math.floor(CAP_FACTOR * num_tokens / num_experts)
            cap += cap % 2
            return max(cap, MIN_CAPACITY)

        def _top1_router(gate_logits, capacity):
            s, e = gate_logits.shape
            probs = jax.nn.softmax(gate_logits, axis=-1)
            top1 = jnp.argmax(gate_logits, axis=-1)
            mask = jax.nn.one_hot(top1, e, dtype=jnp.int32)
            ranks = jnp.cumsum(mask, axis=0) - 1
            mask = mask * (ranks < capacity).astype(jnp.int32)
            rank1 = jnp.sum(mask * ranks, axis=-1)
            ranks_oh = jax.nn.one_hot(rank1, capacity, dtype=probs.dtype)
            weight = mask.astype(probs.dtype) * probs
            combine_weights = weight[:, :, None] * ranks_oh[:, None, :]
            sec_mask = combine_weights > 0
            return (combine_weights, sec_mask)
        key = jax.random.key(seed)
        k1, k2, k3, k4 = jax.random.split(key, 4)
        x = jax.random.normal(k1, (4, 256, D_MODEL), dtype=jnp.float32)
        gate_w = jax.random.normal(k2, (N_EXPERTS, D_MODEL), dtype=jnp.float32) * math.sqrt(0.1 / D_MODEL)
        w1 = jax.random.normal(k3, (N_EXPERTS, D_MODEL, D_FF), dtype=jnp.float32) * (1.0 / math.sqrt(D_MODEL))
        w2 = jax.random.normal(k4, (N_EXPERTS, D_FF, D_MODEL), dtype=jnp.float32) * (1.0 / math.sqrt(D_FF))
        return {'x': x, 'gate_w': gate_w, 'w1': w1, 'w2': w2}
    _L1_ffn_all = _L1_ffn_setup()
    _L1_ffn_in = {k: v for k, v in _L1_ffn_all.items() if k in ('gate_w', 'w1', 'w2')}
    del _L1_ffn_all
    return {'x': x, 'src': src, 'dst': dst, 'L0_gnn_W': _L0_gnn_in['W'], 'L0_gnn_a': _L0_gnn_in['a'], 'L0_ffn_clip_x': _L0_ffn_in['clip_x'], 'L0_ffn_clip_down': _L0_ffn_in['clip_down'], 'L0_ffn_w_gate': _L0_ffn_in['w_gate'], 'L0_ffn_w_up': _L0_ffn_in['w_up'], 'L0_ffn_w_down': _L0_ffn_in['w_down'], 'L1_gnn_W1': _L1_gnn_in['W1'], 'L1_gnn_b1': _L1_gnn_in['b1'], 'L1_gnn_Wg': _L1_gnn_in['Wg'], 'L1_gnn_bg': _L1_gnn_in['bg'], 'L1_ffn_gate_w': _L1_ffn_in['gate_w'], 'L1_ffn_w1': _L1_ffn_in['w1'], 'L1_ffn_w2': _L1_ffn_in['w2']}

def reference(x, src, dst, L0_gnn_W, L0_gnn_a, L0_ffn_clip_x, L0_ffn_clip_down, L0_ffn_w_gate, L0_ffn_w_up, L0_ffn_w_down, L1_gnn_W1, L1_gnn_b1, L1_gnn_Wg, L1_gnn_bg, L1_ffn_gate_w, L1_ffn_w1, L1_ffn_w2):
    import jax
    import jax.numpy as jnp

    def _L0_gnn_ref(x, W, a, src, dst):
        import jax, jax.numpy as jnp
        import numpy as np
        NEG_SLOPE = 0.1
        EPS = 1e-05
        N = x.shape[0]
        d = W.shape[1]
        h = x @ W
        a_l, a_r = (a[0, :d], a[0, d:])
        al = h @ a_l
        ar = h @ a_r
        e = jnp.exp(-jax.nn.leaky_relu(al[src] + ar[dst], negative_slope=NEG_SLOPE))
        rowsum = jax.ops.segment_sum(e, src, num_segments=N)
        h_prime = jax.ops.segment_sum(e[:, None] * h[dst], src, num_segments=N)
        h_prime = h_prime / (rowsum[:, None] + EPS)
        return jax.nn.elu(h_prime)

    def _L0_ffn_ref(x, clip_x, clip_down, w_gate, w_up, w_down):
        import jax, jax.numpy as jnp
        import numpy as np
        QMAX = 127.0

        def _ste_round(v):
            return v + jax.lax.stop_gradient(jnp.round(v) - v)

        def _act_fake_quant(x, clip_factor):
            scale = jax.nn.sigmoid(clip_factor) * jnp.max(jnp.abs(x)) / QMAX
            return jnp.clip(_ste_round(x / scale), -QMAX - 1.0, QMAX) * scale

        def _weight_fake_quant(w):
            scale = jnp.max(jnp.abs(w), axis=1, keepdims=True) / QMAX
            return jnp.clip(_ste_round(w / scale), -QMAX - 1.0, QMAX) * scale
        xq = _act_fake_quant(x, clip_x[0])
        gate = jnp.einsum('bsh,ih->bsi', xq, _weight_fake_quant(w_gate))
        up = jnp.einsum('bsh,ih->bsi', xq, _weight_fake_quant(w_up))
        h = _act_fake_quant(jax.nn.silu(gate) * up, clip_down[0])
        return jnp.einsum('bsi,hi->bsh', h, _weight_fake_quant(w_down))

    def _L1_gnn_ref(emotions_feat, W1, b1, Wg, bg, row, col):
        import jax, jax.numpy as jnp
        import numpy as np
        N_DIAS = 64
        L = 60
        N = N_DIAS * L
        E = N_DIAS * L * (L - 1)
        D = 1024
        H = 512
        K = 4

        def _build_edges():
            idx = np.arange(L)
            src = np.repeat(idx, L)
            dst = np.tile(idx, L)
            m = src != dst
            src, dst = (src[m], dst[m])
            offs = (np.arange(N_DIAS) * L)[:, None]
            row = (src[None, :] + offs).reshape(-1)
            col = (dst[None, :] + offs).reshape(-1)
            return (row.astype(np.int32), col.astype(np.int32))
        n = emotions_feat.shape[0]
        x1 = emotions_feat @ W1 + b1
        h = x1.shape[1]
        deg = jax.ops.segment_sum(jnp.ones_like(col, x1.dtype), col, num_segments=n)
        dis = jnp.clip(deg, 1.0) ** (-0.5)
        norm = dis[row] * dis[col]
        gnn = x1
        for k in range(Wg.shape[0]):
            Wi, Wj = (Wg[k, :h], Wg[k, h:])
            x_i = gnn[col]
            x_j = gnn[row]
            alpha = jnp.tanh(x_i @ Wi + x_j @ Wj + bg[k])
            msg = norm[:, None] * alpha * x_j
            agg = jax.ops.segment_sum(msg, col, num_segments=n)
            gnn = gnn + agg
        return jnp.concatenate([x1, gnn], axis=1)

    def _L1_ffn_ref(x, gate_w, w1, w2):
        import jax, jax.numpy as jnp
        import numpy as np
        import math
        D_MODEL = 1024
        N_EXPERTS = 16
        D_FF = 512
        CAP_FACTOR = 1.25
        MIN_CAPACITY = 4

        def _capacity(num_tokens, num_experts):
            cap = math.floor(CAP_FACTOR * num_tokens / num_experts)
            cap += cap % 2
            return max(cap, MIN_CAPACITY)

        def _top1_router(gate_logits, capacity):
            s, e = gate_logits.shape
            probs = jax.nn.softmax(gate_logits, axis=-1)
            top1 = jnp.argmax(gate_logits, axis=-1)
            mask = jax.nn.one_hot(top1, e, dtype=jnp.int32)
            ranks = jnp.cumsum(mask, axis=0) - 1
            mask = mask * (ranks < capacity).astype(jnp.int32)
            rank1 = jnp.sum(mask * ranks, axis=-1)
            ranks_oh = jax.nn.one_hot(rank1, capacity, dtype=probs.dtype)
            weight = mask.astype(probs.dtype) * probs
            combine_weights = weight[:, :, None] * ranks_oh[:, None, :]
            sec_mask = combine_weights > 0
            return (combine_weights, sec_mask)
        tokens = x.reshape(-1, D_MODEL)
        s = tokens.shape[0]
        capacity = _capacity(s, N_EXPERTS)
        gate_logits = tokens.astype(jnp.float32) @ gate_w.T
        combine_weights, sec_mask = _top1_router(gate_logits, capacity)
        dispatch = jnp.einsum('sec,sd->ecd', sec_mask.astype(tokens.dtype), tokens)
        h = jax.nn.gelu(jnp.einsum('ecd,edf->ecf', dispatch, w1))
        expert_out = jnp.einsum('ecf,efd->ecd', h, w2)
        out = jnp.einsum('sec,ecd->sd', combine_weights.astype(tokens.dtype), expert_out)
        return out.reshape(x.shape)
    x = x + _L0_gnn_ref(_layernorm(x, axis=-1), L0_gnn_W, L0_gnn_a, src, dst)
    x = x + _L0_ffn_ref(_layernorm(x, axis=-1)[None], L0_ffn_clip_x, L0_ffn_clip_down, L0_ffn_w_gate, L0_ffn_w_up, L0_ffn_w_down)[0]
    x = x + _L1_gnn_ref(_layernorm(x, axis=-1), L1_gnn_W1, L1_gnn_b1, L1_gnn_Wg, L1_gnn_bg, src, dst)
    x = x + _L1_ffn_ref(_layernorm(x, axis=-1)[None], L1_ffn_gate_w, L1_ffn_w1, L1_ffn_w2)[0]
    return x

_drawn_inputs = setup_inputs


def setup_inputs(seed=0):
    import zlib

    import numpy as np

    out = dict(_drawn_inputs(seed))
    spreads = {'L1_gnn_b1': (0.0, 0.1), 'L1_gnn_bg': (0.0, 0.1)}
    factors = {}
    for name, (base, spread) in spreads.items():
        noise = np.random.default_rng([zlib.crc32(name.encode()), seed]).standard_normal(out[name].shape)
        drawn = base * np.exp(spread * noise) if base else spread * noise
        out[name] = jnp.asarray(drawn.astype(out[name].dtype))
    for name, factor in factors.items():
        out[name] = (out[name] * factor).astype(out[name].dtype)
    return out
```

```python
from contextlib import ExitStack

import concourse.bass as bass
from concourse import mybir

ALU = mybir.AluOpType
ACT = mybir.ActivationFunctionType
AX_X = mybir.AxisListType.X
AX_XY = mybir.AxisListType.XY
F32 = mybir.dt.float32
F16 = mybir.dt.float16
BF16 = mybir.dt.bfloat16
I16 = mybir.dt.int16
I32 = mybir.dt.int32
U32 = mybir.dt.uint32
RMAX = bass.bass_isa.ReduceOp.absmax

P = 128
EPS = 1e-5
MAGIC = 1.5 * 2.0 ** 23
X_SCALE, W_SCALE = 2.0 ** 8, 2.0 ** 10
G_SCALE = 2.0 ** 6
A_SCALE = 2.0 ** 11
NO_NODE = 4096.0
QMAX = 127.0


class Steps:

    def __init__(self, eng, sem):
        self.eng, self.sem, self.base, self.n = eng, sem, 0, 0

    def __call__(self, ins):
        ins.then_inc(self.sem, 1)
        self.n += 1

    def wait(self):
        self.eng.wait_ge(self.sem, self.base + self.n)

    def link(self, ins):
        self(ins)
        self.wait()

    def enter(self, item, per, items=1):
        self.start, self.per, self.items = self.base + self.n, per, items
        self.base, self.n = item * per + self.start, 0

    def leave(self, total):
        assert self.n == self.per * self.items, (self.n, self.per, self.items)
        self.base, self.n = self.start + total * self.per, 0


CREDIT = 2


def done(i):
    return i + (1 + CREDIT)


def freed(i):
    return i + 1


def wait_from(eng, sem, count):
    if not (isinstance(count, int) and count <= 0):
        eng.wait_ge(sem, count)


def pairs(eng, n):
    return eng.Fori(0, n - 1, 2)


def gnn_moe_kernel(nc, x, src, dst, L0_gnn_W, L0_gnn_a, L0_ffn_clip_x, L0_ffn_clip_down, L0_ffn_w_gate,
                   L0_ffn_w_up, L0_ffn_w_down, L1_gnn_W1, L1_gnn_b1, L1_gnn_Wg, L1_gnn_bg,
                   L1_ffn_gate_w, L1_ffn_w1, L1_ffn_w2, out, x_rows):
    N, D = x.shape
    E = src.shape[0]
    NT = -(-N // P)
    NP = NT * P
    LAST = N - (NT - 1) * P
    KD = D // P
    ET = -(-E // P)
    EA = ET - P
    HD = D // 2
    FF = L0_ffn_w_gate.shape[0]
    FC = -(-FF // P)
    H1 = L1_gnn_W1.shape[1]
    K1 = L1_gnn_Wg.shape[0]
    NE = L1_ffn_gate_w.shape[0]
    CAP = int(1.25 * N / NE)
    CAP += CAP % 2
    assert (NT % 2, LAST > 0, H1, HD, KD) == (0, True, 512, 512, 8) and P < ET <= 2 * P - 4

    ctx = ExitStack()
    with ctx:
        def sb(name, shape, dt):
            return ctx.enter_context(nc.sbuf_tensor(name, shape, dt))

        def sem(name):
            return ctx.enter_context(nc.semaphore(name))

        arena = sb("arena", [P, 32768], F32)
        X = sb("X", [P, NT, D], F32)
        STG = sb("STG", [P, 4096], F32)
        BD = sb("BD", [P, 2 * NP], F32)
        PS = ctx.enter_context(nc.psum_tensor("PS", [P, 8, 512], F32))

        def part(at, size, dt=F32):
            a = arena[:, at:at + size]
            return a if dt is F32 else a.bitcast(dt)

        HB0 = 0
        CC0 = NT * D + 256
        CT0 = CC0 + NT * NP // 2
        GW0 = CT0 + NT * NP // 2
        C = part(CC0, NT * NP // 2, I16).rearrange("p (t n) -> p t n", t=NT)
        CT = part(CT0, NT * NP // 2, I16).rearrange("p (t n) -> p t n", t=NT)
        hbuf = part(HB0, NT * D).rearrange("p (t d) -> p t d", t=NT)
        ct_stage = part(HB0 + (NT - 1) * D, NP)
        W_raw = part(HB0, KD * D).rearrange("p (k n) -> p k n", k=KD)
        W_hi = part(GW0, KD * D // 2, F16).rearrange("p (k n) -> p k n", k=KD)
        W_lo = part(GW0 + KD * D // 2, KD * D // 2, F16).rearrange("p (k n) -> p k n", k=KD)
        junk = part(GW0 + KD * D, D)
        xn_stage = STG[:, 0:2 * D].rearrange("p (b d) -> p b d", b=2)
        xnT_stage = STG[:, 2 * D:4 * D].rearrange("p (b k n) -> p b k n", b=2, k=KD)
        ln_x = STG[:, D:2 * D]
        x_parts = STG[:, 2 * D:3 * D].bitcast(F16).rearrange("p (s d) -> p s d", s=2)
        xT_parts = STG[:, 3 * D:4 * D].bitcast(F16).rearrange("p (s k n) -> p s k n", s=2, k=KD)
        a_row = BD[:, 0:2 * D].rearrange("p (s d) -> p s d", s=2)
        alb = BD[:, 0:NP]
        diag = BD[:, NP:2 * NP]

        AT = STG[:, 0:2 * NP].rearrange("p (b t n) -> p b t n", b=2, t=NT)
        S = STG[:, 2 * NP:3 * NP].rearrange("p (t n) -> p t n", t=NT)
        FFP = FC * P
        wguT = part(GW0, KD * 2 * FFP // 2, BF16).rearrange("p (k s f) -> p k s f", k=KD, s=2)
        wdT = part(GW0 + 3072, FC * D // 2, BF16).rearrange("p (c d) -> p c d", c=FC)
        w_raw = part(GW0 + 4608, 2 * D).rearrange("p (b d) -> p b d", b=2)
        w_q = part(GW0 + 6656, D, BF16).rearrange("p (b d) -> p b d", b=2)
        tmp_m = part(GW0 + 7680, D)
        tmp_p = BD[:, NP:NP + D]
        gu_tmp = w_raw[:, :, 0:320]
        xqT = part(HB0, KD * NP // 2, BF16).rearrange("p (k n) -> p k n", k=KD)
        xq_stage = STG[:, 2 * D:3 * D].bitcast(BF16).rearrange("p (b d) -> p b d", b=2)
        hT = part(HB0 + 5120, FC * NP).rearrange("p (c n) -> p c n", c=FC)
        hq = part(HB0, FC * NP // 2, BF16).rearrange("p (c n) -> p c n", c=FC)

        W1_raw = part(CT0, KD * H1).rearrange("p (k n) -> p k n", k=KD)
        W1_hi = STG[:, 0:KD * H1 // 2].bitcast(F16).rearrange("p (k n) -> p k n", k=KD)
        W1_lo = STG[:, KD * H1 // 2:KD * H1].bitcast(F16).rearrange("p (k n) -> p k n", k=KD)
        G = part(HB0, NT * H1).rearrange("p (t h) -> p t h", t=NT)
        L0 = HB0 + NT * H1
        ln2 = part(L0, D)
        parts2 = part(L0 + D, 2 * D, F16).rearrange("p (b s d) -> p b s d", b=2, s=2)
        partsT2 = part(L0 + 3 * D, 2 * D, F16).rearrange("p (b s k n) -> p b s k n", b=2, s=2, k=KD)
        b1_row = part(CT0 + 4096, H1)
        wg_row = part(CT0 + 4608, 2 * H1).rearrange("p (s h) -> p s h", s=2)
        GS = part(CT0 + 5632, 2 * NT * H1, F16).rearrange("p (q s t h) -> p q s t h", q=2, s=2, t=NT)
        gs_raw = part(CT0, H1)
        SS = part(CT0 + H1, 2 * NP).rearrange("p (b t n) -> p b t n", b=2, t=NT)
        AP = STG[:, 0:2 * NP].bitcast(F16).rearrange("p (b s t n) -> p b s t n", b=2, s=2, t=NT)
        agg_row = part(CT0 + H1 + 2 * NP, H1)
        dot_out = BD[:, NP:NP + H1]
        W1E = arena[:].rearrange("p (b s k f) -> p b s k f", b=4, s=2, f=512)[:, :, 0]
        W2E = arena[:].rearrange("p (b s m) -> p b s m", b=4, s=2)[:, :, 1].rearrange("p b (k d) -> p b k d", k=4)
        Xf = X[:].rearrange("p t d -> p (t d)")
        xg = Xf[0:CAP, 0:4 * D].rearrange("p (b d) -> p b d", b=4)
        xgn = Xf[0:CAP, 4 * D:6 * D].rearrange("p (b d) -> p b d", b=2)
        xgT = Xf[:, 6 * D:6 * D + 2 * KD * CAP].rearrange("p (b k c) -> p b k c", b=2, k=KD)
        ge = Xf[0:CAP, 8 * D:9 * D].rearrange("p (b f) -> p b f", b=2)
        geT = Xf[:, 9 * D:9 * D + 8 * CAP].rearrange("p (b k c) -> p b k c", b=2, k=4)
        o_stage = BD[0:CAP, 0:2 * D].rearrange("p (b d) -> p b d", b=2)
        gw_raw = BD[0:NE, 0:D]
        gwT = BD[:, D:D + KD * NE].rearrange("p (k e) -> p k e", k=KD)
        NR = 5 * NE
        slot_of = STG[:, 0:NT * CAP].rearrange("p (t c) -> p t c", t=NT)
        facts = STG[:, 2 * D:2 * D + NT * NR].rearrange("p (t q e) -> p t q e", t=NT, q=5)

        def route(i):
            return STG[:, 3 * D + i * NT * NE:3 * D + (i + 1) * NT * NE].rearrange("p (t e) -> p t e", t=NT)

        ident = sb("ident", [P, P], F32)
        tri = sb("tri", [P, P], F32)
        node_id = sb("node_id", [P, NT], F32)
        exp_id = sb("exp_id", [P, NE], F32)
        dis_in = sb("dis_in", [P, NT], F32)
        dis_out = sb("dis_out", [P, NT], F32)
        dis = sb("dis", [P, NT], F32)
        bg_row = sb("bg_row", [P, K1], F32)
        U = sb("U", [P, NT], F32)
        UB = sb("UB", [P, NT], F32)
        V = sb("V", [P, 2, NT], F32)
        LG = sb("LG", [P, NT, NE], F32)
        lg_top = sb("lg_top", [P, NT], F32)
        valid = sb("valid", [P, NT], F32)
        first = sb("first", [P, NT], F32)
        wt = sb("wt", [P, NT], F32)
        rank1 = sb("rank1", [P, NT], F32)
        slots = sb("slots", [P, 5, NE], F32)
        take = sb("take", [P, NE], I32)
        give = sb("give", [P, NE], I32)
        away = sb("away", [P, NE], F32)
        identb = sb("identb", [P, P], BF16)
        identh = sb("identh", [P, P], F16)
        st_one = sb("st_one", [P, 2, 6], F32)
        mv_one = sb("mv_one", [P, 2], F32)
        neg_mean = sb("neg_mean", [P, NT], F32)
        ones = sb("ones", [P, P], F32)
        zerosb = sb("zerosb", [P, 512], BF16)
        iota_n = sb("iota_n", [P, NP], F16)
        OH = 4
        oh_dst = sb("oh_dst", [P, OH, P], BF16)
        oh_src = sb("oh_src", [P, OH, NP], BF16)
        edges_i = STG[:, 0:4 * P].bitcast(I32).rearrange("p (s h e) -> p s h e", s=2, h=2)
        edges_f = STG[:, 4 * P:8 * P].rearrange("p (s h e) -> p s h e", s=2, h=2)
        edgeT = sb("edgeT", [P, 2, 2 * P], F32)
        tile_lo = sb("tile_lo", [P, 2], F32)
        tile_hi = sb("tile_hi", [P, 2], F32)
        tile_id = sb("tile_id", [P, 2], F32)
        block_lo = sb("block_lo", [P, NT], F32)
        cross = sb("cross", [P, 2, 2, NT], F32)
        rng_f = sb("rng_f", [P, 2, 2, NT], F32)
        rng_c = sb("rng_c", [NT, 2], F32)
        rng_i = sb("rng_i", [1, 2 * NT], I32)
        deg = sb("deg", [P, NT], F32)
        bst = sb("bst", [P, NT, 2, 6], F32)
        MV = sb("MV", [P, NT, 2], F32)
        var_e = sb("var_e", [P, NT], F32)
        neg_half = sb("neg_half", [P, NT], F32)
        RSTD = sb("RSTD", [P, NT], F32)
        NMR = sb("NMR", [P, NT], F32)
        AL = sb("AL", [P, 2, NT], F32)

        at_sum = sb("at_sum", [P, 2, P], F32)
        rs = sb("rs", [P, 2], F32)
        w_max = sb("w_max", [P, 16], F32)
        w_inv = sb("w_inv", [P, 16], F32)
        clips = sb("clips", [P, 2], F32)
        sig = sb("sig", [P, 2], F32)
        x_max = sb("x_max", [P, NT], F32)
        x_min = sb("x_min", [P, NT], F32)
        top = sb("top", [P, 4], F32)
        s_act = sb("s_act", [P, 4], F32)
        qscale = sb("qscale", [P, NT], F32)
        qbias = sb("qbias", [P, NT], F32)
        s_half = sb("s_half", [P, FC], F32)
        s_gu = sb("s_gu", [P, FC], F32)
        s_down = sb("s_down", [P, KD], F32)

        x_first_in = sem("x_first_in")
        x_in = sem("x_in")
        w_hi_ready = sem("w_hi_ready")
        w_lo_ready = sem("w_lo_ready")
        stats_ready = sem("stats_ready")
        norm_ready = sem("norm_ready")
        ln_ready = sem("ln_ready")
        hi_ready = sem("hi_ready")
        lo_ready = sem("lo_ready")
        parts_psum = sem("parts_psum")
        partsT_ready = sem("partsT_ready")
        w_in = sem("w_in")
        a_in = sem("a_in")
        edges_in = sem("edges_in")
        pad_set = sem("pad_set")
        consts = sem("consts")
        pool_s = sem("pool_s")
        dve_s = sem("dve_s")
        act_s = sem("act_s")
        edges_ready = sem("edges_ready")
        edgeT_psum = sem("edgeT_psum")
        rng_ready = sem("rng_ready")
        rngT_psum = sem("rngT_psum")
        rng_col = sem("rng_col")
        rng_row_psum = sem("rng_row_psum")
        rng_row = sem("rng_row")
        oh_ready = sem("oh_ready")
        oh_free = sem("oh_free")
        ct_psum = sem("ct_psum")
        ct_psum_free = sem("ct_psum_free")
        ct_staged = sem("ct_staged")
        ct_stored = sem("ct_stored")
        c_psum = sem("c_psum")
        c_stored = sem("c_stored")
        var_ready = sem("var_ready")
        rstd_ready = sem("rstd_ready")
        nmr_ready = sem("nmr_ready")
        xn_ready = sem("xn_ready")
        xn_free = sem("xn_free")
        xnT_psum = sem("xnT_psum")
        xnT_ready = sem("xnT_ready")
        xnT_free = sem("xnT_free")
        h_psum = sem("h_psum")
        h_ready = sem("h_ready")
        clips_in = sem("clips_in")
        wraw_in0 = sem("wraw_in0")
        wraw_in1 = sem("wraw_in1")
        diag_ready = sem("diag_ready")
        row_psum = sem("row_psum")
        row_stored = sem("row_stored")
        sum_ready = sem("sum_ready")
        act_out = sem("act_out")
        at_ready = sem("at_ready")
        agg_psum = sem("agg_psum")
        m_ready = sem("m_ready")
        e_ready = sem("e_ready")
        x_updated = sem("x_updated")
        w_scaled = sem("w_scaled")
        w_rounded = sem("w_rounded")
        wT_psum = sem("wT_psum")
        wT_stored = sem("wT_stored")
        sig_ready = sem("sig_ready")
        max_ready = sem("max_ready")
        max_all = sem("max_all")
        qs_ready = sem("qs_ready")
        y_ready = sem("y_ready")
        yq_ready = sem("yq_ready")
        yT_psum = sem("yT_psum")
        yT_stored = sem("yT_stored")
        gu_psum = sem("gu_psum")
        tanh_ready = sem("tanh_ready")
        hT_ready = sem("hT_ready")
        hmax_ready = sem("hmax_ready")
        hmax_all = sem("hmax_all")
        hq_ready = sem("hq_ready")
        d_psum = sem("d_psum")
        d_scaled = sem("d_scaled")
        d_added = sem("d_added")

        wpad_set = sem("wpad_set")


        NG, GN = NP // 320, 320
        W_ITEMS = 2 * FC + KD // 2
        assert W_ITEMS == NT
        w1_in = sem("w1_in")
        b1_in = sem("b1_in")
        wg_in = sem("wg_in")
        dis_deg = sem("dis_deg")
        dis_ready = sem("dis_ready")
        dis_scaled = sem("dis_scaled")
        w1_scaled = sem("w1_scaled")
        w1_hi_ready = sem("w1_hi_ready")
        w1_lo_ready = sem("w1_lo_ready")
        hi2_ready = sem("hi2_ready")
        lo2_ready = sem("lo2_ready")
        parts2_psum = sem("parts2_psum")
        parts2T_ready = sem("parts2T_ready")
        gs_made = sem("gs_made")
        tanh2_ready = sem("tanh2_ready")
        aw_ready = sem("aw_ready")
        aw_hi_ready = sem("aw_hi_ready")
        aw_lo_ready = sem("aw_lo_ready")
        at_summed = sem("at_summed")
        x1_psum = sem("x1_psum")
        x1_ready = sem("x1_ready")
        gs_ready = sem("gs_ready")
        uv_ready = sem("uv_ready")
        sum2_ready = sem("sum2_ready")
        agg2_psum = sem("agg2_psum")
        g_ready = sem("g_ready")
        xl_added = sem("xl_added")
        x_final = sem("x_final")
        rows_out = sem("rows_out")
        gw_in = sem("gw_in")
        gwT_psum = sem("gwT_psum")
        gwT_ready = sem("gwT_ready")
        lg_psum = sem("lg_psum")
        lg_ready = sem("lg_ready")
        soft_in = sem("soft_in")
        soft_out = sem("soft_out")
        mask_ready = sem("mask_ready")
        rank_psum = sem("rank_psum")
        cast_ready = sem("cast_ready")
        slots_psum = sem("slots_psum")
        slots_ready = sem("slots_ready")
        we1_in0 = sem("we1_in0")
        we1_in1 = sem("we1_in1")
        we2_in0 = sem("we2_in0")
        we2_in1 = sem("we2_in1")
        got0 = sem("got0")
        got1 = sem("got1")
        got2 = sem("got2")
        got3 = sem("got3")
        xgn_ready = sem("xgn_ready")
        xgT_psum = sem("xgT_psum")
        xgT_ready = sem("xgT_ready")
        m1_psum = sem("m1_psum")
        ge_ready = sem("ge_ready")
        geT_psum = sem("geT_psum")
        geT_ready = sem("geT_ready")
        m2_psum = sem("m2_psum")
        o_ready = sem("o_ready")
        sent0 = sem("sent0")
        sent1 = sem("sent1")

        CONSTS = 13
        CG = -(-NT // 4)

        block = ctx.enter_context(nc.Block())

        @block.sync
        def _(sp):
            for s in (oh_free, xn_ready, xnT_psum, xnT_ready,
                      act_out, at_ready, agg_psum, x_updated, w_rounded, wT_psum, wT_stored, y_ready, yq_ready, yT_psum,
                      yT_stored, gu_psum, tanh_ready, hT_ready, d_psum, d_scaled, d_added, x1_psum, x1_ready, hi2_ready, lo2_ready, parts2_psum, parts2T_ready,
                      gs_ready, gs_made, aw_ready, aw_hi_ready, aw_lo_ready, agg2_psum, g_ready, lg_psum,
                      lg_ready, xgn_ready, xgT_psum, xgT_ready, m1_psum, ge_ready, geT_psum, geT_ready, m2_psum, o_ready):
                sp.sem_inc(s, CREDIT)
            for s in (we1_in0, we1_in1, we2_in0, we2_in1):
                sp.sem_inc(s, 16)
            sp.wait_ge(pad_set, 1)
            for s, e in enumerate((dst, src)):
                full = P * P
                rows = (E - full) // P
                rest = E - full - rows * P
                sp.dma_start(edges_i[:, s, 0, :], e[0:full].rearrange("(t e) -> t e", e=P)).then_inc(edges_in, 16)
                sp.dma_start(edges_i[0:rows, s, 1, :],
                             e[full:full + rows * P].rearrange("(t e) -> t e", e=P)).then_inc(edges_in, 16)
                if rest:
                    sp.dma_start(edges_i[rows:rows + 1, s, 1, 0:rest],
                                 e[E - rest:E].rearrange("(t e) -> t e", t=1)).then_inc(edges_in, 16)
            sp.wait_ge(pad_set, 2)
            sp.dma_start(X[:, 0:2, :], x[0:2 * P, :].rearrange("(t p) d -> p t d", p=P)).then_inc(x_first_in, 16)
            sp.dma_start(W_raw, L0_gnn_W.rearrange("(k p) n -> p k n", p=P)).then_inc(w_in, 16)
            sp.dma_start(X[:, 2:NT - 1, :],
                         x[2 * P:(NT - 1) * P, :].rearrange("(t p) d -> p t d", p=P)).then_inc(x_in, 16)
            sp.dma_start(X[0:LAST, NT - 1, :], x[(NT - 1) * P:N, :]).then_inc(x_in, 16)
            for i, clip in enumerate((L0_ffn_clip_x, L0_ffn_clip_down)):
                sp.dma_start(clips[:, i:i + 1], clip.partition_broadcast(P)).then_inc(clips_in, 16)
            sp.dma_start(a_row.rearrange("p s d -> p (s d)"), L0_gnn_a[0, :].partition_broadcast(P)).then_inc(a_in, 16)

            sp.wait_ge(h_psum, NT)
            for i in range(W_ITEMS):
                b = i % 2
                sp.wait_ge(w_rounded, freed(i))
                sem_b = (wraw_in0, wraw_in1)[b]
                if i < 2 * FC:
                    w = (L0_ffn_w_gate, L0_ffn_w_up)[i % 2]
                    r0 = i // 2 * P
                    n = min(P, FF - r0)
                    if n < P:
                        sp.wait_ge(wpad_set, i % 2 + 1)
                    sp.dma_start(w_raw[0:n, b, :], w[r0:r0 + n, :]).then_inc(sem_b, 16)
                else:
                    r0 = (i - 2 * FC) * 2 * P
                    sp.dma_start(w_raw[:, b, 0:2 * FF].rearrange("p (r f) -> p r f", r=2),
                                 L0_ffn_w_down[r0:r0 + 2 * P, :].rearrange("(r p) f -> p r f", p=P)
                                 ).then_inc(sem_b, 16)


            sp.wait_ge(x_updated, NT + CREDIT)
            sp.dma_start(W1_raw, L1_gnn_W1.rearrange("(k p) n -> p k n", p=P)).then_inc(w1_in, 16)
            sp.dma_start(b1_row, L1_gnn_b1.partition_broadcast(P)).then_inc(b1_in, 16)
            sp.dma_start(bg_row[:], L1_gnn_bg.rearrange("k o -> (k o)").partition_broadcast(P)).then_inc(b1_in, 16)
            for k in range(K1):
                if k:
                    sp.wait_ge(uv_ready, k * NT)
                sp.dma_start(wg_row.rearrange("p s h -> p (s h)"),
                             L1_gnn_Wg[k].rearrange("h o -> (h o)").partition_broadcast(P)).then_inc(wg_in, 16)

            for t in range(NT):
                n = min(P, N - t * P)
                sp.wait_ge(x_final, t + 1)
                sp.dma_start(x_rows[t * P:t * P + n, :], X[0:n, t, :]).then_inc(rows_out, 16)
                sp.dma_start(out[t * P:t * P + n, :], X[0:n, t, :]).then_inc(rows_out, 16)
            sp.dma_start(gw_raw, L1_ffn_gate_w).then_inc(gw_in, 16)

            def load_expert(e, j):
                sp.wait_ge(m2_psum, e + (j - 1))
                for w, m, s, k in ((L1_ffn_w1, W1E, (we1_in0, we1_in1)[j], KD), (L1_ffn_w2, W2E, (we2_in0, we2_in1)[j], 4)):
                    sp.wait_ge(s, (e // 2 + 1) * 16)
                    sp.dma_start(m[:, bass.ds((e + j) % 4, 1)].squeeze(1),
                                 w[bass.ds(e + j, 1)].rearrange("o (k p) f -> p (o k) f", p=P)).then_inc(s, 16)

            for e in range(0, 4, 2):
                for j in range(2):
                    for w, m, s, k in ((L1_ffn_w1, W1E, (we1_in0, we1_in1)[j], KD), (L1_ffn_w2, W2E, (we2_in0, we2_in1)[j], 4)):
                        sp.wait_ge(s, (e // 2 + 1) * 16)
                        sp.dma_start(m[:, e + j], w[e + j].rearrange("(k p) f -> p k f", p=P)).then_inc(s, 16)
            with sp.Fori(4, NE - 1, 2) as e:
                load_expert(e, 0)
                load_expert(e, 1)

            sp.wait_ge(rows_out, 2 * NT * 16)
            sp.wait_ge(sent0, NE // 2 * 16)
            sp.wait_ge(sent1, NE // 2 * 16)

        @block.gpsimd
        def _(pool):
            nc.gpsimd.memset(edges_i[:, :, 1, :], int(NO_NODE)).then_inc(pad_set, 1)
            nc.gpsimd.memset(X[:, NT - 1, :], 0.0).then_inc(pad_set, 1)
            ps = Steps(pool, pool_s)
            ps(nc.gpsimd.memset(ident[:], 0.0))
            nc.gpsimd.iota(tile_id[:], pattern=[[P, 2]], base=0, channel_multiplier=1,
                           allow_small_or_imprecise_dtypes=True).then_inc(consts, 1)
            nc.gpsimd.iota(block_lo[:], pattern=[[P, NT]], base=0, channel_multiplier=0,
                           allow_small_or_imprecise_dtypes=True).then_inc(consts, 1)
            ps.wait()
            nc.gpsimd.affine_select(out=ident[:], in_=ident[:], compare_op=ALU.not_equal, fill=1.0, base=0,
                                    pattern=[[-1, P]], channel_multiplier=1).then_inc(consts, 1)
            nc.gpsimd.iota(iota_n[:], pattern=[[1, NP]], base=0, channel_multiplier=0,
                           allow_small_or_imprecise_dtypes=True).then_inc(consts, 1)
            nc.gpsimd.memset(zerosb[:], 0.0).then_inc(consts, 1)
            nc.gpsimd.memset(ones[:], 1.0).then_inc(consts, 1)
            nc.gpsimd.memset(neg_half[:], -0.5).then_inc(consts, 1)
            pool.wait_ge(consts, 7)
            nc.gpsimd.affine_select(out=tri[:], in_=ones[:], compare_op=ALU.is_gt, fill=0.0, base=0,
                                    pattern=[[1, P]], channel_multiplier=-1).then_inc(consts, 1)
            nc.gpsimd.iota(node_id[:], pattern=[[P, NT]], base=0, channel_multiplier=1,
                           allow_small_or_imprecise_dtypes=True).then_inc(consts, 1)
            nc.gpsimd.iota(exp_id[:], pattern=[[1, NE]], base=0, channel_multiplier=0,
                           allow_small_or_imprecise_dtypes=True).then_inc(consts, 1)
            pool.wait_ge(consts, 10)
            nc.gpsimd.tensor_scalar(valid[:], node_id[:], float(N), None, ALU.is_lt).then_inc(consts, 1)
            nc.gpsimd.tensor_copy(identb[:], ident[:]).then_inc(consts, 1)
            nc.gpsimd.tensor_copy(identh[:], ident[:]).then_inc(consts, 1)

            def norm(t):
                c = bass.ds(t, 1)
                pool.wait_ge(stats_ready, t + 1)
                ps.link(nc.gpsimd.tensor_tensor(RSTD[:, c], var_e[:, c], neg_half[:, 0:1], ALU.pow))
                nc.gpsimd.tensor_tensor(NMR[:, c], neg_mean[:, c], RSTD[:, c], ALU.mult).then_inc(norm_ready, 1)

            def lo_part(t):
                pool.wait_ge(hi_ready, t + 1)
                wait_from(pool, parts_psum, t)
                nc.gpsimd.tensor_tensor(x_parts[:, 1, :], ln_x, x_parts[:, 0, :], ALU.subtract).then_inc(lo_ready, 1)

            def ct_store(t):
                pool.wait_ge(ct_staged, t + 1)
                nc.gpsimd.tensor_copy(CT[:, bass.ds(t, 1), :], ct_stage.unsqueeze(1)).then_inc(ct_stored, 1)

            norm(0)
            pool.wait_ge(w_hi_ready, 2)
            nc.gpsimd.tensor_tensor(W_lo[:, 0:KD // 2, :], W_raw[:, 0:KD // 2, :], W_hi[:, 0:KD // 2, :],
                                    ALU.subtract).then_inc(w_lo_ready, 1)
            lo_part(0)
            norm(1)
            ct_store(0)
            with pool.Fori(1, NT - 1) as t:
                ps.enter(t - 1, 1)
                lo_part(t)
                norm(t + 1)
                ct_store(t)
                ps.leave(NT - 2)
            lo_part(NT - 1)
            ct_store(NT - 1)

            def rstd():
                nc.gpsimd.tensor_tensor(RSTD[:], var_e[:], neg_half[:], ALU.pow).then_inc(rstd_ready, 1)

            for i in range(W_ITEMS):
                b = i % 2
                pool.wait_ge(w_scaled, i + 1)
                pool.wait_ge(wT_psum, freed(i))
                if i < 2 * FC:
                    parts = [(w_raw[:, b, :], w_inv[:, i:i + 1], w_q[:, b, :])]
                else:
                    parts = [(w_raw[:, b, r * FF:(r + 1) * FF], w_inv[:, w:w + 1], w_q[:, b, r * FF:(r + 1) * FF])
                             for r in range(2) for w in [2 * FC + 2 * (i - 2 * FC) + r]]
                for raw, inv, _ in parts:
                    ps(nc.gpsimd.tensor_scalar(raw, raw, inv, MAGIC, ALU.mult, ALU.add))
                ps.wait()
                for raw, _, q in parts:
                    last = nc.gpsimd.tensor_scalar(q, raw, -MAGIC, 1.0, ALU.add, ALU.mult)
                last.then_inc(w_rounded, 1)
                if 2 * FC - 4 <= i < 2 * FC - 2:
                    pool.wait_ge(w_rounded, done(i))
                    nc.gpsimd.memset(w_raw[FF % P:P, b, :], 0.0).then_inc(wpad_set, 1)
                    pool.wait_ge(wpad_set, b + 1)

            pool.wait_ge(var_ready, 1)
            rstd()
            for n in range(2):
                pool.wait_ge(max_ready, n + 1)
                nc.gpsimd.partition_all_reduce(top[:, 2 * n + 1:2 * n + 2], top[:, 2 * n:2 * n + 1], P,
                                               RMAX).then_inc(max_all, 1)
                if n == 0:
                    pool.wait_ge(w1_in, 16)
                    nc.gpsimd.tensor_scalar(W1_raw, W1_raw, W_SCALE, None, ALU.mult).then_inc(w1_scaled, 1)
                    pool.wait_ge(w1_hi_ready, 1)
                    nc.gpsimd.tensor_tensor(W1_lo, W1_raw, W1_hi, ALU.subtract).then_inc(w1_lo_ready, 1)

            def add_down(t, j):
                pool.wait_ge(d_scaled, done(t + j))
                xt = X[:, bass.ds(t + j, 1), :].squeeze(1)
                nc.gpsimd.tensor_tensor(xt, xt, w_raw[:, j, :], ALU.add).then_inc(d_added, 1)

            with pairs(pool, NT) as t:
                add_down(t, 0)
                add_down(t, 1)

            pool.wait_ge(dis_deg, 1)
            nc.gpsimd.tensor_tensor(dis[:], dis[:], neg_half[:], ALU.pow).then_inc(dis_ready, 1)
            pool.wait_ge(var_ready, 2)
            rstd()

            def gs_low(k, t, j):
                n = k * NT + j
                pool.wait_ge(gs_made, done(t + n))
                q = k % 2
                nc.gpsimd.tensor_tensor(GS[:, q, 1, bass.ds(t + j, 1), :].squeeze(1), gs_raw,
                                        GS[:, q, 0, bass.ds(t + j, 1), :].squeeze(1), ALU.subtract).then_inc(gs_ready, 1)

            with pool.Fori(0, NT) as t:
                pool.wait_ge(x1_ready, done(t))
                xl = X[:, bass.ds(t, 1), 0:HD].squeeze(1)
                nc.gpsimd.tensor_tensor(xl, xl, G[:, bass.ds(t, 1), :].squeeze(1), ALU.add).then_inc(xl_added, 1)
                gs_low(0, t, 0)
            for k in range(1, K1):
                with pool.Fori(0, NT) as t:
                    gs_low(k, t, 0)

            pool.wait_ge(var_ready, 3)
            rstd()

            def fetch(e):
                pool.wait_ge(o_ready, e - 1)
                nc.gpsimd.indirect_dma_start(
                    out=xg[:, e % 4, :], out_offset=None, in_=x_rows,
                    in_offset=bass.IndirectOffsetOnAxis(ap=take[0:CAP, e:e + 1], axis=0)
                ).then_inc((got0, got1, got2, got3)[e % 4], 16)

            def send(e):
                pool.wait_ge(o_ready, done(e))
                nc.gpsimd.indirect_dma_start(
                    out=out, out_offset=bass.IndirectOffsetOnAxis(ap=give[0:CAP, e:e + 1], axis=0),
                    in_=o_stage[:, e % 2, :], in_offset=None, bounds_check=N - 1, oob_is_err=False
                ).then_inc((sent0, sent1)[e % 2], 16)

            pool.wait_ge(rows_out, 2 * NT * 16)
            pool.wait_ge(slots_ready, 1)
            for e in range(min(4, NE)):
                nc.gpsimd.indirect_dma_start(
                    out=xg[:, e % 4, :], out_offset=None, in_=x_rows,
                    in_offset=bass.IndirectOffsetOnAxis(ap=take[0:CAP, e:e + 1], axis=0)
                ).then_inc((got0, got1, got2, got3)[e % 4], 16)
            for e in range(NE):
                send(e)
                if e + 4 < NE:
                    fetch(e + 4)

        @block.vector
        def _(dve):
            st = Steps(dve, dve_s)
            v = nc.vector

            def row_stats(t):
                for g in range(2):
                    st(v.bn_stats(bst[:, bass.ds(t, 1), g, :].squeeze(1),
                                  X[:, bass.ds(t, 1), g * HD:(g + 1) * HD].squeeze(1)))

            def variances(scale=1.0):
                st.wait()
                for t in range(NT):
                    st(v.bn_aggr(MV[:, t, :], bst[:, t, :, :]))
                st.wait()
                v.tensor_scalar(var_e[:], MV[:, :, 1], EPS, scale ** -2, ALU.add, ALU.mult).then_inc(var_ready, 1)

            def means(n):
                dve.wait_ge(rstd_ready, n)
                v.scalar_tensor_tensor(out=NMR[:], in0=MV[:, :, 0], scalar=-1.0, in1=RSTD[:],
                                       op0=ALU.mult, op1=ALU.mult).then_inc(nmr_ready, 1)

            dve.wait_ge(edges_in, 16 * 6)
            dve.wait_ge(consts, CONSTS)
            v.tensor_copy(edges_f.rearrange("p a b c -> p (a b c)"),
                          edges_i.rearrange("p a b c -> p (a b c)")).then_inc(edges_ready, 1)
            dve.wait_ge(edges_ready, 1)
            st(v.tensor_reduce(tile_lo[:], edges_f[:, 0, :, :], AX_X, ALU.min))
            st(v.tensor_reduce(tile_hi[:], edges_f[:, 0, :, :], AX_X, ALU.max))
            st.wait()
            for h in range(2):
                st(v.tensor_scalar(cross[:, 0, h, :], block_lo[:], tile_hi[:, h:h + 1], None, ALU.is_le))
                st(v.tensor_scalar(cross[:, 1, h, :], block_lo[:], float(P - 1), tile_lo[:, h:h + 1],
                                   ALU.add, ALU.is_ge))
            st.wait()
            st.link(v.tensor_tensor(cross[:, 0, :, :], cross[:, 0, :, :], cross[:, 1, :, :], ALU.mult))
            for h in range(2):
                st(v.tensor_scalar(rng_f[:, 0, h, :], cross[:, 0, h, :], -1000.0, 1000.0, ALU.mult, ALU.add))
                st(v.tensor_scalar(rng_f[:, 1, h, :], cross[:, 0, h, :], 1.0, None, ALU.mult))
            st.wait()
            for h in range(2):
                last = v.tensor_scalar(rng_f[:, 0, h, :], rng_f[:, 0, h, :], tile_id[:, h:h + 1], None, ALU.add)
                st(last)
                st(v.tensor_scalar(rng_f[:, 1, h, :], rng_f[:, 1, h, :], tile_id[:, h:h + 1], None, ALU.mult))
            st.wait()
            v.tensor_tensor(rng_f[:, 1, :, :], rng_f[:, 1, :, :], cross[:, 0, :, :],
                            ALU.add).then_inc(rng_ready, 1)
            dve.wait_ge(edgeT_psum, 1)
            st(v.tensor_copy(edgeT[:], PS[:, 6, :].rearrange("p (s e) -> p s e", s=2)))
            dve.wait_ge(rngT_psum, 1)
            st(v.tensor_reduce(rng_c[:, 0:1], PS[0:NT, 7, 0:2 * P], AX_X, ALU.min))
            st(v.tensor_reduce(rng_c[:, 1:2], PS[0:NT, 7, 2 * P:4 * P], AX_X, ALU.max))
            st.wait()
            v.tensor_scalar(rng_c[:, 0:1], rng_c[:, 0:1], float(ET - 1), None, ALU.min).then_inc(rng_col, 1)
            dve.wait_ge(rng_row_psum, 1)
            v.tensor_copy(rng_i[:], PS[0:1, 7, 0:2 * NT]).then_inc(rng_row, 1)
            dve.wait_ge(rng_row, 1)

            made = dve.alloc_register("oh_made")
            dve.reg_mov(made, 1)

            def one_hots(b):
                lo = dve.value_load(rng_i[0:1, bass.ds(b, 1)], min_val=0, max_val=ET - 1)
                hi = dve.value_load(rng_i[0:1, bass.ds(b + NT, 1)], min_val=0, max_val=ET)
                with dve.Fori(lo, hi, OH) as t:
                    now = dve.snap(made, min_val=1, max_val=2000)
                    for j in range(OH):
                        if j % 2 == 0:
                            dve.wait_ge(oh_free, now + j // 2)
                        v.tensor_scalar(oh_dst[:, j, :], iota_n[:, bass.ds(b * P, P)],
                                        edgeT[:, 0, bass.ds(t + j, 1)], None, ALU.is_equal)
                        last = v.tensor_scalar(oh_src[:, j, :], iota_n[:],
                                               edgeT[:, 1, bass.ds(t + j, 1)], None, ALU.is_equal)
                        if j % 2:
                            last.then_inc(oh_ready, 1)
                    dve.reg_add(made, made, OH // 2)

            def tile_stats(t):
                for g in range(2):
                    st(v.bn_stats(st_one[:, g, :], X[:, bass.ds(t, 1), g * HD:(g + 1) * HD].squeeze(1)))

            def tile_norm(t):
                st.link(v.bn_aggr(mv_one[:], st_one[:]))
                st.link(v.tensor_scalar(neg_mean[:, bass.ds(t, 1)], mv_one[:, 0:1], -1.0, None, ALU.mult))
                v.tensor_scalar(var_e[:, bass.ds(t, 1)], mv_one[:, 1:2], EPS, X_SCALE ** -2, ALU.add,
                                ALU.mult).then_inc(stats_ready, 1)

            def h_dot(t, s):
                st(v.scalar_tensor_tensor(out=junk, in0=hbuf[:, bass.ds(t, 1), :].squeeze(1),
                                          scalar=1.0, in1=a_row[:, s, :], op0=ALU.mult, op1=ALU.mult,
                                          accum_out=AL[:, s, bass.ds(t, 1)]))

            def first_item(b):
                one_hots(b)
                if b == 1:
                    dve.wait_ge(x_in, 32)
                tile_stats(b + 1)
                st.wait()
                tile_norm(b + 1)

            def item(b):
                one_hots(b)
                tile_stats(b + 1)
                st.wait()
                dve.wait_ge(h_ready, b - 1)
                h_dot(b - 2, 0)
                tile_norm(b + 1)
                h_dot(b - 2, 1)

            dve.wait_ge(x_first_in, 16)
            tile_stats(0)
            st.wait()
            tile_norm(0)
            first_item(0)
            dve.wait_ge(w_hi_ready, 1)
            v.scalar_tensor_tensor(out=W_lo[:, KD // 2:KD, :], in0=W_raw[:, KD // 2:KD, :], scalar=W_SCALE,
                                   in1=W_hi[:, KD // 2:KD, :], op0=ALU.mult, op1=ALU.subtract).then_inc(w_lo_ready, 1)
            first_item(1)
            dve.wait_ge(a_in, 16)
            with dve.Fori(2, NT - 1) as b:
                st.enter(b - 2, 6)
                item(b)
                st.leave(NT - 3)
            one_hots(NT - 1)
            for b in range(NT - 3, NT):
                dve.wait_ge(h_ready, b + 1)
                for s in range(2):
                    st.wait()
                    h_dot(b, s)

            def row_of(column):
                n = column.shape[1]
                st.wait()
                v.tensor_tensor(diag[:, 0:n * P].rearrange("p (t n) -> p t n", n=P),
                                ident[:].unsqueeze(1).broadcast_to([P, n, P]),
                                column.unsqueeze(2).broadcast_to([P, n, P]), ALU.mult).then_inc(diag_ready, 1)

            def columns_of(i):
                return bass.ds(i * P, P)

            def weights(i, j):
                cols = columns_of(i + j)
                dve.wait_ge(at_ready, i + (j + CREDIT))
                v.tensor_tensor(S, alb[:, cols].unsqueeze(1).broadcast_to([P, NT, P]),
                                AL[:, 1, :].unsqueeze(2).broadcast_to([P, NT, P]), ALU.add).then_inc(sum_ready, 1)
                dve.wait_ge(sum_ready, i * 2 + (2 * j + 1))
                v.scalar_tensor_tensor(out=S, in0=S, scalar=0.1, in1=S, op0=ALU.mult,
                                       op1=ALU.max).then_inc(sum_ready, 1)
                dve.wait_ge(act_out, done(i + j))
                dve.wait_ge(agg_psum, freed(i + j))
                v.tensor_tensor(AT[:, j, :, :], S, CT[:, :, cols], ALU.mult).then_inc(at_ready, 1)
                dve.wait_ge(at_ready, done(i + j))
                v.tensor_reduce(at_sum[:, j, :], AT[:, j, :, :].rearrange("p t n -> p n t"), AX_X,
                                ALU.add).then_inc(at_summed, 1)

            def aggregate(i, j):
                dve.wait_ge(agg_psum, done(i + j))
                acc = PS[:, 3 * j:3 * j + 2, :].rearrange("p a n -> p (a n)")
                st.link(v.tensor_scalar(rs[:, 0:1], PS[:, 3 * j + 2, 0:1], EPS, None, ALU.add))
                st.link(v.reciprocal(rs[:, 1:2], rs[:, 0:1]))
                v.tensor_scalar(tmp_m, acc, rs[:, 1:2], 0.0, ALU.mult, ALU.min).then_inc(m_ready, 1)
                st(v.tensor_scalar(tmp_p, acc, rs[:, 1:2], 0.0, ALU.mult, ALU.max))
                dve.wait_ge(e_ready, i + (j + 1))
                st.wait()
                st.link(v.scalar_tensor_tensor(out=tmp_p, in0=tmp_m, scalar=-1.0, in1=tmp_p,
                                               op0=ALU.add, op1=ALU.add))
                xt = X[:, bass.ds(i + j, 1), :].squeeze(1)
                v.tensor_tensor(xt, xt, tmp_p, ALU.add).then_inc(x_updated, 1)
                dve.wait_ge(x_updated, done(i + j))
                row_stats(i + j)

            def extremes(i, j):
                for ends, op in ((x_max, ALU.max), (x_min, ALU.min)):
                    st(v.tensor_reduce(ends[:, bass.ds(i + j, 1)], X[:, bass.ds(i + j, 1), :].squeeze(1), AX_X, op))

            def ffn_scales(i, j):
                dve.wait_ge((wraw_in0, wraw_in1)[j], i * 8 + 16)
                if isinstance(i, int) and i >= 2 * FC:
                    w = slice(2 * (i + j - FC), 2 * (i + j - FC) + 2)
                    rows = w_raw[:, j, 0:2 * FF].rearrange("p (r f) -> p r f", r=2)
                else:
                    w = bass.ds(i + j, 1)
                    rows = w_raw[:, j, :]
                st.link(v.tensor_reduce(w_max[:, w], rows, AX_X, ALU.max, apply_absolute_value=True))
                st.link(v.tensor_scalar(w_max[:, w], w_max[:, w], 1.0 / QMAX, 1e-35, ALU.mult, ALU.max))
                v.reciprocal(w_inv[:, w], w_max[:, w]).then_inc(w_scaled, 1)

            def attention_item(i, j):
                ffn_scales(i, j)
                aggregate(i, j)
                extremes(i, j)

            row_of(AL[:, 0, :])
            dve.wait_ge(row_stored, 1)
            weights(0, 0)
            with pairs(dve, 2 * FC) as i:
                st.enter(i, 10, 2)
                weights(i, 1)
                attention_item(i, 0)
                weights(i + 2, 0)
                attention_item(i, 1)
                st.leave(2 * FC)
            for i in range(2 * FC, NT, 2):
                weights(i, 1)
                attention_item(i, 0)
                if i + 2 < NT:
                    weights(i + 2, 0)
                attention_item(i, 1)
            variances()
            means(1)

            def act_scale(n):
                dve.wait_ge(max_all, n + 1)
                st.link(v.tensor_scalar(s_act[:, 2 * n:2 * n + 1], top[:, 2 * n + 1:2 * n + 2], sig[:, n:n + 1],
                                        1.0 / QMAX, ALU.mult, ALU.mult))
                st.link(v.reciprocal(s_act[:, 2 * n + 1:2 * n + 2], s_act[:, 2 * n:2 * n + 1]))

            dve.wait_ge(sig_ready, 1)
            st.link(v.tensor_scalar(sig[:], sig[:], 0.5, 0.5, ALU.mult, ALU.add))
            for ends in (x_max, x_min):
                st.link(v.tensor_tensor(ends[:], ends[:], RSTD[:], ALU.mult))
                st.link(v.tensor_tensor(ends[:], ends[:], NMR[:], ALU.add))
            st.link(v.tensor_scalar(x_min[:], x_min[:], -1.0, None, ALU.mult))
            st.link(v.tensor_tensor(x_max[:], x_max[:], x_min[:], ALU.max))
            v.tensor_reduce(top[:, 0:1], x_max[:], AX_X, ALU.max).then_inc(max_ready, 1)
            act_scale(0)
            st(v.tensor_scalar(qscale[:], RSTD[:], s_act[:, 1:2], None, ALU.mult))
            v.tensor_scalar(qbias[:], NMR[:], s_act[:, 1:2], None, ALU.mult).then_inc(qs_ready, 1)
            st(v.tensor_scalar(s_half[:], w_max[:, 0:2 * FC:2], s_act[:, 0:1], 0.5, ALU.mult, ALU.mult))
            st(v.tensor_scalar(s_gu[:], w_max[:, 1:2 * FC:2], s_act[:, 0:1], None, ALU.mult))
            st.wait()
            v.tensor_tensor(s_gu[:], s_gu[:], s_half[:], ALU.mult).then_inc(qs_ready, 1)
            dve.wait_ge(qs_ready, 2)

            def round_x(t, j):
                dve.wait_ge(y_ready, done(t + j))
                dve.wait_ge(yT_psum, freed(t + j))
                y = xn_stage[:, j, :]
                st.link(v.tensor_scalar(y, y, QMAX, -QMAX - 1, ALU.min, ALU.max))
                v.tensor_scalar(xq_stage[:, j, :], y, MAGIC, -MAGIC, ALU.add, ALU.add).then_inc(yq_ready, 1)

            with pairs(dve, NT) as t:
                st.enter(t, 1, 2)
                round_x(t, 0)
                round_x(t, 1)
                st.leave(NT)

            def gate_up(g, i, c):
                n = i * FC + c
                j = n % 2
                dve.wait_ge(tanh_ready, done(g * FC + n))
                st.link(v.scalar_tensor_tensor(out=gu_tmp[:, j, :], in0=gu_tmp[:, j, :], scalar=1.0,
                                               in1=PS[:, 2 * j, 0:GN], op0=ALU.add, op1=ALU.mult))
                v.scalar_tensor_tensor(out=hT[:, c, bass.ds((g + i) * GN, GN)], in0=gu_tmp[:, j, :],
                                       scalar=s_gu[:, c:c + 1], in1=PS[:, 2 * j + 1, 0:GN],
                                       op0=ALU.mult, op1=ALU.mult).then_inc(hT_ready, 1)

            with pairs(dve, NG) as g:
                st.enter(g, FC, 2)
                for i in range(2):
                    for c in range(FC):
                        gate_up(g, i, c)
                st.leave(NG)
            dve.wait_ge(hT_ready, FC * NG + CREDIT)
            v.tensor_reduce(top[:, 2:3], hT, AX_XY, ALU.max, apply_absolute_value=True).then_inc(max_ready, 1)
            act_scale(1)
            st(v.tensor_scalar(s_down[:], w_max[:, 2 * FC:2 * FC + KD], s_act[:, 2:3], None, ALU.mult))
            st.link(v.tensor_scalar(hT, hT, s_act[:, 3:4], QMAX, ALU.mult, ALU.min))
            row_of(s_down[:])
            st.link(v.tensor_scalar(hT, hT, -QMAX - 1, MAGIC, ALU.max, ALU.add))
            v.tensor_scalar(hq, hT, -MAGIC, None, ALU.add).then_inc(hq_ready, 1)

            def down(t, j):
                dve.wait_ge(d_psum, done(t + j))
                dve.wait_ge(d_added, freed(t + j))
                v.tensor_tensor(w_raw[:, j, :], PS[:, 2 * j:2 * j + 2, :].rearrange("p a n -> p (a n)"), tmp_m,
                                ALU.mult).then_inc(d_scaled, 1)

            def down_stats(t, j):
                dve.wait_ge(d_added, done(t + j))
                row_stats(t + j)

            v.tensor_scalar(dis[:], deg[:], 1.0, None, ALU.max).then_inc(dis_deg, 1)
            dve.wait_ge(row_stored, 2)
            down(0, 0)
            with pairs(dve, NT - 2) as t:
                st.enter(t, 2, 2)
                down(t, 1)
                down_stats(t, 0)
                down(t + 2, 0)
                down_stats(t, 1)
                st.leave(NT - 2)
            down(NT - 2, 1)
            down_stats(NT - 2, 0)
            down_stats(NT - 2, 1)
            variances(X_SCALE)
            means(2)

            def dots(rows, t, q):
                st(v.scalar_tensor_tensor(out=dot_out, in0=rows, scalar=1.0, in1=wg_row[:, 0, :], op0=ALU.mult,
                                          op1=ALU.mult, accum_out=U[:, bass.ds(t, 1)]))
                st.wait()
                v.scalar_tensor_tensor(out=dot_out, in0=rows, scalar=1.0, in1=wg_row[:, 1, :], op0=ALU.mult,
                                       op1=ALU.mult, accum_out=V[:, q, bass.ds(t, 1)]).then_inc(uv_ready, 1)

            def lo_part(t, j):
                dve.wait_ge(hi2_ready, done(t + j))
                v.tensor_tensor(parts2[:, j % 2, 1, :], ln2, parts2[:, j % 2, 0, :],
                                ALU.subtract).then_inc(lo2_ready, 1)

            def x1_out(t, j):
                dve.wait_ge(x1_psum, done(t + j))
                rows = G[:, bass.ds(t + j, 1), :].squeeze(1)
                v.scalar_tensor_tensor(out=rows, in0=PS[:, j, :], scalar=1.0 / (X_SCALE * W_SCALE), in1=b1_row,
                                       op0=ALU.mult, op1=ALU.add).then_inc(x1_ready, 1)
                dve.wait_ge(x1_ready, done(t + j))
                dots(rows, t + j, 0)

            dve.wait_ge(b1_in, 32)
            dve.wait_ge(wg_in, 16)
            dve.wait_ge(dis_ready, 1)
            st(v.tensor_scalar(dis_in[:], dis[:], G_SCALE, None, ALU.mult))
            v.tensor_scalar(dis_out[:], dis[:], 1.0 / G_SCALE, None, ALU.mult).then_inc(dis_scaled, 1)
            lo_part(0, 0)
            lo_part(0, 1)
            with pairs(dve, NT - 2) as t:
                st.enter(t, 1, 2)
                for j in range(2):
                    lo_part(t, j + 2)
                    x1_out(t, j)
                st.leave(NT - 2)
            x1_out(NT - 2, 0)
            x1_out(NT - 2, 1)

            def edge_weights(k, c, j):
                dve.wait_ge(tanh2_ready, c + (k * NT + j + 1))
                s = SS[:, j % 2, :, :]
                v.scalar_tensor_tensor(out=s, in0=s, scalar=A_SCALE, in1=C[:, :, columns_of(c + j)], op0=ALU.mult,
                                       op1=ALU.mult).then_inc(aw_ready, 1)

            def weights_low(k, c, j):
                dve.wait_ge(aw_hi_ready, done(c + (k * NT + j)))
                v.scalar_tensor_tensor(out=AP[:, j % 2, 1, :, :], in0=AP[:, j % 2, 0, :, :], scalar=-A_SCALE,
                                       in1=SS[:, j % 2, :, :], op0=ALU.mult, op1=ALU.add).then_inc(aw_lo_ready, 1)

            def gather_edges(k, c, j):
                dve.wait_ge(agg2_psum, done(c + (k * NT + j)))
                rows = G[:, bass.ds(c + j, 1), :].squeeze(1)
                st.link(v.tensor_scalar(agg_row, PS[:, 5 + j, :], 1.0 / A_SCALE, None, ALU.mult))
                st.link(v.tensor_tensor(agg_row, agg_row, PS[:, 3 + j, :], ALU.add))
                v.scalar_tensor_tensor(out=rows, in0=agg_row, scalar=dis_out[:, bass.ds(c + j, 1)], in1=rows,
                                       op0=ALU.mult, op1=ALU.add).then_inc(g_ready, 1)
                dve.wait_ge(g_ready, done(c + (k * NT + j)))
                if k + 1 < K1:
                    dots(rows, c + j, (k + 1) % 2)
                else:
                    xr = X[:, bass.ds(c + j, 1), HD:D].squeeze(1)
                    v.tensor_tensor(xr, xr, rows, ALU.add).then_inc(x_final, 1)
                    dve.wait_ge(x_final, c + (j + 1))
                    row_stats(c + j)

            dve.wait_ge(xl_added, NT)
            for k in range(K1):
                per = 3 if k + 1 < K1 else 4
                dve.wait_ge(uv_ready, (k + 1) * NT)
                st(v.tensor_scalar(UB[:], U[:], bg_row[:, k:k + 1], None, ALU.add))
                row_of(UB[:])
                if k + 1 < K1:
                    dve.wait_ge(wg_in, 16 * (k + 2))
                edge_weights(k, 0, 0)
                edge_weights(k, 0, 1)
                weights_low(k, 0, 0)
                with pairs(dve, NT - 2) as c:
                    st.enter(c, per, 2)
                    for j in range(2):
                        weights_low(k, c, j + 1)
                        edge_weights(k, c, j + 2)
                        gather_edges(k, c, j)
                    st.leave(NT - 2)
                weights_low(k, NT - 2, 1)
                gather_edges(k, NT - 2, 0)
                gather_edges(k, NT - 2, 1)
            variances()
            means(3)

            def logits_out(t, j):
                dve.wait_ge(lg_psum, done(t + j))
                v.tensor_copy(LG[:, bass.ds(t + j, 1), :].squeeze(1), PS[:, j, 0:NE]).then_inc(lg_ready, 1)

            dve.wait_ge(gwT_psum, 1)
            v.tensor_copy(gwT, PS[:, 2, 0:KD * NE].rearrange("p (k e) -> p k e", k=KD)).then_inc(gwT_ready, 1)
            def xnT_out(t, j):
                dve.wait_ge(xnT_psum, done(t + j))
                dve.wait_ge(lg_psum, freed(t + j))
                v.tensor_copy(xnT_stage[:, j, :, :].rearrange("p (a k) n -> p a (k n)", a=2),
                              PS[:, 4 + 2 * j:6 + 2 * j, :]).then_inc(xnT_ready, 1)

            xnT_out(0, 0)
            with pairs(dve, NT - 2) as t:
                xnT_out(t, 1)
                logits_out(t, 0)
                xnT_out(t + 2, 0)
                logits_out(t, 1)
            xnT_out(NT - 2, 1)
            logits_out(NT - 2, 0)
            logits_out(NT - 2, 1)
            dve.wait_ge(lg_ready, NT + CREDIT)

            diff, mask, rank, keep, was = (route(i) for i in range(5))
            of_experts = [P, NT, NE]
            st.link(v.tensor_reduce(lg_top[:], LG[:], AX_X, ALU.max))
            top_b = lg_top[:].unsqueeze(2).broadcast_to(of_experts)
            ids = exp_id[:].unsqueeze(1).broadcast_to(of_experts)
            v.tensor_tensor(diff, LG[:], top_b, ALU.subtract).then_inc(soft_in, 1)
            st.link(v.tensor_tensor(mask, LG[:], top_b, ALU.is_equal))
            st.link(v.tensor_scalar(mask, mask, -100.0, None, ALU.mult))
            st.link(v.tensor_tensor(mask, mask, ids, ALU.add))
            st.link(v.tensor_reduce(first[:], mask, AX_X, ALU.min))
            st.link(v.tensor_tensor(mask, mask, first[:].unsqueeze(2).broadcast_to(of_experts), ALU.is_equal))
            v.tensor_tensor(mask, mask, valid[:].unsqueeze(2).broadcast_to(of_experts),
                            ALU.mult).then_inc(mask_ready, 1)
            dve.wait_ge(soft_out, 1)
            st.link(v.tensor_reduce(wt[:], diff, AX_X, ALU.add))
            st.link(v.reciprocal(wt[:], wt[:]))
            dve.wait_ge(rank_psum, 1)
            st(v.tensor_copy(keep, PS[:, 4, 0:NT * NE].rearrange("p (t e) -> p t e", t=NT)))
            st(v.memset(was[:, 0, :], 0.0))
            st.wait()
            for t in range(NT - 1):
                st.link(v.tensor_tensor(was[:, t + 1, :], was[:, t, :], keep[:, t, :], ALU.add))
            st.link(v.tensor_tensor(rank, PS[:, 3, 0:NT * NE].rearrange("p (t e) -> p t e", t=NT), was, ALU.add))
            st(v.tensor_scalar(keep, rank, float(CAP), None, ALU.is_lt))
            st.link(v.tensor_tensor(rank, rank, mask, ALU.mult))
            st(v.tensor_reduce(rank1[:], rank, AX_X, ALU.add))
            st.link(v.tensor_tensor(keep, keep, mask, ALU.mult))
            st(v.tensor_tensor(slot_of, iota_n[:, 0:CAP].unsqueeze(1).broadcast_to([P, NT, CAP]),
                               rank1[:].unsqueeze(2).broadcast_to([P, NT, CAP]), ALU.is_equal))
            st(v.tensor_copy(facts[:, :, 0, :], keep))
            for i, what in enumerate((node_id, wt, RSTD, NMR)):
                last = v.tensor_tensor(facts[:, :, i + 1, :], keep, what[:].unsqueeze(2).broadcast_to(of_experts),
                                       ALU.mult)
                if i < 3:
                    st(last)
            last.then_inc(cast_ready, 1)
            dve.wait_ge(slots_psum, 1)
            st.link(v.tensor_copy(slots[0:CAP].rearrange("p q e -> p (q e)"), PS[0:CAP, 5, 0:NR]))
            st(v.tensor_copy(take[0:CAP, :], slots[0:CAP, 1, :]))
            st.link(v.tensor_scalar(away[0:CAP, :], slots[0:CAP, 0, :], -65536.0, 65536.0, ALU.mult, ALU.add))
            st.link(v.tensor_tensor(away[0:CAP, :], away[0:CAP, :], slots[0:CAP, 1, :], ALU.add))
            v.tensor_copy(give[0:CAP, :], away[0:CAP, :]).then_inc(slots_ready, 1)

            def xgT_out(e, j):
                dve.wait_ge(xgT_psum, done(e + j))
                dve.wait_ge(m1_psum, freed(e + j))
                v.tensor_copy(xgT[:, j % 2, :, :].rearrange("p (a k) c -> p a (k c)", a=2),
                              PS[:, 0:2, 0:4 * CAP]).then_inc(xgT_ready, 1)

            def geT_out(e, j):
                dve.wait_ge(geT_psum, done(e + j))
                dve.wait_ge(m2_psum, freed(e + j))
                v.tensor_copy(geT[:, j % 2, :, :].rearrange("p k c -> p (k c)"), PS[:, 4, 0:4 * CAP]
                              ).then_inc(geT_ready, 1)

            def rows_made(e, j):
                dve.wait_ge(m2_psum, done(e + j))
                if not (isinstance(e, int) and e + j < 2):
                    dve.wait_ge((sent0, sent1)[j % 2], (e + j) // 2 * 16)
                v.scalar_tensor_tensor(out=o_stage[:, j % 2, :],
                                       in0=PS[0:CAP, 5:7, :].rearrange("p a n -> p (a n)"),
                                       scalar=slots[0:CAP, 2, bass.ds(e + j, 1)],
                                       in1=xg[:, bass.ds((e + j) % 4, 1), :].squeeze(1),
                                       op0=ALU.mult, op1=ALU.add).then_inc(o_ready, 1)

            xgT_out(0, 0)
            xgT_out(0, 1)
            geT_out(0, 0)
            for j in (1, 2):
                xgT_out(0, j + 1)
                rows_made(0, j - 1)
                geT_out(0, j)
            with dve.Fori(2, NE - 3, 2) as e:
                for j in (1, 2):
                    xgT_out(e, j + 1)
                    rows_made(e, j - 1)
                    geT_out(e, j)
            rows_made(NE - 2, 0)
            geT_out(NE - 2, 1)
            rows_made(NE - 2, 1)

        @block.scalar
        def _(act):
            a = nc.scalar
            act.wait_ge(consts, CONSTS)

            def ln_out(t):
                c = bass.ds(t, 1)
                act.wait_ge(norm_ready, t + 1)
                wait_from(act, lo_ready, t)
                ln_steps(a.activation(ln_x, X[:, c, :].squeeze(1), ACT.Identity,
                                      scale=RSTD[:, c], bias=NMR[:, c]))
                ln_steps.wait()
                wait_from(act, parts_psum, t)
                a.copy(x_parts[:, 0, :], ln_x).then_inc(hi_ready, 1)

            def ct_out(t):
                act.wait_ge(ct_psum, t + 1)
                wait_from(act, ct_stored, t)
                a.activation(ct_stage, PS[:, 0:3, :].rearrange("p a n -> p (a n)")[:, 0:NP],
                             ACT.Identity, accum_out=deg[:, bass.ds(t, 1)]).then_inc(ct_staged, 1)

            def h_out(t):
                act.wait_ge(h_psum, t + 1)
                a.activation(hbuf[:, bass.ds(t, 1), :].squeeze(1), PS[:, 4:6, :].rearrange("p a n -> p (a n)"),
                             ACT.Copy, scale=1.0 / (X_SCALE * W_SCALE)).then_inc(h_ready, 1)

            def c_out(t):
                for g in range(CG):
                    n = min(4, NT - 4 * g)
                    act.wait_ge(c_psum, t * CG + (g + 1))
                    a.copy(C[:, 4 * g:4 * g + n, bass.ds(t * P, P)],
                           PS[:, g, 0:n * P].rearrange("p (t n) -> p t n", n=P)).then_inc(c_stored, 1)

            def xT_out(t):
                act.wait_ge(parts_psum, t + 1)
                wait_from(act, h_psum, t)
                a.copy(xT_parts.rearrange("p s k n -> p s (k n)"),
                       PS[:, 6:8, :].bitcast(F16)).then_inc(partsT_ready, 1)

            ln_steps = Steps(act, act_s)
            act.wait_ge(w_in, 16)
            h = slice(KD // 2, KD)
            a.activation(W_hi[:, h, :], W_raw[:, h, :], ACT.Copy, scale=W_SCALE).then_inc(w_hi_ready, 1)
            h = slice(0, KD // 2)
            ln_steps(a.mul(W_raw[:, h, :], W_raw[:, h, :], W_SCALE))
            ln_steps.wait()
            a.copy(W_hi[:, h, :], W_raw[:, h, :]).then_inc(w_hi_ready, 1)
            ln_out(0)
            ct_out(0)
            c_out(0)
            xT_out(0)
            act.wait_ge(w_lo_ready, 2)
            with act.Fori(1, NT) as t:
                ln_steps.enter(t - 1, 1)
                ln_out(t)
                ct_out(t)
                h_out(t - 1)
                c_out(t)
                xT_out(t)
                ln_steps.leave(NT - 1)
            act.wait_ge(ct_stored, NT)
            h_out(NT - 1)

            def row_out(n, w):
                act.wait_ge(row_psum, n)
                a.copy((alb if n != 2 else tmp_m)[:, 0:w],
                       PS[:, 0:-(-w // 512), :].rearrange("p a n -> p (a n)")[:, 0:w]).then_inc(row_stored, 1)

            def exp_weights(i, j):
                act.wait_ge(sum_ready, i * 2 + (2 * j + 2))
                a.activation(S, S, ACT.Exp, scale=-1.0).then_inc(act_out, 1)

            def exp_elu(i, j):
                act.wait_ge(m_ready, i + (j + 1))
                a.activation(tmp_m, tmp_m, ACT.Exp).then_inc(e_ready, 1)

            row_out(1, NP)
            act.wait_ge(clips_in, 32)
            a.activation(sig[:], clips[:], ACT.Tanh, scale=0.5).then_inc(sig_ready, 1)
            def ffn_weights_out(i, j):
                act.wait_ge(wT_psum, done(i + j))
                bank = PS[:, 6 + j, :].bitcast(BF16).rearrange("p (k n) -> p k n", n=P)
                if isinstance(i, int) and i >= 2 * FC:
                    r = 2 * (i + j - 2 * FC)
                    for q in range(2):
                        cols = slice((r + q) * P, (r + q + 1) * P)
                        a.copy(wdT[:, 0:FC - 1, cols], bank[:, q * FC:(q + 1) * FC - 1, :])
                        last = a.copy(wdT[0:FF % P, FC - 1, cols], bank[0:FF % P, (q + 1) * FC - 1, :])
                    last.then_inc(wT_stored, 1)
                else:
                    a.copy(wguT[:, :, j, bass.ds(i * (P // 2), P)], bank).then_inc(wT_stored, 1)

            exp_weights(0, 0)
            with pairs(act, 2 * FC) as i:
                exp_weights(i, 1)
                exp_elu(i, 0)
                exp_weights(i + 2, 0)
                exp_elu(i, 1)
                ffn_weights_out(i, 0)
                ffn_weights_out(i, 1)
            for i in range(2 * FC, NT, 2):
                exp_weights(i, 1)
                exp_elu(i, 0)
                if i + 2 < NT:
                    exp_weights(i + 2, 0)
                exp_elu(i, 1)
                ffn_weights_out(i, 0)
                ffn_weights_out(i, 1)

            def y_out(t, j):
                act.wait_ge(yq_ready, freed(t + j))
                a.activation(xn_stage[:, j, :], X[:, bass.ds(t + j, 1), :].squeeze(1), ACT.Identity,
                             scale=qscale[:, bass.ds(t + j, 1)], bias=qbias[:, bass.ds(t + j, 1)]).then_inc(y_ready, 1)

            def yT_out(t, j):
                act.wait_ge(yT_psum, done(t + j))
                a.copy(xqT[:, :, bass.ds((t + j) * P, P)],
                       PS[:, 4 + j, :].bitcast(BF16).rearrange("p (k n) -> p k n", n=P)).then_inc(yT_stored, 1)

            act.wait_ge(qs_ready, 1)
            y_out(0, 0)
            with pairs(act, NT - 2) as t:
                y_out(t, 1)
                yT_out(t, 0)
                y_out(t + 2, 0)
                yT_out(t, 1)
            y_out(NT - 2, 1)
            yT_out(NT - 2, 0)
            yT_out(NT - 2, 1)

            act.wait_ge(w1_scaled, 1)
            act.wait_ge(yT_psum, NT + CREDIT)
            a.copy(W1_hi, W1_raw).then_inc(w1_hi_ready, 1)

            act.wait_ge(qs_ready, 2)
            with pairs(act, NG) as g:
                for n in range(2 * FC):
                    j = n % 2
                    act.wait_ge(gu_psum, done(g * FC + n))
                    a.activation(gu_tmp[:, j, :], PS[:, 2 * j, 0:GN], ACT.Tanh,
                                 scale=s_half[:, n % FC:n % FC + 1]).then_inc(tanh_ready, 1)
            row_out(2, D)

            def ln_out2(t, j):
                c = bass.ds(t + j, 1)
                act.wait_ge(lo2_ready, t + (j + CREDIT))
                steps(a.activation(ln2, X[:, c, :].squeeze(1), ACT.Identity, scale=RSTD[:, c], bias=NMR[:, c]))
                steps.wait()
                act.wait_ge(parts2_psum, freed(t + j))
                a.copy(parts2[:, j % 2, 0, :], ln2).then_inc(hi2_ready, 1)

            def xT_out2(t, j):
                act.wait_ge(parts2_psum, done(t + j))
                act.wait_ge(x1_psum, freed(t + j))
                b = j % 2
                a.copy(partsT2[:, b].rearrange("p s k n -> p s (k n)"),
                       PS[:, 4 + 2 * b:6 + 2 * b, :].bitcast(F16)).then_inc(parts2T_ready, 1)

            def scaled_rows(t, j, n):
                rows = G[:, bass.ds(t + j, 1), :].squeeze(1)
                by = dis_in[:, bass.ds(t + j, 1)]
                if n == 0:
                    act.wait_ge(x1_ready, done(t + j))
                else:
                    act.wait_ge(g_ready, done(t + (j + (n - 1) * NT)))
                act.wait_ge(gs_ready, t + (j + n * NT + CREDIT))
                steps(a.mul(gs_raw, rows, by))
                steps.wait()
                a.copy(GS[:, n % 2, 0, bass.ds(t + j, 1), :].squeeze(1), gs_raw).then_inc(gs_made, 1)

            steps = ln_steps
            act.wait_ge(nmr_ready, 2)
            act.wait_ge(dis_scaled, 1)
            act.wait_ge(w1_lo_ready, 1)
            ln_out2(0, 0)
            ln_out2(0, 1)
            xT_out2(0, 0)
            with pairs(act, NT - 2) as t:
                steps.enter(t, 2, 2)
                for j in range(2):
                    ln_out2(t, j + 2)
                    xT_out2(t, j + 1)
                    scaled_rows(t, j, 0)
                steps.leave(NT - 2)
            xT_out2(NT - 2, 1)
            scaled_rows(NT - 2, 0, 0)
            scaled_rows(NT - 2, 1, 0)

            def tanh_weights(k, c, j):
                act.wait_ge(aw_lo_ready, freed(c + (k * NT + j)))
                for t in range(NT):
                    last = a.activation(SS[:, j % 2, t, :], alb[:, bass.ds((c + j) * P, P)], ACT.Tanh,
                                        bias=V[:, k % 2, t:t + 1])
                last.then_inc(tanh2_ready, 1)

            def weights_high(k, c, j):
                act.wait_ge(aw_ready, done(c + (k * NT + j)))
                act.wait_ge(agg2_psum, freed(c + (k * NT + j)))
                a.activation(AP[:, j % 2, 0, :, :], SS[:, j % 2, :, :], ACT.Copy,
                             scale=1.0 / A_SCALE).then_inc(aw_hi_ready, 1)

            for k in range(K1):
                more = k + 1 < K1
                row_out(3 + k, NP)
                act.wait_ge(row_stored, 3 + k)
                tanh_weights(k, 0, 0)
                tanh_weights(k, 0, 1)
                weights_high(k, 0, 0)
                weights_high(k, 0, 1)
                tanh_weights(k, 0, 2)
                with pairs(act, NT - 4) as c:
                    steps.enter(c, int(more), 2)
                    for j in range(2):
                        weights_high(k, c, j + 2)
                        tanh_weights(k, c, j + 3)
                        if more:
                            scaled_rows(c, j, k + 1)
                    steps.leave(NT - 4)
                c = NT - 4
                for j in range(4):
                    if j < 2:
                        weights_high(k, c, j + 2)
                    if j < 1:
                        tanh_weights(k, c, j + 3)
                    if more:
                        scaled_rows(c, j, k + 1)

            def xn_later(t, j):
                act.wait_ge(xnT_psum, freed(t + j))
                a.activation(xn_stage[:, j, :], X[:, bass.ds(t + j, 1), :].squeeze(1), ACT.Identity,
                             scale=RSTD[:, bass.ds(t + j, 1)], bias=NMR[:, bass.ds(t + j, 1)]).then_inc(xn_ready, 1)

            act.wait_ge(nmr_ready, 3)
            with pairs(act, NT) as t:
                xn_later(t, 0)
                xn_later(t, 1)
            act.wait_ge(soft_in, 1)
            a.activation(route(0), route(0), ACT.Exp).then_inc(soft_out, 1)

            def xgn_out(e, j):
                act.wait_ge(xgT_psum, freed(e + j))
                a.activation(xgn[:, j % 2, :], xg[:, bass.ds((e + j) % 4, 1), :].squeeze(1), ACT.Identity,
                             scale=slots[0:CAP, 3, bass.ds(e + j, 1)],
                             bias=slots[0:CAP, 4, bass.ds(e + j, 1)]).then_inc(xgn_ready, 1)

            def gelu_out(e, j):
                act.wait_ge(m1_psum, done(e + j))
                act.wait_ge(geT_psum, freed(e + j))
                a.activation(ge[:, j % 2, :], PS[0:CAP, 2 + j % 2, :], ACT.Gelu_apprx_tanh).then_inc(ge_ready, 1)

            got = (got0, got1, got2, got3)
            act.wait_ge(slots_ready, 1)
            act.wait_ge(got0, 16)
            xgn_out(0, 0)
            act.wait_ge(got1, 16)
            xgn_out(0, 1)
            with act.Fori(0, NE - 5, 4) as e:
                for j in range(4):
                    gelu_out(e, j)
                    act.wait_ge(got[(j + 2) % 4], (e + (j + 2)) // 4 * 16 + 16)
                    xgn_out(e, j + 2)
            for j in range(4):
                e = NE - 4
                gelu_out(e, j)
                if j < 2:
                    act.wait_ge(got[(j + 2) % 4], (e + j + 2) // 4 * 16 + 16)
                    xgn_out(e, j + 2)

        @block.tensor
        def _(pe):
            t_ = nc.tensor
            pe.wait_ge(consts, CONSTS)
            pe.wait_ge(edges_ready, 1)
            for s in range(2):
                for h in range(2):
                    last = t_.transpose(PS[:, 6, (2 * s + h) * P:(2 * s + h + 1) * P], edges_f[:, s, h, :], ident[:])
            last.then_inc(edgeT_psum, 1)
            pe.wait_ge(rng_ready, 1)
            for s in range(2):
                for h in range(2):
                    last = t_.transpose(PS[0:NT, 7, (2 * s + h) * P:(2 * s + h + 1) * P], rng_f[:, s, h, :], ident[:])
            last.then_inc(rngT_psum, 1)
            pe.wait_ge(rng_col, 1)
            for s in range(2):
                last = t_.matmul(PS[0:1, 7, s * NT:(s + 1) * NT], rng_c[:, s:s + 1], ident[0:NT, 0:NT],
                                 start=True, stop=True)
            last.then_inc(rng_row_psum, 1)
            pe.wait_ge(rng_row, 1)

            used = pe.alloc_register("oh_used")
            pe.reg_mov(used, 1)
            COLS = [(g, min(512, NP - 512 * g)) for g in range(-(-NP // 512))]

            def zero(n, first):
                for g, w in COLS:
                    last = t_.matmul(PS[:, g, 0:(w if first else n)], zerosb[:, 0:P],
                                     zerosb[:, 0:(w if first else n)], start=first, stop=not first,
                                     skip_group_check=True)
                return last

            def count(b):
                wait_from(pe, c_stored, b * CG)
                zero(512, True)
                lo = pe.value_load(rng_i[0:1, bass.ds(b, 1)], min_val=0, max_val=ET - 1)
                hi = pe.value_load(rng_i[0:1, bass.ds(b + NT, 1)], min_val=0, max_val=ET)
                with pe.Fori(lo, hi, OH) as t:
                    now = pe.snap(used, min_val=1, max_val=2000)
                    for i in range(OH):
                        if i % 2 == 0:
                            pe.wait_ge(oh_ready, now + i // 2)
                        for g, w in COLS:
                            last = t_.matmul(PS[:, g, 0:w], oh_dst[:, i, :], oh_src[:, i, 512 * g:512 * g + w],
                                             start=False, stop=False, skip_group_check=True)
                        if i % 2:
                            last.then_inc(oh_free, 1)
                    pe.reg_add(used, used, OH // 2)
                zero(2, False).then_inc(ct_psum, 1)

            def c_transposes(b):
                pe.wait_ge(ct_staged, b + 1)
                for g in range(CG):
                    for i in range(min(4, NT - 4 * g)):
                        last = t_.transpose(PS[:, g, i * P:(i + 1) * P],
                                            ct_stage[:, (4 * g + i) * P:(4 * g + i + 1) * P], ident[:])
                    last.then_inc(c_psum, 1)

            def part_transposes(t):
                pe.wait_ge(lo_ready, t + 1)
                wait_from(pe, partsT_ready, t)
                for s in range(2):
                    bank = PS[:, 6 + s, :].bitcast(F16)
                    for k in range(KD):
                        last = t_.transpose(bank[:, k * P:(k + 1) * P], x_parts[:, s, k * P:(k + 1) * P], identh[:])
                last.then_inc(parts_psum, 1)

            def h_products(t):
                pe.wait_ge(partsT_ready, t + 1)
                wait_from(pe, h_ready, t)
                for g in range(2):
                    cols = slice(g * HD, (g + 1) * HD)
                    for k in range(KD):
                        for xs, w in ((0, W_hi), (0, W_lo), (1, W_hi)):
                            last = t_.matmul(PS[:, 4 + g, :], xT_parts[:, xs, k, :], w[:, k, cols],
                                             start=(k == 0 and w is W_hi and xs == 0),
                                             stop=(k == KD - 1 and xs == 1))
                last.then_inc(h_psum, 1)

            count(0)
            c_transposes(0)
            part_transposes(0)
            pe.wait_ge(w_lo_ready, 2)
            with pe.Fori(1, NT) as t:
                count(t)
                h_products(t - 1)
                c_transposes(t)
                part_transposes(t)
            h_products(NT - 1)
            pe.wait_ge(c_stored, NT * CG)

            def row_products(n, w):
                pe.wait_ge(diag_ready, n)
                for g in range(-(-w // 512)):
                    c = min(512, w - 512 * g)
                    last = t_.matmul(PS[:, g, 0:c], ones[:], diag[:, 512 * g:512 * g + c], start=True, stop=True)
                last.then_inc(row_psum, 1)

            def agg_products(i, j):
                pe.wait_ge(at_ready, done(i + j))
                pe.wait_ge(x_updated, freed(i + j))
                for t in range(NT):
                    for g in range(2):
                        t_.matmul(PS[:, 3 * j + g, :], AT[:, j, t, :], hbuf[:, t, g * HD:(g + 1) * HD],
                                  start=(t == 0), stop=(t == NT - 1))
                pe.wait_ge(at_summed, i + (j + 1))
                t_.matmul(PS[:, 3 * j + 2, 0:1], at_sum[:, j, :], ones[:, 0:1],
                          start=True, stop=True).then_inc(agg_psum, 1)

            pe.wait_ge(h_ready, NT)
            row_products(1, NP)
            pe.wait_ge(row_stored, 1)
            def ffn_weight_transposes(i, j):
                pe.wait_ge(w_rounded, done(i + j))
                pe.wait_ge(wT_stored, freed(i + j))
                bank = PS[:, 6 + j, :].bitcast(BF16).rearrange("p (k n) -> p k n", n=P)
                if isinstance(i, int) and i >= 2 * FC:
                    for r in range(2):
                        for c in range(FC):
                            n = min(P, FF - c * P)
                            last = t_.transpose(bank[0:n, r * FC + c, :],
                                                w_q[:, j, r * FF + c * P:r * FF + c * P + n], identb[:])
                else:
                    for k in range(KD):
                        last = t_.transpose(bank[:, k, :], w_q[:, j, k * P:(k + 1) * P], identb[:])
                last.then_inc(wT_psum, 1)

            with pairs(pe, 2 * FC) as i:
                agg_products(i, 0)
                agg_products(i, 1)
                ffn_weight_transposes(i, 0)
                ffn_weight_transposes(i, 1)
            for i in range(2 * FC, NT, 2):
                agg_products(i, 0)
                agg_products(i, 1)
                ffn_weight_transposes(i, 0)
                ffn_weight_transposes(i, 1)

            def y_transposes(t, j):
                pe.wait_ge(yq_ready, done(t + j))
                pe.wait_ge(yT_stored, freed(t + j))
                bank = PS[:, 4 + j, :].bitcast(BF16).rearrange("p (k n) -> p k n", n=P)
                for k in range(KD):
                    last = t_.transpose(bank[:, k, :], xq_stage[:, j, k * P:(k + 1) * P], identb[:])
                last.then_inc(yT_psum, 1)

            pe.wait_ge(x_updated, NT + CREDIT)
            with pairs(pe, NT) as t:
                y_transposes(t, 0)
                y_transposes(t, 1)

            pe.wait_ge(yT_stored, NT + CREDIT)
            pe.wait_ge(wT_stored, W_ITEMS + CREDIT)
            with pairs(pe, NG) as g:
                for n in range(2 * FC):
                    i, c, j = n // FC, n % FC, n % 2
                    pe.wait_ge(hT_ready, freed(g * FC + n))
                    for s in range(2):
                        for k in range(KD):
                            last = t_.matmul(PS[:, 2 * j + s, 0:GN], wguT[:, k, s, c * P:(c + 1) * P],
                                             xqT[:, k, bass.ds((g + i) * GN, GN)], start=(k == 0), stop=(k == KD - 1))
                    last.then_inc(gu_psum, 1)

            pe.wait_ge(hT_ready, FC * NG + CREDIT)
            row_products(2, D)
            pe.wait_ge(hq_ready, 1)
            pe.wait_ge(row_stored, 2)

            def down_products(t, j):
                pe.wait_ge(d_scaled, freed(t + j))
                for c in range(FC):
                    n = min(P, FF - c * P)
                    for g in range(2):
                        last = t_.matmul(PS[:, 2 * j + g, :], hq[0:n, c, bass.ds((t + j) * P, P)],
                                         wdT[0:n, c, g * HD:(g + 1) * HD], start=(c == 0), stop=(c == FC - 1))
                last.then_inc(d_psum, 1)

            with pairs(pe, NT) as t:
                down_products(t, 0)
                down_products(t, 1)

            def part_transposes2(t, j):
                pe.wait_ge(lo2_ready, done(t + j))
                pe.wait_ge(parts2T_ready, freed(t + j))
                b = j % 2
                for s in range(2):
                    bank = PS[:, 4 + 2 * b + s, :].bitcast(F16)
                    for k in range(KD):
                        last = t_.transpose(bank[:, k * P:(k + 1) * P], parts2[:, b, s, k * P:(k + 1) * P], identh[:])
                last.then_inc(parts2_psum, 1)

            def x1_products(t, j):
                pe.wait_ge(parts2T_ready, done(t + j))
                pe.wait_ge(x1_ready, freed(t + j))
                for k in range(KD):
                    for xs, w in ((0, W1_hi), (0, W1_lo), (1, W1_hi)):
                        last = t_.matmul(PS[:, j, :], partsT2[:, j, xs, k, :], w[:, k, :],
                                         start=(k == 0 and w is W1_hi and xs == 0), stop=(k == KD - 1 and xs == 1))
                last.then_inc(x1_psum, 1)

            pe.wait_ge(d_scaled, NT + CREDIT)
            pe.wait_ge(w1_lo_ready, 1)
            part_transposes2(0, 0)
            with pairs(pe, NT - 2) as t:
                for j in range(2):
                    part_transposes2(t, j + 1)
                    x1_products(t, j)
            part_transposes2(NT - 2, 1)
            x1_products(NT - 2, 0)
            x1_products(NT - 2, 1)

            def edge_products(k, c, j):
                pe.wait_ge(aw_lo_ready, done(c + (k * NT + j)))
                pe.wait_ge(g_ready, freed(c + (k * NT + j)))
                q = k % 2
                for t in range(NT):
                    for s in range(2):
                        t_.matmul(PS[:, 3 + j, :], AP[:, j, 0, t, :], GS[:, q, s, t, :],
                                  start=(t == 0 and s == 0), stop=(t == NT - 1 and s == 1))
                    last = t_.matmul(PS[:, 5 + j, :], AP[:, j, 1, t, :], GS[:, q, 0, t, :],
                                     start=(t == 0), stop=(t == NT - 1))
                last.then_inc(agg2_psum, 1)

            for k in range(K1):
                row_products(3 + k, NP)
                pe.wait_ge(gs_ready, (k + 1) * NT + CREDIT)
                with pairs(pe, NT) as c:
                    edge_products(k, c, 0)
                    edge_products(k, c, 1)

            def transposes(t, j):
                pe.wait_ge(xn_ready, done(t + j))
                pe.wait_ge(xnT_ready, freed(t + j))
                for k in range(KD):
                    last = t_.transpose(PS[:, 4 + 2 * j + k // 4, (k % 4) * P:(k % 4 + 1) * P],
                                        xn_stage[:, j, k * P:(k + 1) * P], ident[:])
                last.then_inc(xnT_psum, 1)

            pe.wait_ge(gw_in, 16)
            for k in range(KD):
                last = t_.transpose(PS[:, 2, k * NE:(k + 1) * NE], gw_raw[:, k * P:(k + 1) * P], ident[0:NE, 0:NE])
            last.then_inc(gwT_psum, 1)

            def logit_products(t, j):
                pe.wait_ge(xnT_ready, done(t + j))
                pe.wait_ge(lg_ready, freed(t + j))
                for k in range(KD):
                    last = t_.matmul(PS[:, j, 0:NE], xnT_stage[:, j, k, :], gwT[:, k, :],
                                     start=(k == 0), stop=(k == KD - 1))
                last.then_inc(lg_psum, 1)

            pe.wait_ge(gwT_ready, 1)
            pe.wait_ge(g_ready, K1 * NT + CREDIT)
            transposes(0, 0)
            with pairs(pe, NT - 2) as t:
                transposes(t, 1)
                logit_products(t, 0)
                transposes(t + 2, 0)
                logit_products(t, 1)
            transposes(NT - 2, 1)
            logit_products(NT - 2, 0)
            logit_products(NT - 2, 1)
            pe.wait_ge(xnT_ready, NT + CREDIT)
            pe.wait_ge(mask_ready, 1)
            chosen = route(1).rearrange("p t e -> p (t e)")
            t_.matmul(PS[:, 3, 0:NT * NE], tri[:], chosen, start=True, stop=True)
            t_.matmul(PS[:, 4, 0:NT * NE], ones[:], chosen, start=True, stop=True).then_inc(rank_psum, 1)
            pe.wait_ge(cast_ready, 1)
            for t in range(NT):
                last = t_.matmul(PS[0:CAP, 5, 0:NR], slot_of[:, t, :], facts[:, t, :, :].rearrange("p q e -> p (q e)"),
                                 start=(t == 0), stop=(t == NT - 1))
            last.then_inc(slots_psum, 1)
            pe.wait_ge(slots_ready, 1)

            def in_transposes(e, j):
                pe.wait_ge(xgn_ready, done(e + j))
                pe.wait_ge(xgT_ready, e + (j + CREDIT))
                for k in range(KD):
                    last = t_.transpose(PS[:, k // 4, (k % 4) * CAP:(k % 4 + 1) * CAP],
                                        xgn[:, j % 2, k * P:(k + 1) * P], ident[0:CAP, 0:CAP])
                last.then_inc(xgT_psum, 1)

            def into_experts(e, j):
                pe.wait_ge((we1_in0, we1_in1)[j % 2], (e + j) // 2 * 16 + 32)
                pe.wait_ge(xgT_ready, done(e + j))
                pe.wait_ge(ge_ready, freed(e + j))
                w = W1E[:, bass.ds((e + j) % 4, 1)].squeeze(1)
                for k in range(KD):
                    last = t_.matmul(PS[0:CAP, 2 + j % 2, :], xgT[:, j % 2, k, :], w[:, k, :],
                                     start=(k == 0), stop=(k == KD - 1))
                last.then_inc(m1_psum, 1)

            def out_transposes(e, j):
                pe.wait_ge(ge_ready, done(e + j))
                pe.wait_ge(geT_ready, e + (j + CREDIT))
                for k in range(4):
                    last = t_.transpose(PS[:, 4, k * CAP:(k + 1) * CAP], ge[:, j % 2, k * P:(k + 1) * P],
                                        ident[0:CAP, 0:CAP])
                last.then_inc(geT_psum, 1)

            def out_of_experts(e, j):
                pe.wait_ge((we2_in0, we2_in1)[j % 2], (e + j) // 2 * 16 + 32)
                pe.wait_ge(geT_ready, done(e + j))
                pe.wait_ge(o_ready, e + (j + CREDIT))
                w = W2E[:, bass.ds((e + j) % 4, 1)].squeeze(1)
                for k in range(4):
                    for g in range(2):
                        last = t_.matmul(PS[0:CAP, 5 + g, :], geT[:, j % 2, k, :], w[:, k, g * HD:(g + 1) * HD],
                                         start=(k == 0), stop=(k == 3))
                last.then_inc(m2_psum, 1)

            in_transposes(0, 0)
            into_experts(0, 0)
            in_transposes(0, 1)
            out_transposes(0, 0)
            with pe.Fori(0, NE - 3, 2) as e:
                for j in (1, 2):
                    into_experts(e, j)
                    in_transposes(e, j + 1)
                    out_of_experts(e, j - 1)
                    out_transposes(e, j)
            into_experts(NE - 2, 1)
            out_of_experts(NE - 2, 0)
            out_transposes(NE - 2, 1)
            out_of_experts(NE - 2, 1)


_INS = ['x', 'src', 'dst', 'L0_gnn_W', 'L0_gnn_a', 'L0_ffn_clip_x', 'L0_ffn_clip_down', 'L0_ffn_w_gate',
        'L0_ffn_w_up', 'L0_ffn_w_down', 'L1_gnn_W1', 'L1_gnn_b1', 'L1_gnn_Wg', 'L1_gnn_bg',
        'L1_ffn_gate_w', 'L1_ffn_w1', 'L1_ffn_w2']


def build(nc, args):
    n, d = args[0].shape
    out = nc.dram_tensor("out_0_dram", (n, d), F32, kind="ExternalOutput").ap()
    x_rows = nc.dram_tensor("x_rows", (n, d), F32).ap()
    gnn_moe_kernel(nc, *args, out, x_rows)


def kernel(**inputs):
    import numpy as np
    from concourse import bacc
    from concourse.bass_utils import run_bass_kernel_spmd

    nc = bacc.Bacc("TRN2", target_bir_lowering=False, num_devices=1, dynamic_dma_scratch_size=4096)
    arrays, args = {}, []
    for name in _INS:
        a = np.ascontiguousarray(inputs[name])
        arrays[f"in_{name}_dram"] = a
        args.append(nc.dram_tensor(f"in_{name}_dram", a.shape, mybir.dt.from_np(a.dtype), kind="ExternalInput").ap())
    build(nc, args)
    r = run_bass_kernel_spmd(nc, [arrays], core_ids=[0])
    return r.results[0]["out_0_dram"]
```

```python
from contextlib import ExitStack

import concourse.bass as bass
from concourse import mybir

ALU = mybir.AluOpType
ACT = mybir.ActivationFunctionType
AX_X = mybir.AxisListType.X
AX_XY = mybir.AxisListType.XY
F32 = mybir.dt.float32
F16 = mybir.dt.float16
BF16 = mybir.dt.bfloat16
I16 = mybir.dt.int16
I32 = mybir.dt.int32
U32 = mybir.dt.uint32
RMAX = bass.bass_isa.ReduceOp.absmax

P = 128
EPS = 1e-5
MAGIC = 1.5 * 2.0 ** 23
X_SCALE, W_SCALE = 2.0 ** 8, 2.0 ** 10
G_SCALE = 2.0 ** 6
A_SCALE = 2.0 ** 11
NO_NODE = 4096.0
QMAX = 127.0


class Steps:

    def __init__(self, eng, sem):
        self.eng, self.sem, self.base, self.n = eng, sem, 0, 0

    def __call__(self, ins):
        ins.then_inc(self.sem, 1)
        self.n += 1

    def wait(self):
        self.eng.wait_ge(self.sem, self.base + self.n)

    def link(self, ins):
        self(ins)
        self.wait()

    def enter(self, item, per, items=1):
        self.start, self.per, self.items = self.base + self.n, per, items
        self.base, self.n = item * per + self.start, 0

    def leave(self, total):
        assert self.n == self.per * self.items, (self.n, self.per, self.items)
        self.base, self.n = self.start + total * self.per, 0


CREDIT = 2


def done(i):
    return i + (1 + CREDIT)


def freed(i):
    return i + 1


def wait_from(eng, sem, count):
    if not (isinstance(count, int) and count <= 0):
        eng.wait_ge(sem, count)


def pairs(eng, n):
    return eng.Fori(0, n - 1, 2)


def gnn_moe_kernel(nc, x, src, dst, L0_gnn_W, L0_gnn_a, L0_ffn_clip_x, L0_ffn_clip_down, L0_ffn_w_gate,
                   L0_ffn_w_up, L0_ffn_w_down, L1_gnn_W1, L1_gnn_b1, L1_gnn_Wg, L1_gnn_bg,
                   L1_ffn_gate_w, L1_ffn_w1, L1_ffn_w2, out, x_rows):
    N, D = x.shape
    E = src.shape[0]
    NT = -(-N // P)
    NP = NT * P
    LAST = N - (NT - 1) * P
    KD = D // P
    ET = -(-E // P)
    EA = ET - P
    HD = D // 2
    FF = L0_ffn_w_gate.shape[0]
    FC = -(-FF // P)
    H1 = L1_gnn_W1.shape[1]
    K1 = L1_gnn_Wg.shape[0]
    NE = L1_ffn_gate_w.shape[0]
    CAP = int(1.25 * N / NE)
    CAP += CAP % 2
    assert (NT % 2, LAST > 0, H1, HD, KD) == (0, True, 512, 512, 8) and P < ET <= 2 * P - 4

    ctx = ExitStack()
    with ctx:
        def sb(name, shape, dt):
            return ctx.enter_context(nc.sbuf_tensor(name, shape, dt))

        def sem(name):
            return ctx.enter_context(nc.semaphore(name))

        arena = sb("arena", [P, 32768], F32)
        X = sb("X", [P, NT, D], F32)
        STG = sb("STG", [P, 4096], F32)
        BD = sb("BD", [P, 2 * NP], F32)
        PS = ctx.enter_context(nc.psum_tensor("PS", [P, 8, 512], F32))

        def part(at, size, dt=F32):
            a = arena[:, at:at + size]
            return a if dt is F32 else a.bitcast(dt)

        HB0 = 0
        CC0 = NT * D + 256
        CT0 = CC0 + NT * NP // 2
        GW0 = CT0 + NT * NP // 2
        C = part(CC0, NT * NP // 2, I16).rearrange("p (t n) -> p t n", t=NT)
        CT = part(CT0, NT * NP // 2, I16).rearrange("p (t n) -> p t n", t=NT)
        hbuf = part(HB0, NT * D).rearrange("p (t d) -> p t d", t=NT)
        ct_stage = part(HB0 + (NT - 1) * D, NP)
        W_raw = part(HB0, KD * D).rearrange("p (k n) -> p k n", k=KD)
        W_hi = part(GW0, KD * D // 2, F16).rearrange("p (k n) -> p k n", k=KD)
        W_lo = part(GW0 + KD * D // 2, KD * D // 2, F16).rearrange("p (k n) -> p k n", k=KD)
        junk = part(GW0 + KD * D, D)
        xn_stage = STG[:, 0:2 * D].rearrange("p (b d) -> p b d", b=2)
        ln_x = STG[:, D:2 * D]
        x_parts = STG[:, 2 * D:3 * D].bitcast(F16).rearrange("p (s d) -> p s d", s=2)
        xT_parts = STG[:, 3 * D:4 * D].bitcast(F16).rearrange("p (s k n) -> p s k n", s=2, k=KD)
        a_row = BD[:, 0:2 * D].rearrange("p (s d) -> p s d", s=2)
        alb = BD[:, 0:NP]
        diag = BD[:, NP:2 * NP]

        AT = STG[:, 0:2 * NP].rearrange("p (b t n) -> p b t n", b=2, t=NT)
        S = STG[:, 2 * NP:3 * NP].rearrange("p (t n) -> p t n", t=NT)
        FFP = FC * P
        wguT = part(GW0, KD * 2 * FFP // 2, BF16).rearrange("p (k s f) -> p k s f", k=KD, s=2)
        wdT = part(GW0 + 3072, FC * D // 2, BF16).rearrange("p (c d) -> p c d", c=FC)
        w_raw = part(GW0 + 4608, 2 * D).rearrange("p (b d) -> p b d", b=2)
        w_q = part(GW0 + 6656, D, BF16).rearrange("p (b d) -> p b d", b=2)
        tmp_m = part(GW0 + 7680, D)
        tmp_p = BD[:, NP:NP + D]
        gu_tmp = w_raw[:, :, 0:320]
        xqT = part(HB0, KD * NP // 2, BF16).rearrange("p (k n) -> p k n", k=KD)
        xq_stage = STG[:, 2 * D:3 * D].bitcast(BF16).rearrange("p (b d) -> p b d", b=2)
        hT = part(HB0 + 5120, FC * NP).rearrange("p (c n) -> p c n", c=FC)
        hq = part(HB0, FC * NP // 2, BF16).rearrange("p (c n) -> p c n", c=FC)

        W1_raw = part(CT0, KD * H1).rearrange("p (k n) -> p k n", k=KD)
        W1_hi = STG[:, 0:KD * H1 // 2].bitcast(F16).rearrange("p (k n) -> p k n", k=KD)
        W1_lo = STG[:, KD * H1 // 2:KD * H1].bitcast(F16).rearrange("p (k n) -> p k n", k=KD)
        G = part(HB0, NT * H1).rearrange("p (t h) -> p t h", t=NT)
        L0 = HB0 + NT * H1
        ln2 = part(L0, D)
        parts2 = part(L0 + D, 2 * D, F16).rearrange("p (b s d) -> p b s d", b=2, s=2)
        partsT2 = part(L0 + 3 * D, 2 * D, F16).rearrange("p (b s k n) -> p b s k n", b=2, s=2, k=KD)
        b1_row = part(CT0 + 4096, H1)
        wg_row = part(CT0 + 4608, 2 * H1).rearrange("p (s h) -> p s h", s=2)
        GS = part(CT0 + 5632, 2 * NT * H1, F16).rearrange("p (q s t h) -> p q s t h", q=2, s=2, t=NT)
        gs_raw = part(CT0, H1)
        SS = part(CT0 + H1, 2 * NP).rearrange("p (b t n) -> p b t n", b=2, t=NT)
        AP = STG[:, 0:2 * NP].bitcast(F16).rearrange("p (b s t n) -> p b s t n", b=2, s=2, t=NT)
        agg_row = part(CT0 + H1 + 2 * NP, H1)
        dot_out = part(CT0 + 2 * H1 + 2 * NP, H1)
        u_diag = part(HB0 + NT * D, 2 * P).rearrange("p (b n) -> p b n", b=2)
        u_row = BD[:].rearrange("p (q n) -> p q n", q=2)
        W1E = arena[:].rearrange("p (b s k f) -> p b s k f", b=4, s=2, f=512)[:, :, 1]
        W2E = arena[:].rearrange("p (b s m) -> p b s m", b=4, s=2)[:, :, 0].rearrange("p b (k d) -> p b k d", k=4)
        Xf = X[:].rearrange("p t d -> p (t d)")
        xg = Xf[0:CAP, 0:4 * D].rearrange("p (b d) -> p b d", b=4)
        xgn = Xf[0:CAP, 4 * D:6 * D].rearrange("p (b d) -> p b d", b=2)
        xgT = Xf[:, 6 * D:6 * D + 2 * KD * CAP].rearrange("p (b k c) -> p b k c", b=2, k=KD)
        ge = Xf[0:CAP, 8 * D:9 * D].rearrange("p (b f) -> p b f", b=2)
        geT = Xf[:, 9 * D:9 * D + 8 * CAP].rearrange("p (b k c) -> p b k c", b=2, k=4)
        o_stage = BD[0:CAP, 0:2 * D].rearrange("p (b d) -> p b d", b=2)
        x_copy = STG[:, 3 * D:4 * D]
        xT = part(L0, 2 * D).rearrange("p (b k n) -> p b k n", b=2, k=KD)
        gw_raw = part(L0 + 2 * D, D)[0:NE]
        gwT = STG[:, 2 * NP:2 * NP + KD * NE].rearrange("p (k e) -> p k e", k=KD)
        NR = 5 * NE
        slot_of = STG[:, 0:NT * CAP].rearrange("p (t c) -> p t c", t=NT)
        facts = STG[:, 2 * D:2 * D + NT * NR].rearrange("p (t q e) -> p t q e", t=NT, q=5)

        def route(i):
            return STG[:, 3 * D + i * NT * NE:3 * D + (i + 1) * NT * NE].rearrange("p (t e) -> p t e", t=NT)

        ident = sb("ident", [P, P], F32)
        tri = sb("tri", [P, P], F32)
        node_id = sb("node_id", [P, NT], F32)
        exp_id = sb("exp_id", [P, NE], F32)
        dis_in = sb("dis_in", [P, NT], F32)
        dis_out = sb("dis_out", [P, NT], F32)
        dis = sb("dis", [P, NT], F32)
        bg_row = sb("bg_row", [P, K1], F32)
        U = sb("U", [P, NT], F32)
        V = sb("V", [P, 2, NT], F32)
        gw_sum = sb("gw_sum", [P, NE], F32)
        lg_mean = sb("lg_mean", [P, NT, NE], F32)
        LG = sb("LG", [P, NT, NE], F32)
        lg_top = sb("lg_top", [P, NT], F32)
        valid = sb("valid", [P, NT], F32)
        first = sb("first", [P, NT], F32)
        wt = sb("wt", [P, NT], F32)
        rank1 = sb("rank1", [P, NT], F32)
        slots = sb("slots", [P, 5, NE], F32)
        take = sb("take", [P, NE], I32)
        give = sb("give", [P, NE], I32)
        away = sb("away", [P, NE], F32)
        identb = sb("identb", [P, P], BF16)
        identh = sb("identh", [P, P], F16)
        st_one = sb("st_one", [P, 2, 6], F32)
        mv_one = sb("mv_one", [P, 2], F32)
        neg_mean = sb("neg_mean", [P, NT], F32)
        ones = sb("ones", [P, P], F32)
        zerosb = sb("zerosb", [P, 512], BF16)
        iota_n = sb("iota_n", [P, NP], F16)
        OH = 4
        oh_dst = sb("oh_dst", [P, OH, P], BF16)
        oh_src = sb("oh_src", [P, OH, NP], BF16)
        edges_i = STG[:, 0:4 * P].bitcast(I32).rearrange("p (s h e) -> p s h e", s=2, h=2)
        edges_f = STG[:, 4 * P:8 * P].rearrange("p (s h e) -> p s h e", s=2, h=2)
        edgeT = sb("edgeT", [P, 2, 2 * P], F32)
        tile_lo = sb("tile_lo", [P, 2], F32)
        tile_hi = sb("tile_hi", [P, 2], F32)
        tile_id = sb("tile_id", [P, 2], F32)
        block_lo = sb("block_lo", [P, NT], F32)
        cross = sb("cross", [P, 2, 2, NT], F32)
        rng_f = sb("rng_f", [P, 2, 2, NT], F32)
        rng_c = sb("rng_c", [NT, 2], F32)
        rng_i = sb("rng_i", [1, 2 * NT], I32)
        deg = sb("deg", [P, NT], F32)
        bst = sb("bst", [P, NT, 2, 6], F32)
        MV = sb("MV", [P, NT, 2], F32)
        var_e = sb("var_e", [P, NT], F32)
        neg_half = sb("neg_half", [P, NT], F32)
        RSTD = sb("RSTD", [P, NT], F32)
        NMR = sb("NMR", [P, NT], F32)
        AL = sb("AL", [P, 2, NT], F32)

        at_sum = sb("at_sum", [P, 2, P], F32)
        rs = sb("rs", [P, 2], F32)
        w_max = sb("w_max", [P, 16], F32)
        w_inv = sb("w_inv", [P, 16], F32)
        clips = sb("clips", [P, 2], F32)
        sig = sb("sig", [P, 2], F32)
        x_max = sb("x_max", [P, NT], F32)
        x_min = sb("x_min", [P, NT], F32)
        top = sb("top", [P, 4], F32)
        s_act = sb("s_act", [P, 4], F32)
        qscale = sb("qscale", [P, NT], F32)
        qbias = sb("qbias", [P, NT], F32)
        s_half = sb("s_half", [P, FC], F32)
        s_gu = sb("s_gu", [P, FC], F32)
        s_down = sb("s_down", [P, KD], F32)

        x_first_in = sem("x_first_in")
        x_in = sem("x_in")
        w_hi_ready = sem("w_hi_ready")
        w_lo_ready = sem("w_lo_ready")
        stats_ready = sem("stats_ready")
        norm_ready = sem("norm_ready")
        ln_ready = sem("ln_ready")
        hi_ready = sem("hi_ready")
        lo_ready = sem("lo_ready")
        parts_psum = sem("parts_psum")
        partsT_ready = sem("partsT_ready")
        w_in = sem("w_in")
        a_in = sem("a_in")
        edges_in = sem("edges_in")
        pad_set = sem("pad_set")
        consts = sem("consts")
        pool_s = sem("pool_s")
        dve_s = sem("dve_s")
        act_s = sem("act_s")
        edges_ready = sem("edges_ready")
        edgeT_psum = sem("edgeT_psum")
        rng_ready = sem("rng_ready")
        rngT_psum = sem("rngT_psum")
        rng_col = sem("rng_col")
        rng_row_psum = sem("rng_row_psum")
        rng_row = sem("rng_row")
        oh_ready = sem("oh_ready")
        oh_free = sem("oh_free")
        ct_psum = sem("ct_psum")
        ct_psum_free = sem("ct_psum_free")
        ct_staged = sem("ct_staged")
        ct_stored = sem("ct_stored")
        c_psum = sem("c_psum")
        c_stored = sem("c_stored")
        var_ready = sem("var_ready")
        rstd_ready = sem("rstd_ready")
        nmr_ready = sem("nmr_ready")
        h_psum = sem("h_psum")
        h_ready = sem("h_ready")
        clips_in = sem("clips_in")
        wraw_in0 = sem("wraw_in0")
        wraw_in1 = sem("wraw_in1")
        diag_ready = sem("diag_ready")
        row_psum = sem("row_psum")
        row_stored = sem("row_stored")
        sum_ready = sem("sum_ready")
        act_out = sem("act_out")
        at_ready = sem("at_ready")
        agg_psum = sem("agg_psum")
        m_ready = sem("m_ready")
        e_ready = sem("e_ready")
        x_updated = sem("x_updated")
        w_scaled = sem("w_scaled")
        w_rounded = sem("w_rounded")
        wT_psum = sem("wT_psum")
        wT_stored = sem("wT_stored")
        sig_ready = sem("sig_ready")
        max_ready = sem("max_ready")
        max_all = sem("max_all")
        qs_ready = sem("qs_ready")
        y_ready = sem("y_ready")
        yq_ready = sem("yq_ready")
        yT_psum = sem("yT_psum")
        yT_stored = sem("yT_stored")
        gu_psum = sem("gu_psum")
        tanh_ready = sem("tanh_ready")
        hT_ready = sem("hT_ready")
        hmax_ready = sem("hmax_ready")
        hmax_all = sem("hmax_all")
        hq_ready = sem("hq_ready")
        d_psum = sem("d_psum")
        d_scaled = sem("d_scaled")
        d_added = sem("d_added")

        wpad_set = sem("wpad_set")


        NG, GN = NP // 320, 320
        W_ITEMS = 2 * FC + KD // 2
        assert W_ITEMS == NT
        w1_in = sem("w1_in")
        b1_in = sem("b1_in")
        wg_in = sem("wg_in")
        dis_deg = sem("dis_deg")
        dis_ready = sem("dis_ready")
        dis_scaled = sem("dis_scaled")
        w1_scaled = sem("w1_scaled")
        w1_hi_ready = sem("w1_hi_ready")
        w1_lo_ready = sem("w1_lo_ready")
        hi2_ready = sem("hi2_ready")
        lo2_ready = sem("lo2_ready")
        parts2_psum = sem("parts2_psum")
        parts2T_ready = sem("parts2T_ready")
        gs_made = sem("gs_made")
        tanh2_ready = sem("tanh2_ready")
        aw_ready = sem("aw_ready")
        aw_hi_ready = sem("aw_hi_ready")
        aw_lo_ready = sem("aw_lo_ready")
        at_summed = sem("at_summed")
        diag2_ready = sem("diag2_ready")
        u_psum = sem("u_psum")
        u_stored = sem("u_stored")
        early_tanh = sem("early_tanh")
        early_aw = sem("early_aw")
        early_hi = sem("early_hi")
        early_lo = sem("early_lo")
        x1_psum = sem("x1_psum")
        x1_ready = sem("x1_ready")
        gs_ready = sem("gs_ready")
        uv_ready = sem("uv_ready")
        sum2_ready = sem("sum2_ready")
        agg2_psum = sem("agg2_psum")
        g_ready = sem("g_ready")
        xl_added = sem("xl_added")
        x_final = sem("x_final")
        rows_out = sem("rows_out")
        gw_in = sem("gw_in")
        xcopy_ready = sem("xcopy_ready")
        xT_psum = sem("xT_psum")
        xT_ready = sem("xT_ready")
        gwT_psum = sem("gwT_psum")
        gws_psum = sem("gws_psum")
        gws_ready = sem("gws_ready")
        gwT_ready = sem("gwT_ready")
        lg_psum = sem("lg_psum")
        lg_ready = sem("lg_ready")
        soft_in = sem("soft_in")
        soft_out = sem("soft_out")
        mask_ready = sem("mask_ready")
        rank_psum = sem("rank_psum")
        cast_ready = sem("cast_ready")
        slots_psum = sem("slots_psum")
        slots_ready = sem("slots_ready")
        we1_in0 = sem("we1_in0")
        we1_in1 = sem("we1_in1")
        we2_in0 = sem("we2_in0")
        we2_in1 = sem("we2_in1")
        got0 = sem("got0")
        got1 = sem("got1")
        got2 = sem("got2")
        got3 = sem("got3")
        xgn_ready = sem("xgn_ready")
        xgT_psum = sem("xgT_psum")
        xgT_ready = sem("xgT_ready")
        m1_psum = sem("m1_psum")
        ge_ready = sem("ge_ready")
        geT_psum = sem("geT_psum")
        geT_ready = sem("geT_ready")
        m2_psum = sem("m2_psum")
        o_ready = sem("o_ready")
        sent0 = sem("sent0")
        sent1 = sem("sent1")

        CONSTS = 13
        FT = NT - 2
        CG = -(-NT // 4)

        block = ctx.enter_context(nc.Block())

        @block.sync
        def _(sp):
            for s in (oh_free, xcopy_ready, xT_psum, xT_ready,
                      act_out, at_ready, agg_psum, x_updated, w_rounded, wT_psum, wT_stored, y_ready, yq_ready, yT_psum,
                      yT_stored, gu_psum, tanh_ready, hT_ready, d_psum, d_scaled, d_added, x1_psum, x1_ready, hi2_ready, lo2_ready, parts2_psum, parts2T_ready,
                      gs_ready, gs_made, diag2_ready, u_psum, u_stored, aw_ready, aw_hi_ready, aw_lo_ready, agg2_psum, g_ready, lg_psum,
                      lg_ready, xgn_ready, xgT_psum, xgT_ready, m1_psum, ge_ready, geT_psum, geT_ready, m2_psum, o_ready):
                sp.sem_inc(s, CREDIT)
            for s in (we1_in0, we1_in1, we2_in0, we2_in1):
                sp.sem_inc(s, 16)
            sp.wait_ge(pad_set, 1)
            for s, e in enumerate((dst, src)):
                full = P * P
                rows = (E - full) // P
                rest = E - full - rows * P
                sp.dma_start(edges_i[:, s, 0, :], e[0:full].rearrange("(t e) -> t e", e=P)).then_inc(edges_in, 16)
                sp.dma_start(edges_i[0:rows, s, 1, :],
                             e[full:full + rows * P].rearrange("(t e) -> t e", e=P)).then_inc(edges_in, 16)
                if rest:
                    sp.dma_start(edges_i[rows:rows + 1, s, 1, 0:rest],
                                 e[E - rest:E].rearrange("(t e) -> t e", t=1)).then_inc(edges_in, 16)
            sp.wait_ge(pad_set, 2)
            sp.dma_start(X[:, 0:2, :], x[0:2 * P, :].rearrange("(t p) d -> p t d", p=P)).then_inc(x_first_in, 16)
            sp.dma_start(W_raw, L0_gnn_W.rearrange("(k p) n -> p k n", p=P)).then_inc(w_in, 16)
            sp.dma_start(X[:, 2:NT - 1, :],
                         x[2 * P:(NT - 1) * P, :].rearrange("(t p) d -> p t d", p=P)).then_inc(x_in, 16)
            sp.dma_start(X[0:LAST, NT - 1, :], x[(NT - 1) * P:N, :]).then_inc(x_in, 16)
            for i, clip in enumerate((L0_ffn_clip_x, L0_ffn_clip_down)):
                sp.dma_start(clips[:, i:i + 1], clip.partition_broadcast(P)).then_inc(clips_in, 16)
            sp.dma_start(a_row.rearrange("p s d -> p (s d)"), L0_gnn_a[0, :].partition_broadcast(P)).then_inc(a_in, 16)

            sp.wait_ge(h_psum, NT)
            for i in range(W_ITEMS):
                b = i % 2
                sp.wait_ge(w_rounded, freed(i))
                sem_b = (wraw_in0, wraw_in1)[b]
                if i < 2 * FC:
                    w = (L0_ffn_w_gate, L0_ffn_w_up)[i % 2]
                    r0 = i // 2 * P
                    n = min(P, FF - r0)
                    if n < P:
                        sp.wait_ge(wpad_set, i % 2 + 1)
                    sp.dma_start(w_raw[0:n, b, :], w[r0:r0 + n, :]).then_inc(sem_b, 16)
                else:
                    r0 = (i - 2 * FC) * 2 * P
                    sp.dma_start(w_raw[:, b, 0:2 * FF].rearrange("p (r f) -> p r f", r=2),
                                 L0_ffn_w_down[r0:r0 + 2 * P, :].rearrange("(r p) f -> p r f", p=P)
                                 ).then_inc(sem_b, 16)


            sp.wait_ge(x_updated, NT + CREDIT)
            sp.dma_start(W1_raw, L1_gnn_W1.rearrange("(k p) n -> p k n", p=P)).then_inc(w1_in, 16)
            sp.dma_start(b1_row, L1_gnn_b1.partition_broadcast(P)).then_inc(b1_in, 16)
            sp.dma_start(bg_row[:], L1_gnn_bg.rearrange("k o -> (k o)").partition_broadcast(P)).then_inc(b1_in, 16)
            for k in range(K1):
                if k:
                    sp.wait_ge(uv_ready, k * NT)
                if k == 1:
                    sp.wait_ge(x1_psum, NT + CREDIT)
                    sp.dma_start(gw_raw, L1_ffn_gate_w).then_inc(gw_in, 16)
                sp.dma_start(wg_row.rearrange("p s h -> p (s h)"),
                             L1_gnn_Wg[k].rearrange("h o -> (h o)").partition_broadcast(P)).then_inc(wg_in, 16)

            sp.wait_ge(agg2_psum, (K1 - 1) * NT + CREDIT)
            sp.dma_start(W1E[:, 3], L1_ffn_w1[0].rearrange("(k p) f -> p k f", p=P)).then_inc(we1_in0, 16)

            for t in range(NT):
                n = min(P, N - t * P)
                sp.wait_ge(x_final, t + 1)
                sp.dma_start(x_rows[t * P:t * P + n, :], X[0:n, t, :]).then_inc(rows_out, 16)
                sp.dma_start(out[t * P:t * P + n, :], X[0:n, t, :]).then_inc(rows_out, 16)
            sp.wait_ge(lg_psum, NT + CREDIT)

            def load_expert(e, j):
                sp.wait_ge(m2_psum, e + (j - 1))
                for w, m, s in ((L1_ffn_w1, W1E, (we1_in0, we1_in1)[j % 2]),
                                (L1_ffn_w2, W2E, (we2_in0, we2_in1)[j % 2])):
                    sp.wait_ge(s, (e // 2 + (j // 2 + 1)) * 16)
                    sp.dma_start(m[:, 3 - j], w[bass.ds(e + j, 1)].rearrange("o (k p) f -> p (o k) f", p=P)
                                 ).then_inc(s, 16)

            for e in range(4):
                if e == 2:
                    for s in (got0, got1, got2, got3):
                        sp.wait_ge(s, 16)
                for w, m, s in ((L1_ffn_w1, W1E, (we1_in0, we1_in1)[e % 2]), (L1_ffn_w2, W2E, (we2_in0, we2_in1)[e % 2])):
                    if w is L1_ffn_w1 and e == 0:
                        continue
                    sp.wait_ge(s, (e // 2 + 1) * 16)
                    sp.dma_start(m[:, 3 - e], w[e].rearrange("(k p) f -> p k f", p=P)).then_inc(s, 16)
            with sp.Fori(4, NE - 3, 4) as e:
                for j in range(4):
                    load_expert(e, j)

            sp.wait_ge(rows_out, 2 * NT * 16)
            sp.wait_ge(sent0, NE // 2 * 16)
            sp.wait_ge(sent1, NE // 2 * 16)

        @block.gpsimd
        def _(pool):
            nc.gpsimd.memset(edges_i[:, :, 1, :], int(NO_NODE)).then_inc(pad_set, 1)
            nc.gpsimd.memset(X[:, NT - 1, :], 0.0).then_inc(pad_set, 1)
            ps = Steps(pool, pool_s)
            ps(nc.gpsimd.memset(ident[:], 0.0))
            nc.gpsimd.iota(tile_id[:], pattern=[[P, 2]], base=0, channel_multiplier=1,
                           allow_small_or_imprecise_dtypes=True).then_inc(consts, 1)
            nc.gpsimd.iota(block_lo[:], pattern=[[P, NT]], base=0, channel_multiplier=0,
                           allow_small_or_imprecise_dtypes=True).then_inc(consts, 1)
            ps.wait()
            nc.gpsimd.affine_select(out=ident[:], in_=ident[:], compare_op=ALU.not_equal, fill=1.0, base=0,
                                    pattern=[[-1, P]], channel_multiplier=1).then_inc(consts, 1)
            nc.gpsimd.iota(iota_n[:], pattern=[[1, NP]], base=0, channel_multiplier=0,
                           allow_small_or_imprecise_dtypes=True).then_inc(consts, 1)
            nc.gpsimd.memset(zerosb[:], 0.0).then_inc(consts, 1)
            nc.gpsimd.memset(ones[:], 1.0).then_inc(consts, 1)
            nc.gpsimd.memset(neg_half[:], -0.5).then_inc(consts, 1)
            pool.wait_ge(consts, 7)
            nc.gpsimd.affine_select(out=tri[:], in_=ones[:], compare_op=ALU.is_gt, fill=0.0, base=0,
                                    pattern=[[1, P]], channel_multiplier=-1).then_inc(consts, 1)
            nc.gpsimd.iota(node_id[:], pattern=[[P, NT]], base=0, channel_multiplier=1,
                           allow_small_or_imprecise_dtypes=True).then_inc(consts, 1)
            nc.gpsimd.iota(exp_id[:], pattern=[[1, NE]], base=0, channel_multiplier=0,
                           allow_small_or_imprecise_dtypes=True).then_inc(consts, 1)
            pool.wait_ge(consts, 10)
            nc.gpsimd.tensor_scalar(valid[:], node_id[:], float(N), None, ALU.is_lt).then_inc(consts, 1)
            nc.gpsimd.tensor_copy(identb[:], ident[:]).then_inc(consts, 1)
            nc.gpsimd.tensor_copy(identh[:], ident[:]).then_inc(consts, 1)

            def norm(t):
                c = bass.ds(t, 1)
                pool.wait_ge(stats_ready, t + 1)
                ps.link(nc.gpsimd.tensor_tensor(RSTD[:, c], var_e[:, c], neg_half[:, 0:1], ALU.pow))
                nc.gpsimd.tensor_tensor(NMR[:, c], neg_mean[:, c], RSTD[:, c], ALU.mult).then_inc(norm_ready, 1)

            def lo_part(t):
                pool.wait_ge(hi_ready, t + 1)
                wait_from(pool, parts_psum, t)
                nc.gpsimd.tensor_tensor(x_parts[:, 1, :], ln_x, x_parts[:, 0, :], ALU.subtract).then_inc(lo_ready, 1)

            def ct_store(t):
                pool.wait_ge(ct_staged, t + 1)
                nc.gpsimd.tensor_copy(CT[:, bass.ds(t, 1), :], ct_stage.unsqueeze(1)).then_inc(ct_stored, 1)

            norm(0)
            pool.wait_ge(w_hi_ready, 2)
            nc.gpsimd.tensor_tensor(W_lo[:, 0:KD // 2, :], W_raw[:, 0:KD // 2, :], W_hi[:, 0:KD // 2, :],
                                    ALU.subtract).then_inc(w_lo_ready, 1)
            lo_part(0)
            norm(1)
            ct_store(0)
            with pool.Fori(1, NT - 1) as t:
                ps.enter(t - 1, 1)
                lo_part(t)
                norm(t + 1)
                ct_store(t)
                ps.leave(NT - 2)
            lo_part(NT - 1)
            ct_store(NT - 1)

            def rstd():
                nc.gpsimd.tensor_tensor(RSTD[:], var_e[:], neg_half[:], ALU.pow).then_inc(rstd_ready, 1)

            for i in range(W_ITEMS):
                b = i % 2
                pool.wait_ge(w_scaled, i + 1)
                pool.wait_ge(wT_psum, freed(i))
                if i < 2 * FC:
                    parts = [(w_raw[:, b, :], w_inv[:, i:i + 1], w_q[:, b, :])]
                else:
                    parts = [(w_raw[:, b, r * FF:(r + 1) * FF], w_inv[:, w:w + 1], w_q[:, b, r * FF:(r + 1) * FF])
                             for r in range(2) for w in [2 * FC + 2 * (i - 2 * FC) + r]]
                for raw, inv, _ in parts:
                    ps(nc.gpsimd.tensor_scalar(raw, raw, inv, MAGIC, ALU.mult, ALU.add))
                ps.wait()
                for raw, _, q in parts:
                    last = nc.gpsimd.tensor_scalar(q, raw, -MAGIC, 1.0, ALU.add, ALU.mult)
                last.then_inc(w_rounded, 1)
                if 2 * FC - 4 <= i < 2 * FC - 2:
                    pool.wait_ge(w_rounded, done(i))
                    nc.gpsimd.memset(w_raw[FF % P:P, b, :], 0.0).then_inc(wpad_set, 1)
                    pool.wait_ge(wpad_set, b + 1)

            pool.wait_ge(var_ready, 1)
            rstd()
            for n in range(2):
                pool.wait_ge(max_ready, n + 1)
                nc.gpsimd.partition_all_reduce(top[:, 2 * n + 1:2 * n + 2], top[:, 2 * n:2 * n + 1], P,
                                               RMAX).then_inc(max_all, 1)
                if n == 0:
                    pool.wait_ge(w1_hi_ready, 1)
                    nc.gpsimd.tensor_tensor(W1_lo, W1_raw, W1_hi, ALU.subtract).then_inc(w1_lo_ready, 1)

            def add_down(t, j):
                pool.wait_ge(d_scaled, done(t + j))
                xt = X[:, bass.ds(t + j, 1), :].squeeze(1)
                nc.gpsimd.tensor_tensor(xt, xt, w_raw[:, j, :], ALU.add).then_inc(d_added, 1)

            with pairs(pool, NT) as t:
                add_down(t, 0)
                add_down(t, 1)

            pool.wait_ge(dis_deg, 1)
            nc.gpsimd.tensor_tensor(dis[:], dis[:], neg_half[:], ALU.pow).then_inc(dis_ready, 1)
            pool.wait_ge(var_ready, 2)
            rstd()

            def gs_low(k, t, j):
                n = k * NT + j
                pool.wait_ge(gs_made, done(t + n))
                q = (k + 1) % 2
                nc.gpsimd.tensor_tensor(GS[:, q, 1, bass.ds(t + j, 1), :].squeeze(1), gs_raw,
                                        GS[:, q, 0, bass.ds(t + j, 1), :].squeeze(1), ALU.subtract).then_inc(gs_ready, 1)

            with pool.Fori(0, NT) as t:
                pool.wait_ge(x1_ready, done(t))
                xl = X[:, bass.ds(t, 1), 0:HD].squeeze(1)
                nc.gpsimd.tensor_tensor(xl, xl, G[:, bass.ds(t, 1), :].squeeze(1), ALU.add).then_inc(xl_added, 1)
                gs_low(0, t, 0)
            for k in range(1, K1):
                with pool.Fori(0, NT) as t:
                    gs_low(k, t, 0)

            pool.wait_ge(var_ready, 3)
            rstd()

            def fetch(e):
                pool.wait_ge(o_ready, e - 1)
                nc.gpsimd.indirect_dma_start(
                    out=xg[:, e % 4, :], out_offset=None, in_=x_rows,
                    in_offset=bass.IndirectOffsetOnAxis(ap=take[0:CAP, e:e + 1], axis=0)
                ).then_inc((got0, got1, got2, got3)[e % 4], 16)

            def send(e):
                pool.wait_ge(o_ready, done(e))
                nc.gpsimd.indirect_dma_start(
                    out=out, out_offset=bass.IndirectOffsetOnAxis(ap=give[0:CAP, e:e + 1], axis=0),
                    in_=o_stage[:, e % 2, :], in_offset=None, bounds_check=N - 1, oob_is_err=False
                ).then_inc((sent0, sent1)[e % 2], 16)

            pool.wait_ge(rows_out, 2 * NT * 16)
            pool.wait_ge(slots_ready, 1)
            for e in range(min(4, NE)):
                nc.gpsimd.indirect_dma_start(
                    out=xg[:, e % 4, :], out_offset=None, in_=x_rows,
                    in_offset=bass.IndirectOffsetOnAxis(ap=take[0:CAP, e:e + 1], axis=0)
                ).then_inc((got0, got1, got2, got3)[e % 4], 16)
            for e in range(NE):
                send(e)
                if e + 4 < NE:
                    fetch(e + 4)

        @block.vector
        def _(dve):
            st = Steps(dve, dve_s)
            v = nc.vector

            def row_stats(t):
                for g in range(2):
                    st(v.bn_stats(bst[:, bass.ds(t, 1), g, :].squeeze(1),
                                  X[:, bass.ds(t, 1), g * HD:(g + 1) * HD].squeeze(1)))

            def variances(scale=1.0):
                st.wait()
                for t in range(NT):
                    st(v.bn_aggr(MV[:, t, :], bst[:, t, :, :]))
                st.wait()
                v.tensor_scalar(var_e[:], MV[:, :, 1], EPS, scale ** -2, ALU.add, ALU.mult).then_inc(var_ready, 1)

            def means(n):
                dve.wait_ge(rstd_ready, n)
                v.scalar_tensor_tensor(out=NMR[:], in0=MV[:, :, 0], scalar=-1.0, in1=RSTD[:],
                                       op0=ALU.mult, op1=ALU.mult).then_inc(nmr_ready, 1)

            dve.wait_ge(edges_in, 16 * 6)
            dve.wait_ge(consts, CONSTS)
            v.tensor_copy(edges_f.rearrange("p a b c -> p (a b c)"),
                          edges_i.rearrange("p a b c -> p (a b c)")).then_inc(edges_ready, 1)
            dve.wait_ge(edges_ready, 1)
            st(v.tensor_reduce(tile_lo[:], edges_f[:, 0, :, :], AX_X, ALU.min))
            st(v.tensor_reduce(tile_hi[:], edges_f[:, 0, :, :], AX_X, ALU.max))
            st.wait()
            for h in range(2):
                st(v.tensor_scalar(cross[:, 0, h, :], block_lo[:], tile_hi[:, h:h + 1], None, ALU.is_le))
                st(v.tensor_scalar(cross[:, 1, h, :], block_lo[:], float(P - 1), tile_lo[:, h:h + 1],
                                   ALU.add, ALU.is_ge))
            st.wait()
            st.link(v.tensor_tensor(cross[:, 0, :, :], cross[:, 0, :, :], cross[:, 1, :, :], ALU.mult))
            for h in range(2):
                st(v.tensor_scalar(rng_f[:, 0, h, :], cross[:, 0, h, :], -1000.0, 1000.0, ALU.mult, ALU.add))
                st(v.tensor_scalar(rng_f[:, 1, h, :], cross[:, 0, h, :], 1.0, None, ALU.mult))
            st.wait()
            for h in range(2):
                last = v.tensor_scalar(rng_f[:, 0, h, :], rng_f[:, 0, h, :], tile_id[:, h:h + 1], None, ALU.add)
                st(last)
                st(v.tensor_scalar(rng_f[:, 1, h, :], rng_f[:, 1, h, :], tile_id[:, h:h + 1], None, ALU.mult))
            st.wait()
            v.tensor_tensor(rng_f[:, 1, :, :], rng_f[:, 1, :, :], cross[:, 0, :, :],
                            ALU.add).then_inc(rng_ready, 1)
            dve.wait_ge(edgeT_psum, 1)
            st(v.tensor_copy(edgeT[:], PS[:, 6, :].rearrange("p (s e) -> p s e", s=2)))
            dve.wait_ge(rngT_psum, 1)
            st(v.tensor_reduce(rng_c[:, 0:1], PS[0:NT, 7, 0:2 * P], AX_X, ALU.min))
            st(v.tensor_reduce(rng_c[:, 1:2], PS[0:NT, 7, 2 * P:4 * P], AX_X, ALU.max))
            st.wait()
            v.tensor_scalar(rng_c[:, 0:1], rng_c[:, 0:1], float(ET - 1), None, ALU.min).then_inc(rng_col, 1)
            dve.wait_ge(rng_row_psum, 1)
            v.tensor_copy(rng_i[:], PS[0:1, 7, 0:2 * NT]).then_inc(rng_row, 1)
            dve.wait_ge(rng_row, 1)

            made = dve.alloc_register("oh_made")
            dve.reg_mov(made, 1)

            def one_hots(b):
                lo = dve.value_load(rng_i[0:1, bass.ds(b, 1)], min_val=0, max_val=ET - 1)
                hi = dve.value_load(rng_i[0:1, bass.ds(b + NT, 1)], min_val=0, max_val=ET)
                with dve.Fori(lo, hi, OH) as t:
                    now = dve.snap(made, min_val=1, max_val=2000)
                    for j in range(OH):
                        if j % 2 == 0:
                            dve.wait_ge(oh_free, now + j // 2)
                        v.tensor_scalar(oh_dst[:, j, :], iota_n[:, bass.ds(b * P, P)],
                                        edgeT[:, 0, bass.ds(t + j, 1)], None, ALU.is_equal)
                        last = v.tensor_scalar(oh_src[:, j, :], iota_n[:],
                                               edgeT[:, 1, bass.ds(t + j, 1)], None, ALU.is_equal)
                        if j % 2:
                            last.then_inc(oh_ready, 1)
                    dve.reg_add(made, made, OH // 2)

            def tile_stats(t):
                for g in range(2):
                    st(v.bn_stats(st_one[:, g, :], X[:, bass.ds(t, 1), g * HD:(g + 1) * HD].squeeze(1)))

            def tile_norm(t):
                st.link(v.bn_aggr(mv_one[:], st_one[:]))
                st.link(v.tensor_scalar(neg_mean[:, bass.ds(t, 1)], mv_one[:, 0:1], -1.0, None, ALU.mult))
                v.tensor_scalar(var_e[:, bass.ds(t, 1)], mv_one[:, 1:2], EPS, X_SCALE ** -2, ALU.add,
                                ALU.mult).then_inc(stats_ready, 1)

            def h_dot(t, s):
                st(v.scalar_tensor_tensor(out=junk, in0=hbuf[:, bass.ds(t, 1), :].squeeze(1),
                                          scalar=1.0, in1=a_row[:, s, :], op0=ALU.mult, op1=ALU.mult,
                                          accum_out=AL[:, s, bass.ds(t, 1)]))

            def first_item(b):
                one_hots(b)
                if b == 1:
                    dve.wait_ge(x_in, 32)
                tile_stats(b + 1)
                st.wait()
                tile_norm(b + 1)

            def item(b):
                one_hots(b)
                tile_stats(b + 1)
                st.wait()
                dve.wait_ge(h_ready, b - 1)
                h_dot(b - 2, 0)
                tile_norm(b + 1)
                h_dot(b - 2, 1)

            dve.wait_ge(x_first_in, 16)
            tile_stats(0)
            st.wait()
            tile_norm(0)
            first_item(0)
            dve.wait_ge(w_hi_ready, 1)
            v.scalar_tensor_tensor(out=W_lo[:, KD // 2:KD, :], in0=W_raw[:, KD // 2:KD, :], scalar=W_SCALE,
                                   in1=W_hi[:, KD // 2:KD, :], op0=ALU.mult, op1=ALU.subtract).then_inc(w_lo_ready, 1)
            first_item(1)
            dve.wait_ge(a_in, 16)
            with dve.Fori(2, NT - 1) as b:
                st.enter(b - 2, 6)
                item(b)
                st.leave(NT - 3)
            one_hots(NT - 1)
            for b in range(NT - 3, NT):
                dve.wait_ge(h_ready, b + 1)
                for s in range(2):
                    st.wait()
                    h_dot(b, s)

            def row_of(column):
                n = column.shape[1]
                st.wait()
                v.tensor_tensor(diag[:, 0:n * P].rearrange("p (t n) -> p t n", n=P),
                                ident[:].unsqueeze(1).broadcast_to([P, n, P]),
                                column.unsqueeze(2).broadcast_to([P, n, P]), ALU.mult).then_inc(diag_ready, 1)

            def columns_of(i):
                return bass.ds(i * P, P)

            def weights(i, j):
                cols = columns_of(i + j)
                dve.wait_ge(at_ready, i + (j + CREDIT))
                v.tensor_tensor(S, alb[:, cols].unsqueeze(1).broadcast_to([P, NT, P]),
                                AL[:, 1, :].unsqueeze(2).broadcast_to([P, NT, P]), ALU.add).then_inc(sum_ready, 1)
                dve.wait_ge(sum_ready, i * 2 + (2 * j + 1))
                v.scalar_tensor_tensor(out=S, in0=S, scalar=0.1, in1=S, op0=ALU.mult,
                                       op1=ALU.max).then_inc(sum_ready, 1)
                dve.wait_ge(act_out, done(i + j))
                dve.wait_ge(agg_psum, freed(i + j))
                v.tensor_tensor(AT[:, j, :, :], S, CT[:, :, cols], ALU.mult).then_inc(at_ready, 1)
                dve.wait_ge(at_ready, done(i + j))
                v.tensor_reduce(at_sum[:, j, :], AT[:, j, :, :].rearrange("p t n -> p n t"), AX_X,
                                ALU.add).then_inc(at_summed, 1)

            def aggregate(i, j):
                dve.wait_ge(agg_psum, done(i + j))
                acc = PS[:, 3 * j:3 * j + 2, :].rearrange("p a n -> p (a n)")
                st.link(v.tensor_scalar(rs[:, 0:1], PS[:, 3 * j + 2, 0:1], EPS, None, ALU.add))
                st.link(v.reciprocal(rs[:, 1:2], rs[:, 0:1]))
                v.tensor_scalar(tmp_m, acc, rs[:, 1:2], 0.0, ALU.mult, ALU.min).then_inc(m_ready, 1)
                st(v.tensor_scalar(tmp_p, acc, rs[:, 1:2], 0.0, ALU.mult, ALU.max))
                dve.wait_ge(e_ready, i + (j + 1))
                st.wait()
                st.link(v.scalar_tensor_tensor(out=tmp_p, in0=tmp_m, scalar=-1.0, in1=tmp_p,
                                               op0=ALU.add, op1=ALU.add))
                xt = X[:, bass.ds(i + j, 1), :].squeeze(1)
                v.tensor_tensor(xt, xt, tmp_p, ALU.add).then_inc(x_updated, 1)
                dve.wait_ge(x_updated, done(i + j))
                row_stats(i + j)

            def extremes(i, j):
                for ends, op in ((x_max, ALU.max), (x_min, ALU.min)):
                    st(v.tensor_reduce(ends[:, bass.ds(i + j, 1)], X[:, bass.ds(i + j, 1), :].squeeze(1), AX_X, op))

            def ffn_scales(i, j):
                dve.wait_ge((wraw_in0, wraw_in1)[j], i * 8 + 16)
                if isinstance(i, int) and i >= 2 * FC:
                    w = slice(2 * (i + j - FC), 2 * (i + j - FC) + 2)
                    rows = w_raw[:, j, 0:2 * FF].rearrange("p (r f) -> p r f", r=2)
                else:
                    w = bass.ds(i + j, 1)
                    rows = w_raw[:, j, :]
                st.link(v.tensor_reduce(w_max[:, w], rows, AX_X, ALU.max, apply_absolute_value=True))
                st.link(v.tensor_scalar(w_max[:, w], w_max[:, w], 1.0 / QMAX, 1e-35, ALU.mult, ALU.max))
                v.reciprocal(w_inv[:, w], w_max[:, w]).then_inc(w_scaled, 1)

            def attention_item(i, j):
                ffn_scales(i, j)
                aggregate(i, j)
                extremes(i, j)

            row_of(AL[:, 0, :])
            dve.wait_ge(row_stored, 1)
            weights(0, 0)
            with pairs(dve, 2 * FC) as i:
                st.enter(i, 10, 2)
                weights(i, 1)
                attention_item(i, 0)
                weights(i + 2, 0)
                attention_item(i, 1)
                st.leave(2 * FC)
            for i in range(2 * FC, NT, 2):
                weights(i, 1)
                attention_item(i, 0)
                if i + 2 < NT:
                    weights(i + 2, 0)
                attention_item(i, 1)
            variances()
            means(1)

            def act_scale(n):
                dve.wait_ge(max_all, n + 1)
                st.link(v.tensor_scalar(s_act[:, 2 * n:2 * n + 1], top[:, 2 * n + 1:2 * n + 2], sig[:, n:n + 1],
                                        1.0 / QMAX, ALU.mult, ALU.mult))
                st.link(v.reciprocal(s_act[:, 2 * n + 1:2 * n + 2], s_act[:, 2 * n:2 * n + 1]))

            dve.wait_ge(sig_ready, 1)
            st.link(v.tensor_scalar(sig[:], sig[:], 0.5, 0.5, ALU.mult, ALU.add))
            for ends in (x_max, x_min):
                st.link(v.tensor_tensor(ends[:], ends[:], RSTD[:], ALU.mult))
                st.link(v.tensor_tensor(ends[:], ends[:], NMR[:], ALU.add))
            st.link(v.tensor_scalar(x_min[:], x_min[:], -1.0, None, ALU.mult))
            st.link(v.tensor_tensor(x_max[:], x_max[:], x_min[:], ALU.max))
            v.tensor_reduce(top[:, 0:1], x_max[:], AX_X, ALU.max).then_inc(max_ready, 1)
            act_scale(0)
            st(v.tensor_scalar(qscale[:], RSTD[:], s_act[:, 1:2], None, ALU.mult))
            v.tensor_scalar(qbias[:], NMR[:], s_act[:, 1:2], None, ALU.mult).then_inc(qs_ready, 1)
            st(v.tensor_scalar(s_half[:], w_max[:, 0:2 * FC:2], s_act[:, 0:1], 0.5, ALU.mult, ALU.mult))
            st(v.tensor_scalar(s_gu[:], w_max[:, 1:2 * FC:2], s_act[:, 0:1], None, ALU.mult))
            st.wait()
            v.tensor_tensor(s_gu[:], s_gu[:], s_half[:], ALU.mult).then_inc(qs_ready, 1)
            dve.wait_ge(qs_ready, 2)

            def round_x(t, j):
                dve.wait_ge(y_ready, done(t + j))
                dve.wait_ge(yT_psum, freed(t + j))
                y = xn_stage[:, j, :]
                st.link(v.tensor_scalar(y, y, QMAX, -QMAX - 1, ALU.min, ALU.max))
                v.tensor_scalar(xq_stage[:, j, :], y, MAGIC, -MAGIC, ALU.add, ALU.add).then_inc(yq_ready, 1)

            with pairs(dve, NT) as t:
                st.enter(t, 1, 2)
                round_x(t, 0)
                round_x(t, 1)
                st.leave(NT)

            def gate_up(g, i, c):
                n = i * FC + c
                j = n % 2
                dve.wait_ge(tanh_ready, done(g * FC + n))
                st.link(v.scalar_tensor_tensor(out=gu_tmp[:, j, :], in0=gu_tmp[:, j, :], scalar=1.0,
                                               in1=PS[:, 2 * j, 0:GN], op0=ALU.add, op1=ALU.mult))
                v.scalar_tensor_tensor(out=hT[:, c, bass.ds((g + i) * GN, GN)], in0=gu_tmp[:, j, :],
                                       scalar=s_gu[:, c:c + 1], in1=PS[:, 2 * j + 1, 0:GN],
                                       op0=ALU.mult, op1=ALU.mult).then_inc(hT_ready, 1)

            with pairs(dve, NG) as g:
                st.enter(g, FC, 2)
                for i in range(2):
                    for c in range(FC):
                        gate_up(g, i, c)
                st.leave(NG)
            dve.wait_ge(hT_ready, FC * NG + CREDIT)
            v.tensor_reduce(top[:, 2:3], hT, AX_XY, ALU.max, apply_absolute_value=True).then_inc(max_ready, 1)
            act_scale(1)
            st(v.tensor_scalar(s_down[:], w_max[:, 2 * FC:2 * FC + KD], s_act[:, 2:3], None, ALU.mult))
            st.link(v.tensor_scalar(hT, hT, s_act[:, 3:4], QMAX, ALU.mult, ALU.min))
            row_of(s_down[:])
            st.link(v.tensor_scalar(hT, hT, -QMAX - 1, MAGIC, ALU.max, ALU.add))
            v.tensor_scalar(hq, hT, -MAGIC, None, ALU.add).then_inc(hq_ready, 1)

            def down(t, j):
                dve.wait_ge(d_psum, done(t + j))
                dve.wait_ge(d_added, freed(t + j))
                v.tensor_tensor(w_raw[:, j, :], PS[:, 2 * j:2 * j + 2, :].rearrange("p a n -> p (a n)"), tmp_m,
                                ALU.mult).then_inc(d_scaled, 1)

            def down_stats(t, j):
                dve.wait_ge(d_added, done(t + j))
                row_stats(t + j)

            v.tensor_scalar(dis[:], deg[:], 1.0, None, ALU.max).then_inc(dis_deg, 1)
            dve.wait_ge(row_stored, 2)
            down(0, 0)
            with pairs(dve, NT - 2) as t:
                st.enter(t, 2, 2)
                down(t, 1)
                down_stats(t, 0)
                down(t + 2, 0)
                down_stats(t, 1)
                st.leave(NT - 2)
            down(NT - 2, 1)
            down_stats(NT - 2, 0)
            down_stats(NT - 2, 1)
            variances(X_SCALE)
            means(2)

            def dots(rows, k, t, j):
                c = bass.ds(t + j, 1)
                st(v.scalar_tensor_tensor(out=dot_out, in0=rows, scalar=1.0, in1=wg_row[:, 0, :], op0=ALU.mult,
                                          op1=ALU.mult, accum_out=U[:, c]))
                st.wait()
                v.scalar_tensor_tensor(out=dot_out, in0=rows, scalar=1.0, in1=wg_row[:, 1, :], op0=ALU.mult,
                                       op1=ALU.mult, accum_out=V[:, k % 2, c]).then_inc(uv_ready, 1)
                dve.wait_ge(u_psum, freed(t + (j + k * NT)))
                v.tensor_scalar(u_diag[:, j, :], ident[:], U[:, c], None, ALU.mult).then_inc(diag2_ready, 1)

            def lo_part(t, j):
                dve.wait_ge(hi2_ready, done(t + j))
                v.tensor_tensor(parts2[:, j % 2, 1, :], ln2, parts2[:, j % 2, 0, :],
                                ALU.subtract).then_inc(lo2_ready, 1)

            def x1_out(t, j):
                dve.wait_ge(x1_psum, done(t + j))
                rows = G[:, bass.ds(t + j, 1), :].squeeze(1)
                v.scalar_tensor_tensor(out=rows, in0=PS[:, j, :], scalar=1.0 / (X_SCALE * W_SCALE), in1=b1_row,
                                       op0=ALU.mult, op1=ALU.add).then_inc(x1_ready, 1)
                dve.wait_ge(x1_ready, done(t + j))
                dots(rows, 0, t, j)

            dve.wait_ge(b1_in, 32)
            dve.wait_ge(wg_in, 16)
            dve.wait_ge(dis_ready, 1)
            st(v.tensor_scalar(dis_in[:], dis[:], G_SCALE, None, ALU.mult))
            v.tensor_scalar(dis_out[:], dis[:], 1.0 / G_SCALE, None, ALU.mult).then_inc(dis_scaled, 1)
            lo_part(0, 0)
            lo_part(0, 1)
            with pairs(dve, NT - 2) as t:
                st.enter(t, 1, 2)
                for j in range(2):
                    lo_part(t, j + 2)
                    x1_out(t, j)
                st.leave(NT - 2)
            def edge_weights(k, c, j):
                dve.wait_ge(tanh2_ready, c + (k * NT + j + 1))
                s = SS[:, j % 2, :, :]
                v.scalar_tensor_tensor(out=s, in0=s, scalar=A_SCALE, in1=C[:, :, columns_of(c + j)], op0=ALU.mult,
                                       op1=ALU.mult).then_inc(aw_ready, 1)

            def weights_low(k, c, j):
                dve.wait_ge(aw_hi_ready, done(c + (k * NT + j)))
                v.scalar_tensor_tensor(out=AP[:, j % 2, 1, :, :], in0=AP[:, j % 2, 0, :, :], scalar=-A_SCALE,
                                       in1=SS[:, j % 2, :, :], op0=ALU.mult, op1=ALU.add).then_inc(aw_lo_ready, 1)

            def gather_edges(k, c, j):
                dve.wait_ge(agg2_psum, done(c + (k * NT + j)))
                rows = G[:, bass.ds(c + j, 1), :].squeeze(1)
                st.link(v.tensor_scalar(agg_row, PS[:, 5 + j, :], 1.0 / A_SCALE, None, ALU.mult))
                st.link(v.tensor_tensor(agg_row, agg_row, PS[:, 3 + j, :], ALU.add))
                v.scalar_tensor_tensor(out=rows, in0=agg_row, scalar=dis_out[:, bass.ds(c + j, 1)], in1=rows,
                                       op0=ALU.mult, op1=ALU.add).then_inc(g_ready, 1)
                dve.wait_ge(g_ready, done(c + (k * NT + j)))
                if k + 1 < K1:
                    dots(rows, k + 1, c, j)
                else:
                    xr = X[:, bass.ds(c + j, 1), HD:D].squeeze(1)
                    v.tensor_tensor(xr, xr, rows, ALU.add).then_inc(x_final, 1)
                    dve.wait_ge(x_final, c + (j + 1))
                    row_stats(c + j)

            def early_weights(k):
                for j in range(2):
                    dve.wait_ge(early_tanh, 2 * k + j + 1)
                    s = SS[:, j, 0:FT, :]
                    v.scalar_tensor_tensor(out=s, in0=s, scalar=A_SCALE, in1=C[:, 0:FT, j * P:(j + 1) * P],
                                           op0=ALU.mult, op1=ALU.mult).then_inc(early_aw, 1)

            def early_low(k):
                dve.wait_ge(early_hi, k + 1)
                v.scalar_tensor_tensor(out=AP[:, 0, 1, 0:FT, :], in0=AP[:, 0, 0, 0:FT, :], scalar=-A_SCALE,
                                       in1=SS[:, 0, 0:FT, :], op0=ALU.mult, op1=ALU.add).then_inc(early_lo, 1)

            def late_weights(k):
                for j in range(2):
                    dve.wait_ge(tanh2_ready, k * NT + j + 1)
                    s = SS[:, j, FT:NT, :]
                    v.scalar_tensor_tensor(out=s, in0=s, scalar=A_SCALE, in1=C[:, FT:NT, j * P:(j + 1) * P],
                                           op0=ALU.mult, op1=ALU.mult).then_inc(aw_ready, 1)
                    if j == 0:
                        dve.wait_ge(aw_hi_ready, done(k * NT))
                        v.scalar_tensor_tensor(out=AP[:, 0, 1, FT:NT, :], in0=AP[:, 0, 0, FT:NT, :], scalar=-A_SCALE,
                                               in1=SS[:, 0, FT:NT, :], op0=ALU.mult,
                                               op1=ALU.add).then_inc(aw_lo_ready, 1)

            x1_out(NT - 2, 0)
            early_weights(0)
            x1_out(NT - 2, 1)
            early_low(0)
            late_weights(0)
            dve.wait_ge(xl_added, NT)
            for k in range(K1):
                per = 3 if k + 1 < K1 else 4
                if k + 1 < K1:
                    dve.wait_ge(wg_in, 16 * (k + 2))
                with pairs(dve, NT - 2) as c:
                    st.enter(c, per, 2)
                    for j in range(2):
                        weights_low(k, c, j + 1)
                        edge_weights(k, c, j + 2)
                        gather_edges(k, c, j)
                    st.leave(NT - 2)
                weights_low(k, NT - 2, 1)
                if k + 1 < K1:
                    early_weights(k + 1)
                gather_edges(k, NT - 2, 0)
                if k + 1 < K1:
                    early_low(k + 1)
                gather_edges(k, NT - 2, 1)
                if k + 1 < K1:
                    late_weights(k + 1)
            variances()
            means(3)
            dve.wait_ge(nmr_ready, 3)

            dve.wait_ge(gws_ready, 1)
            v.tensor_tensor(lg_mean[:], NMR[:].unsqueeze(2).broadcast_to([P, NT, NE]),
                            gw_sum[:].unsqueeze(1).broadcast_to([P, NT, NE]), ALU.mult).then_inc(nmr_ready, 1)
            dve.wait_ge(lg_ready, NT + CREDIT)
            st.link(v.tensor_tensor(LG[:], LG[:], RSTD[:].unsqueeze(2).broadcast_to([P, NT, NE]), ALU.mult))
            dve.wait_ge(nmr_ready, 4)
            st.link(v.tensor_tensor(LG[:], LG[:], lg_mean[:], ALU.add))

            diff, mask, rank, keep, was = (route(i) for i in range(5))
            of_experts = [P, NT, NE]
            st.link(v.tensor_reduce(lg_top[:], LG[:], AX_X, ALU.max))
            top_b = lg_top[:].unsqueeze(2).broadcast_to(of_experts)
            ids = exp_id[:].unsqueeze(1).broadcast_to(of_experts)
            v.tensor_tensor(diff, LG[:], top_b, ALU.subtract).then_inc(soft_in, 1)
            st.link(v.tensor_tensor(mask, LG[:], top_b, ALU.is_equal))
            st.link(v.tensor_scalar(mask, mask, -100.0, None, ALU.mult))
            st.link(v.tensor_tensor(mask, mask, ids, ALU.add))
            st.link(v.tensor_reduce(first[:], mask, AX_X, ALU.min))
            st.link(v.tensor_tensor(mask, mask, first[:].unsqueeze(2).broadcast_to(of_experts), ALU.is_equal))
            v.tensor_tensor(mask, mask, valid[:].unsqueeze(2).broadcast_to(of_experts),
                            ALU.mult).then_inc(mask_ready, 1)
            dve.wait_ge(soft_out, 1)
            st.link(v.tensor_reduce(wt[:], diff, AX_X, ALU.add))
            st.link(v.reciprocal(wt[:], wt[:]))
            dve.wait_ge(rank_psum, 1)
            st(v.tensor_copy(keep, PS[:, 4, 0:NT * NE].rearrange("p (t e) -> p t e", t=NT)))
            st(v.memset(was[:, 0, :], 0.0))
            st.wait()
            for t in range(NT - 1):
                st.link(v.tensor_tensor(was[:, t + 1, :], was[:, t, :], keep[:, t, :], ALU.add))
            st.link(v.tensor_tensor(rank, PS[:, 3, 0:NT * NE].rearrange("p (t e) -> p t e", t=NT), was, ALU.add))
            st(v.tensor_scalar(keep, rank, float(CAP), None, ALU.is_lt))
            st.link(v.tensor_tensor(rank, rank, mask, ALU.mult))
            st(v.tensor_reduce(rank1[:], rank, AX_X, ALU.add))
            st.link(v.tensor_tensor(keep, keep, mask, ALU.mult))
            st(v.tensor_tensor(slot_of, iota_n[:, 0:CAP].unsqueeze(1).broadcast_to([P, NT, CAP]),
                               rank1[:].unsqueeze(2).broadcast_to([P, NT, CAP]), ALU.is_equal))
            st(v.tensor_copy(facts[:, :, 0, :], keep))
            for i, what in enumerate((node_id, wt, RSTD, NMR)):
                last = v.tensor_tensor(facts[:, :, i + 1, :], keep, what[:].unsqueeze(2).broadcast_to(of_experts),
                                       ALU.mult)
                if i < 3:
                    st(last)
            last.then_inc(cast_ready, 1)
            dve.wait_ge(slots_psum, 1)
            st.link(v.tensor_copy(slots[0:CAP].rearrange("p q e -> p (q e)"), PS[0:CAP, 5, 0:NR]))
            st(v.tensor_copy(take[0:CAP, :], slots[0:CAP, 1, :]))
            st.link(v.tensor_scalar(away[0:CAP, :], slots[0:CAP, 0, :], -65536.0, 65536.0, ALU.mult, ALU.add))
            st.link(v.tensor_tensor(away[0:CAP, :], away[0:CAP, :], slots[0:CAP, 1, :], ALU.add))
            v.tensor_copy(give[0:CAP, :], away[0:CAP, :]).then_inc(slots_ready, 1)

            def xgT_out(e, j):
                dve.wait_ge(xgT_psum, done(e + j))
                dve.wait_ge(m1_psum, freed(e + j))
                v.tensor_copy(xgT[:, j % 2, :, :].rearrange("p (a k) c -> p a (k c)", a=2),
                              PS[:, 0:2, 0:4 * CAP]).then_inc(xgT_ready, 1)

            def geT_out(e, j):
                dve.wait_ge(geT_psum, done(e + j))
                dve.wait_ge(m2_psum, freed(e + j))
                v.tensor_copy(geT[:, j % 2, :, :].rearrange("p k c -> p (k c)"), PS[:, 4, 0:4 * CAP]
                              ).then_inc(geT_ready, 1)

            def rows_made(e, j):
                dve.wait_ge(m2_psum, done(e + j))
                if not (isinstance(e, int) and e + j < 2):
                    dve.wait_ge((sent0, sent1)[j % 2], (e + j) // 2 * 16)
                v.scalar_tensor_tensor(out=o_stage[:, j % 2, :],
                                       in0=PS[0:CAP, 5:7, :].rearrange("p a n -> p (a n)"),
                                       scalar=slots[0:CAP, 2, bass.ds(e + j, 1)],
                                       in1=xg[:, bass.ds((e + j) % 4, 1), :].squeeze(1),
                                       op0=ALU.mult, op1=ALU.add).then_inc(o_ready, 1)

            xgT_out(0, 0)
            xgT_out(0, 1)
            geT_out(0, 0)
            for j in (1, 2):
                xgT_out(0, j + 1)
                rows_made(0, j - 1)
                geT_out(0, j)
            with dve.Fori(2, NE - 3, 2) as e:
                for j in (1, 2):
                    xgT_out(e, j + 1)
                    rows_made(e, j - 1)
                    geT_out(e, j)
            rows_made(NE - 2, 0)
            geT_out(NE - 2, 1)
            rows_made(NE - 2, 1)

        @block.scalar
        def _(act):
            a = nc.scalar
            act.wait_ge(consts, CONSTS)

            def ln_out(t):
                c = bass.ds(t, 1)
                act.wait_ge(norm_ready, t + 1)
                wait_from(act, lo_ready, t)
                ln_steps(a.activation(ln_x, X[:, c, :].squeeze(1), ACT.Identity,
                                      scale=RSTD[:, c], bias=NMR[:, c]))
                ln_steps.wait()
                wait_from(act, parts_psum, t)
                a.copy(x_parts[:, 0, :], ln_x).then_inc(hi_ready, 1)

            def ct_out(t):
                act.wait_ge(ct_psum, t + 1)
                wait_from(act, ct_stored, t)
                a.activation(ct_stage, PS[:, 0:3, :].rearrange("p a n -> p (a n)")[:, 0:NP],
                             ACT.Identity, accum_out=deg[:, bass.ds(t, 1)]).then_inc(ct_staged, 1)

            def h_out(t):
                act.wait_ge(h_psum, t + 1)
                a.activation(hbuf[:, bass.ds(t, 1), :].squeeze(1), PS[:, 4:6, :].rearrange("p a n -> p (a n)"),
                             ACT.Copy, scale=1.0 / (X_SCALE * W_SCALE)).then_inc(h_ready, 1)

            def c_out(t):
                for g in range(CG):
                    n = min(4, NT - 4 * g)
                    act.wait_ge(c_psum, t * CG + (g + 1))
                    a.copy(C[:, 4 * g:4 * g + n, bass.ds(t * P, P)],
                           PS[:, g, 0:n * P].rearrange("p (t n) -> p t n", n=P)).then_inc(c_stored, 1)

            def xT_out(t):
                act.wait_ge(parts_psum, t + 1)
                wait_from(act, h_psum, t)
                a.copy(xT_parts.rearrange("p s k n -> p s (k n)"),
                       PS[:, 6:8, :].bitcast(F16)).then_inc(partsT_ready, 1)

            ln_steps = Steps(act, act_s)
            act.wait_ge(w_in, 16)
            h = slice(KD // 2, KD)
            a.activation(W_hi[:, h, :], W_raw[:, h, :], ACT.Copy, scale=W_SCALE).then_inc(w_hi_ready, 1)
            h = slice(0, KD // 2)
            ln_steps(a.mul(W_raw[:, h, :], W_raw[:, h, :], W_SCALE))
            ln_steps.wait()
            a.copy(W_hi[:, h, :], W_raw[:, h, :]).then_inc(w_hi_ready, 1)
            ln_out(0)
            ct_out(0)
            c_out(0)
            xT_out(0)
            act.wait_ge(w_lo_ready, 2)
            with act.Fori(1, NT) as t:
                ln_steps.enter(t - 1, 1)
                ln_out(t)
                ct_out(t)
                h_out(t - 1)
                c_out(t)
                xT_out(t)
                ln_steps.leave(NT - 1)
            act.wait_ge(ct_stored, NT)
            h_out(NT - 1)

            def row_out(n, w):
                act.wait_ge(row_psum, n)
                a.copy((alb if n != 2 else tmp_m)[:, 0:w],
                       PS[:, 0:-(-w // 512), :].rearrange("p a n -> p (a n)")[:, 0:w]).then_inc(row_stored, 1)

            def exp_weights(i, j):
                act.wait_ge(sum_ready, i * 2 + (2 * j + 2))
                a.activation(S, S, ACT.Exp, scale=-1.0).then_inc(act_out, 1)

            def exp_elu(i, j):
                act.wait_ge(m_ready, i + (j + 1))
                a.activation(tmp_m, tmp_m, ACT.Exp).then_inc(e_ready, 1)

            row_out(1, NP)
            act.wait_ge(clips_in, 32)
            a.activation(sig[:], clips[:], ACT.Tanh, scale=0.5).then_inc(sig_ready, 1)
            def ffn_weights_out(i, j):
                act.wait_ge(wT_psum, done(i + j))
                bank = PS[:, 6 + j, :].bitcast(BF16).rearrange("p (k n) -> p k n", n=P)
                if isinstance(i, int) and i >= 2 * FC:
                    r = 2 * (i + j - 2 * FC)
                    for q in range(2):
                        cols = slice((r + q) * P, (r + q + 1) * P)
                        a.copy(wdT[:, 0:FC - 1, cols], bank[:, q * FC:(q + 1) * FC - 1, :])
                        last = a.copy(wdT[0:FF % P, FC - 1, cols], bank[0:FF % P, (q + 1) * FC - 1, :])
                    last.then_inc(wT_stored, 1)
                else:
                    a.copy(wguT[:, :, j, bass.ds(i * (P // 2), P)], bank).then_inc(wT_stored, 1)

            exp_weights(0, 0)
            with pairs(act, 2 * FC) as i:
                exp_weights(i, 1)
                exp_elu(i, 0)
                exp_weights(i + 2, 0)
                exp_elu(i, 1)
                ffn_weights_out(i, 0)
                ffn_weights_out(i, 1)
            for i in range(2 * FC, NT, 2):
                exp_weights(i, 1)
                exp_elu(i, 0)
                if i + 2 < NT:
                    exp_weights(i + 2, 0)
                exp_elu(i, 1)
                ffn_weights_out(i, 0)
                ffn_weights_out(i, 1)

            def y_out(t, j):
                act.wait_ge(yq_ready, freed(t + j))
                a.activation(xn_stage[:, j, :], X[:, bass.ds(t + j, 1), :].squeeze(1), ACT.Identity,
                             scale=qscale[:, bass.ds(t + j, 1)], bias=qbias[:, bass.ds(t + j, 1)]).then_inc(y_ready, 1)

            def yT_out(t, j):
                act.wait_ge(yT_psum, done(t + j))
                a.copy(xqT[:, :, bass.ds((t + j) * P, P)],
                       PS[:, 4 + j, :].bitcast(BF16).rearrange("p (k n) -> p k n", n=P)).then_inc(yT_stored, 1)

            act.wait_ge(w1_in, 16)
            a.mul(W1_raw, W1_raw, W_SCALE).then_inc(w1_scaled, 1)
            act.wait_ge(qs_ready, 1)
            y_out(0, 0)
            with pairs(act, NT - 2) as t:
                y_out(t, 1)
                yT_out(t, 0)
                y_out(t + 2, 0)
                yT_out(t, 1)
            y_out(NT - 2, 1)
            yT_out(NT - 2, 0)
            yT_out(NT - 2, 1)

            act.wait_ge(yT_psum, NT + CREDIT)
            act.wait_ge(w1_scaled, 1)
            a.copy(W1_hi, W1_raw).then_inc(w1_hi_ready, 1)

            act.wait_ge(qs_ready, 2)
            with pairs(act, NG) as g:
                for n in range(2 * FC):
                    j = n % 2
                    act.wait_ge(gu_psum, done(g * FC + n))
                    a.activation(gu_tmp[:, j, :], PS[:, 2 * j, 0:GN], ACT.Tanh,
                                 scale=s_half[:, n % FC:n % FC + 1]).then_inc(tanh_ready, 1)
            row_out(2, D)

            def ln_out2(t, j):
                c = bass.ds(t + j, 1)
                act.wait_ge(lo2_ready, t + (j + CREDIT))
                steps(a.activation(ln2, X[:, c, :].squeeze(1), ACT.Identity, scale=RSTD[:, c], bias=NMR[:, c]))
                steps.wait()
                act.wait_ge(parts2_psum, freed(t + j))
                a.copy(parts2[:, j % 2, 0, :], ln2).then_inc(hi2_ready, 1)

            def xT_out2(t, j):
                act.wait_ge(parts2_psum, done(t + j))
                act.wait_ge(x1_psum, freed(t + j))
                b = j % 2
                a.copy(partsT2[:, b].rearrange("p s k n -> p s (k n)"),
                       PS[:, 4 + 2 * b:6 + 2 * b, :].bitcast(F16)).then_inc(parts2T_ready, 1)

            def scaled_rows(t, j, n):
                rows = G[:, bass.ds(t + j, 1), :].squeeze(1)
                by = dis_in[:, bass.ds(t + j, 1)]
                if n == 0:
                    act.wait_ge(x1_ready, done(t + j))
                else:
                    act.wait_ge(g_ready, done(t + (j + (n - 1) * NT)))
                act.wait_ge(gs_ready, t + (j + n * NT + CREDIT))
                steps(a.mul(gs_raw, rows, by))
                steps.wait()
                a.copy(GS[:, (n + 1) % 2, 0, bass.ds(t + j, 1), :].squeeze(1), gs_raw).then_inc(gs_made, 1)

            steps = ln_steps
            act.wait_ge(nmr_ready, 2)
            act.wait_ge(dis_scaled, 1)
            act.wait_ge(w1_lo_ready, 1)
            def u_out(k, t, j):
                act.wait_ge(u_psum, done(t + (j + k * NT)))
                a.activation(u_row[:, k % 2, bass.ds((t + j) * P, P)], PS[:, 2, 0:P],
                             ACT.Identity, bias=bg_row[:, k:k + 1]).then_inc(u_stored, 1)

            def tanh_weights(k, c, j):
                act.wait_ge(aw_lo_ready, freed(c + (k * NT + j)))
                act.wait_ge(u_stored, done(c + (k * NT + j)))
                for t in range(NT):
                    last = a.activation(SS[:, j % 2, t, :], u_row[:, k % 2, bass.ds((c + j) * P, P)], ACT.Tanh,
                                        bias=V[:, k % 2, t:t + 1])
                last.then_inc(tanh2_ready, 1)

            def weights_high(k, c, j):
                act.wait_ge(aw_ready, done(c + (k * NT + j)))
                act.wait_ge(agg2_psum, freed(c + (k * NT + j)))
                a.activation(AP[:, j % 2, 0, :, :], SS[:, j % 2, :, :], ACT.Copy,
                             scale=1.0 / A_SCALE).then_inc(aw_hi_ready, 1)

            def first_tanhs(k, j, tiles, sem):
                for t in tiles:
                    last = a.activation(SS[:, j, t, :], u_row[:, k % 2, j * P:(j + 1) * P], ACT.Tanh,
                                        bias=V[:, k % 2, t:t + 1])
                last.then_inc(sem, 1)

            def next_round(k):
                act.wait_ge(uv_ready, k * NT + FT)
                act.wait_ge(aw_lo_ready, k * NT + CREDIT)
                act.wait_ge(u_stored, k * NT + 2 + CREDIT)
                act.wait_ge(w1_lo_ready, 1)
                first_tanhs(k, 0, range(FT), early_tanh)
                first_tanhs(k, 1, range(FT), early_tanh)
                u_out(k, NT - 4, 1)
                if k == 0:
                    act.wait_ge(x1_psum, NT + CREDIT)
                else:
                    act.wait_ge(agg2_psum, k * NT - 1 + CREDIT)
                act.wait_ge(early_aw, 2 * k + 1)
                a.activation(AP[:, 0, 0, 0:FT, :], SS[:, 0, 0:FT, :], ACT.Copy,
                             scale=1.0 / A_SCALE).then_inc(early_hi, 1)
                scaled_rows(NT - 2, 0, k)
                u_out(k, NT - 2, 0)
                scaled_rows(NT - 2, 1, k)
                act.wait_ge(uv_ready, (k + 1) * NT)
                first_tanhs(k, 0, range(FT, NT), tanh2_ready)
                first_tanhs(k, 1, range(FT, NT), tanh2_ready)
                act.wait_ge(aw_ready, done(k * NT))
                a.activation(AP[:, 0, 0, FT:NT, :], SS[:, 0, FT:NT, :], ACT.Copy,
                             scale=1.0 / A_SCALE).then_inc(aw_hi_ready, 1)
                weights_high(k, 0, 1)
                tanh_weights(k, 0, 2)
                u_out(k, NT - 2, 1)

            def round_item(k, c, j):
                weights_high(k, c, j + 2)
                tanh_weights(k, c, j + 3)
                if k + 1 < K1:
                    scaled_rows(c, j, k + 1)

            ln_out2(0, 0)
            ln_out2(0, 1)
            xT_out2(0, 0)

            def x1_item(t, j):
                ln_out2(t, j + 2)
                xT_out2(t, j + 1)
                scaled_rows(t, j, 0)

            x1_item(0, 0)
            x1_item(0, 1)
            u_out(0, 0, 0)
            with act.Fori(2, NT - 3, 2) as t:
                steps.enter(t - 2, 2, 2)
                for j in range(2):
                    x1_item(t, j)
                    u_out(0, t, j - 1)
                steps.leave(NT - 4)
            xT_out2(NT - 2, 1)
            next_round(0)

            for k in range(K1 - 1):
                round_item(k, 0, 0)
                round_item(k, 0, 1)
                u_out(k + 1, 0, 0)
                with act.Fori(2, NT - 5, 2) as c:
                    steps.enter(c - 2, 1, 2)
                    for j in range(2):
                        round_item(k, c, j)
                        u_out(k + 1, c, j - 1)
                    steps.leave(NT - 6)
                round_item(k, NT - 4, 0)
                weights_high(k, NT - 4, 3)
                u_out(k + 1, NT - 4, -1)
                scaled_rows(NT - 4, 1, k + 1)
                u_out(k + 1, NT - 4, 0)
                next_round(k + 1)

            def x_copy_out(t, j):
                act.wait_ge(x_final, t + (j + 1))
                act.wait_ge(xT_psum, t + (j + CREDIT))
                a.copy(x_copy, X[:, bass.ds(t + j, 1), :].squeeze(1)).then_inc(xcopy_ready, 1)

            def xT_out(t, j):
                act.wait_ge(xT_psum, done(t + j))
                act.wait_ge(lg_psum, freed(t + j))
                a.copy(xT[:, j % 2, :, :].rearrange("p (a k) n -> p a (k n)", a=2), PS[:, 0:2, :]
                       ).then_inc(xT_ready, 1)

            def logits_out(t, j):
                act.wait_ge(lg_psum, done(t + j))
                a.copy(LG[:, bass.ds(t + j, 1), :].squeeze(1), PS[:, 7, 0:NE]).then_inc(lg_ready, 1)

            k = K1 - 1
            act.wait_ge(gwT_psum, 1)
            a.copy(gwT, PS[:, 7, 0:KD * NE].rearrange("p (k e) -> p k e", k=KD)).then_inc(gwT_ready, 1)
            round_item(k, 0, 0)
            x_copy_out(0, 0)
            round_item(k, 0, 1)
            act.wait_ge(gws_psum, 1)
            a.copy(gw_sum[:], PS[:, 7, 0:NE]).then_inc(gws_ready, 1)
            xT_out(0, 0)
            x_copy_out(0, 1)
            with act.Fori(2, NT - 5, 2) as c:
                for j in range(2):
                    round_item(k, c, j)
                    xT_out(c, j - 1)
                    logits_out(c, j - 2)
                    x_copy_out(c, j)
            c = NT - 4
            for j in range(4):
                if j == 0:
                    round_item(k, c, j)
                elif j == 1:
                    weights_high(k, c, j + 2)
                xT_out(c, j - 1)
                logits_out(c, j - 2)
                x_copy_out(c, j)
            logits_out(NT - 2, 0)
            xT_out(NT - 2, 1)
            logits_out(NT - 2, 1)
            act.wait_ge(soft_in, 1)
            a.activation(route(0), route(0), ACT.Exp).then_inc(soft_out, 1)

            def xgn_out(e, j):
                act.wait_ge(xgT_psum, freed(e + j))
                a.activation(xgn[:, j % 2, :], xg[:, bass.ds((e + j) % 4, 1), :].squeeze(1), ACT.Identity,
                             scale=slots[0:CAP, 3, bass.ds(e + j, 1)],
                             bias=slots[0:CAP, 4, bass.ds(e + j, 1)]).then_inc(xgn_ready, 1)

            def gelu_out(e, j):
                act.wait_ge(m1_psum, done(e + j))
                act.wait_ge(geT_psum, freed(e + j))
                a.activation(ge[:, j % 2, :], PS[0:CAP, 2 + j % 2, :], ACT.Gelu_apprx_tanh).then_inc(ge_ready, 1)

            got = (got0, got1, got2, got3)
            act.wait_ge(slots_ready, 1)
            act.wait_ge(got0, 16)
            xgn_out(0, 0)
            act.wait_ge(got1, 16)
            xgn_out(0, 1)
            with act.Fori(0, NE - 5, 4) as e:
                for j in range(4):
                    gelu_out(e, j)
                    act.wait_ge(got[(j + 2) % 4], (e + (j + 2)) // 4 * 16 + 16)
                    xgn_out(e, j + 2)
            for j in range(4):
                e = NE - 4
                gelu_out(e, j)
                if j < 2:
                    act.wait_ge(got[(j + 2) % 4], (e + j + 2) // 4 * 16 + 16)
                    xgn_out(e, j + 2)

        @block.tensor
        def _(pe):
            t_ = nc.tensor
            pe.wait_ge(consts, CONSTS)
            pe.wait_ge(edges_ready, 1)
            for s in range(2):
                for h in range(2):
                    last = t_.transpose(PS[:, 6, (2 * s + h) * P:(2 * s + h + 1) * P], edges_f[:, s, h, :], ident[:])
            last.then_inc(edgeT_psum, 1)
            pe.wait_ge(rng_ready, 1)
            for s in range(2):
                for h in range(2):
                    last = t_.transpose(PS[0:NT, 7, (2 * s + h) * P:(2 * s + h + 1) * P], rng_f[:, s, h, :], ident[:])
            last.then_inc(rngT_psum, 1)
            pe.wait_ge(rng_col, 1)
            for s in range(2):
                last = t_.matmul(PS[0:1, 7, s * NT:(s + 1) * NT], rng_c[:, s:s + 1], ident[0:NT, 0:NT],
                                 start=True, stop=True)
            last.then_inc(rng_row_psum, 1)
            pe.wait_ge(rng_row, 1)

            used = pe.alloc_register("oh_used")
            pe.reg_mov(used, 1)
            COLS = [(g, min(512, NP - 512 * g)) for g in range(-(-NP // 512))]

            def zero(n, first):
                for g, w in COLS:
                    last = t_.matmul(PS[:, g, 0:(w if first else n)], zerosb[:, 0:P],
                                     zerosb[:, 0:(w if first else n)], start=first, stop=not first,
                                     skip_group_check=True)
                return last

            def count(b):
                wait_from(pe, c_stored, b * CG)
                zero(512, True)
                lo = pe.value_load(rng_i[0:1, bass.ds(b, 1)], min_val=0, max_val=ET - 1)
                hi = pe.value_load(rng_i[0:1, bass.ds(b + NT, 1)], min_val=0, max_val=ET)
                with pe.Fori(lo, hi, OH) as t:
                    now = pe.snap(used, min_val=1, max_val=2000)
                    for i in range(OH):
                        if i % 2 == 0:
                            pe.wait_ge(oh_ready, now + i // 2)
                        for g, w in COLS:
                            last = t_.matmul(PS[:, g, 0:w], oh_dst[:, i, :], oh_src[:, i, 512 * g:512 * g + w],
                                             start=False, stop=False, skip_group_check=True)
                        if i % 2:
                            last.then_inc(oh_free, 1)
                    pe.reg_add(used, used, OH // 2)
                zero(2, False).then_inc(ct_psum, 1)

            def c_transposes(b):
                pe.wait_ge(ct_staged, b + 1)
                for g in range(CG):
                    for i in range(min(4, NT - 4 * g)):
                        last = t_.transpose(PS[:, g, i * P:(i + 1) * P],
                                            ct_stage[:, (4 * g + i) * P:(4 * g + i + 1) * P], ident[:])
                    last.then_inc(c_psum, 1)

            def part_transposes(t):
                pe.wait_ge(lo_ready, t + 1)
                wait_from(pe, partsT_ready, t)
                for s in range(2):
                    bank = PS[:, 6 + s, :].bitcast(F16)
                    for k in range(KD):
                        last = t_.transpose(bank[:, k * P:(k + 1) * P], x_parts[:, s, k * P:(k + 1) * P], identh[:])
                last.then_inc(parts_psum, 1)

            def h_products(t):
                pe.wait_ge(partsT_ready, t + 1)
                wait_from(pe, h_ready, t)
                for g in range(2):
                    cols = slice(g * HD, (g + 1) * HD)
                    for k in range(KD):
                        for xs, w in ((0, W_hi), (0, W_lo), (1, W_hi)):
                            last = t_.matmul(PS[:, 4 + g, :], xT_parts[:, xs, k, :], w[:, k, cols],
                                             start=(k == 0 and w is W_hi and xs == 0),
                                             stop=(k == KD - 1 and xs == 1))
                last.then_inc(h_psum, 1)

            count(0)
            c_transposes(0)
            part_transposes(0)
            pe.wait_ge(w_lo_ready, 2)
            with pe.Fori(1, NT) as t:
                count(t)
                h_products(t - 1)
                c_transposes(t)
                part_transposes(t)
            h_products(NT - 1)
            pe.wait_ge(c_stored, NT * CG)

            def row_products(n, w):
                pe.wait_ge(diag_ready, n)
                for g in range(-(-w // 512)):
                    c = min(512, w - 512 * g)
                    last = t_.matmul(PS[:, g, 0:c], ones[:], diag[:, 512 * g:512 * g + c], start=True, stop=True)
                last.then_inc(row_psum, 1)

            def agg_products(i, j):
                pe.wait_ge(at_ready, done(i + j))
                pe.wait_ge(x_updated, freed(i + j))
                for t in range(NT):
                    for g in range(2):
                        t_.matmul(PS[:, 3 * j + g, :], AT[:, j, t, :], hbuf[:, t, g * HD:(g + 1) * HD],
                                  start=(t == 0), stop=(t == NT - 1))
                pe.wait_ge(at_summed, i + (j + 1))
                t_.matmul(PS[:, 3 * j + 2, 0:1], at_sum[:, j, :], ones[:, 0:1],
                          start=True, stop=True).then_inc(agg_psum, 1)

            pe.wait_ge(h_ready, NT)
            row_products(1, NP)
            pe.wait_ge(row_stored, 1)
            def ffn_weight_transposes(i, j):
                pe.wait_ge(w_rounded, done(i + j))
                pe.wait_ge(wT_stored, freed(i + j))
                bank = PS[:, 6 + j, :].bitcast(BF16).rearrange("p (k n) -> p k n", n=P)
                if isinstance(i, int) and i >= 2 * FC:
                    for r in range(2):
                        for c in range(FC):
                            n = min(P, FF - c * P)
                            last = t_.transpose(bank[0:n, r * FC + c, :],
                                                w_q[:, j, r * FF + c * P:r * FF + c * P + n], identb[:])
                else:
                    for k in range(KD):
                        last = t_.transpose(bank[:, k, :], w_q[:, j, k * P:(k + 1) * P], identb[:])
                last.then_inc(wT_psum, 1)

            with pairs(pe, 2 * FC) as i:
                agg_products(i, 0)
                agg_products(i, 1)
                ffn_weight_transposes(i, 0)
                ffn_weight_transposes(i, 1)
            for i in range(2 * FC, NT, 2):
                agg_products(i, 0)
                agg_products(i, 1)
                ffn_weight_transposes(i, 0)
                ffn_weight_transposes(i, 1)

            def y_transposes(t, j):
                pe.wait_ge(yq_ready, done(t + j))
                pe.wait_ge(yT_stored, freed(t + j))
                bank = PS[:, 4 + j, :].bitcast(BF16).rearrange("p (k n) -> p k n", n=P)
                for k in range(KD):
                    last = t_.transpose(bank[:, k, :], xq_stage[:, j, k * P:(k + 1) * P], identb[:])
                last.then_inc(yT_psum, 1)

            pe.wait_ge(x_updated, NT + CREDIT)
            with pairs(pe, NT) as t:
                y_transposes(t, 0)
                y_transposes(t, 1)

            pe.wait_ge(yT_stored, NT + CREDIT)
            pe.wait_ge(wT_stored, W_ITEMS + CREDIT)
            with pairs(pe, NG) as g:
                for n in range(2 * FC):
                    i, c, j = n // FC, n % FC, n % 2
                    pe.wait_ge(hT_ready, freed(g * FC + n))
                    for s in range(2):
                        for k in range(KD):
                            last = t_.matmul(PS[:, 2 * j + s, 0:GN], wguT[:, k, s, c * P:(c + 1) * P],
                                             xqT[:, k, bass.ds((g + i) * GN, GN)], start=(k == 0), stop=(k == KD - 1))
                    last.then_inc(gu_psum, 1)

            pe.wait_ge(hT_ready, FC * NG + CREDIT)
            row_products(2, D)
            pe.wait_ge(hq_ready, 1)
            pe.wait_ge(row_stored, 2)

            def down_products(t, j):
                pe.wait_ge(d_scaled, freed(t + j))
                for c in range(FC):
                    n = min(P, FF - c * P)
                    for g in range(2):
                        last = t_.matmul(PS[:, 2 * j + g, :], hq[0:n, c, bass.ds((t + j) * P, P)],
                                         wdT[0:n, c, g * HD:(g + 1) * HD], start=(c == 0), stop=(c == FC - 1))
                last.then_inc(d_psum, 1)

            with pairs(pe, NT) as t:
                down_products(t, 0)
                down_products(t, 1)

            def part_transposes2(t, j):
                pe.wait_ge(lo2_ready, done(t + j))
                pe.wait_ge(parts2T_ready, freed(t + j))
                b = j % 2
                for s in range(2):
                    bank = PS[:, 4 + 2 * b + s, :].bitcast(F16)
                    for k in range(KD):
                        last = t_.transpose(bank[:, k * P:(k + 1) * P], parts2[:, b, s, k * P:(k + 1) * P], identh[:])
                last.then_inc(parts2_psum, 1)

            def x1_products(t, j):
                pe.wait_ge(parts2T_ready, done(t + j))
                pe.wait_ge(x1_ready, freed(t + j))
                for k in range(KD):
                    for xs, w in ((0, W1_hi), (0, W1_lo), (1, W1_hi)):
                        last = t_.matmul(PS[:, j % 2, :], partsT2[:, j % 2, xs, k, :], w[:, k, :],
                                         start=(k == 0 and w is W1_hi and xs == 0), stop=(k == KD - 1 and xs == 1))
                last.then_inc(x1_psum, 1)

            pe.wait_ge(d_scaled, NT + CREDIT)
            pe.wait_ge(w1_lo_ready, 1)

            def u_product(k, t, j):
                pe.wait_ge(diag2_ready, done(t + (j + k * NT)))
                pe.wait_ge(u_stored, t + (j + k * NT + CREDIT))
                t_.matmul(PS[:, 2, 0:P], ones[:], u_diag[:, j % 2, :], start=True, stop=True).then_inc(u_psum, 1)

            part_transposes2(0, 0)
            part_transposes2(0, 1)
            x1_products(0, 0)
            with pairs(pe, NT - 2) as t:
                for j in range(2):
                    part_transposes2(t, j + 2)
                    x1_products(t, j + 1)
                    u_product(0, t, j)
            x1_products(NT - 2, 1)
            u_product(0, NT - 2, 0)

            def edge_products(k, c, j):
                first = isinstance(c, int) and c + j == 0
                if first:
                    pe.wait_ge(early_lo, k + 1)
                    pe.wait_ge(gs_ready, k * NT + FT + CREDIT)
                else:
                    pe.wait_ge(aw_lo_ready, done(c + (k * NT + j)))
                pe.wait_ge(g_ready, freed(c + (k * NT + j)))
                q, j = (k + 1) % 2, j % 2
                for t in range(NT):
                    if first and t == FT:
                        pe.wait_ge(aw_lo_ready, done(k * NT))
                        pe.wait_ge(gs_ready, (k + 1) * NT + CREDIT)
                    for s in range(2):
                        t_.matmul(PS[:, 3 + j, :], AP[:, j, 0, t, :], GS[:, q, s, t, :],
                                  start=(t == 0 and s == 0), stop=(t == NT - 1 and s == 1))
                    last = t_.matmul(PS[:, 5 + j, :], AP[:, j, 1, t, :], GS[:, q, 0, t, :],
                                     start=(t == 0), stop=(t == NT - 1))
                last.then_inc(agg2_psum, 1)

            for k in range(K1 - 1):
                edge_products(k, 0, 0)
                u_product(k, NT - 2, 1)
                with pairs(pe, NT - 2) as c:
                    for j in range(2):
                        edge_products(k, c, j + 1)
                        u_product(k + 1, c, j)
                edge_products(k, NT - 2, 1)
                u_product(k + 1, NT - 2, 0)

            def x_transposes(t, j):
                pe.wait_ge(xcopy_ready, done(t + j))
                pe.wait_ge(xT_ready, t + (j + CREDIT))
                for k in range(KD):
                    last = t_.transpose(PS[:, k // 4, (k % 4) * P:(k % 4 + 1) * P], x_copy[:, k * P:(k + 1) * P],
                                        ident[:])
                last.then_inc(xT_psum, 1)

            def logit_products(t, j):
                pe.wait_ge(xT_ready, done(t + j))
                pe.wait_ge(lg_ready, t + (j + CREDIT))
                for k in range(KD):
                    last = t_.matmul(PS[:, 7, 0:NE], xT[:, j % 2, k, :], gwT[:, k, :],
                                     start=(k == 0), stop=(k == KD - 1))
                last.then_inc(lg_psum, 1)

            k = K1 - 1
            edge_products(k, 0, 0)
            u_product(k, NT - 2, 1)
            pe.wait_ge(gw_in, 16)
            for i in range(KD):
                last = t_.transpose(PS[:, 7, i * NE:(i + 1) * NE], gw_raw[:, i * P:(i + 1) * P], ident[0:NE, 0:NE])
            last.then_inc(gwT_psum, 1)
            edge_products(k, 0, 1)
            pe.wait_ge(gwT_ready, 1)
            for i in range(KD):
                last = t_.matmul(PS[:, 7, 0:NE], ones[:], gwT[:, i, :], start=(i == 0), stop=(i == KD - 1))
            last.then_inc(gws_psum, 1)
            x_transposes(0, 0)
            pe.wait_ge(gws_ready, 1)
            with pairs(pe, NT - 2) as c:
                for j in range(2):
                    edge_products(k, c, j + 2)
                    logit_products(c, j)
                    x_transposes(c, j + 1)
            logit_products(NT - 2, 0)
            x_transposes(NT - 2, 1)
            logit_products(NT - 2, 1)

            pe.wait_ge(g_ready, K1 * NT + CREDIT)
            pe.wait_ge(mask_ready, 1)
            chosen = route(1).rearrange("p t e -> p (t e)")
            t_.matmul(PS[:, 3, 0:NT * NE], tri[:], chosen, start=True, stop=True)
            t_.matmul(PS[:, 4, 0:NT * NE], ones[:], chosen, start=True, stop=True).then_inc(rank_psum, 1)
            pe.wait_ge(cast_ready, 1)
            for t in range(NT):
                last = t_.matmul(PS[0:CAP, 5, 0:NR], slot_of[:, t, :], facts[:, t, :, :].rearrange("p q e -> p (q e)"),
                                 start=(t == 0), stop=(t == NT - 1))
            last.then_inc(slots_psum, 1)
            pe.wait_ge(slots_ready, 1)

            def in_transposes(e, j):
                pe.wait_ge(xgn_ready, done(e + j))
                pe.wait_ge(xgT_ready, e + (j + CREDIT))
                for k in range(KD):
                    last = t_.transpose(PS[:, k // 4, (k % 4) * CAP:(k % 4 + 1) * CAP],
                                        xgn[:, j % 2, k * P:(k + 1) * P], ident[0:CAP, 0:CAP])
                last.then_inc(xgT_psum, 1)

            def into_experts(e, j):
                pe.wait_ge((we1_in0, we1_in1)[j % 2], (e + j) // 2 * 16 + 32)
                pe.wait_ge(xgT_ready, done(e + j))
                pe.wait_ge(ge_ready, freed(e + j))
                w = W1E[:, bass.ds(3 - (e + j) % 4, 1)].squeeze(1)
                for k in range(KD):
                    last = t_.matmul(PS[0:CAP, 2 + j % 2, :], xgT[:, j % 2, k, :], w[:, k, :],
                                     start=(k == 0), stop=(k == KD - 1))
                last.then_inc(m1_psum, 1)

            def out_transposes(e, j):
                pe.wait_ge(ge_ready, done(e + j))
                pe.wait_ge(geT_ready, e + (j + CREDIT))
                for k in range(4):
                    last = t_.transpose(PS[:, 4, k * CAP:(k + 1) * CAP], ge[:, j % 2, k * P:(k + 1) * P],
                                        ident[0:CAP, 0:CAP])
                last.then_inc(geT_psum, 1)

            def out_of_experts(e, j):
                pe.wait_ge((we2_in0, we2_in1)[j % 2], (e + j) // 2 * 16 + 32)
                pe.wait_ge(geT_ready, done(e + j))
                pe.wait_ge(o_ready, e + (j + CREDIT))
                w = W2E[:, bass.ds(3 - (e + j) % 4, 1)].squeeze(1)
                for k in range(4):
                    for g in range(2):
                        last = t_.matmul(PS[0:CAP, 5 + g, :], geT[:, j % 2, k, :], w[:, k, g * HD:(g + 1) * HD],
                                         start=(k == 0), stop=(k == 3))
                last.then_inc(m2_psum, 1)

            in_transposes(0, 0)
            into_experts(0, 0)
            in_transposes(0, 1)
            out_transposes(0, 0)
            with pe.Fori(0, NE - 3, 2) as e:
                for j in (1, 2):
                    into_experts(e, j)
                    in_transposes(e, j + 1)
                    out_of_experts(e, j - 1)
                    out_transposes(e, j)
            into_experts(NE - 2, 1)
            out_of_experts(NE - 2, 0)
            out_transposes(NE - 2, 1)
            out_of_experts(NE - 2, 1)


_INS = ['x', 'src', 'dst', 'L0_gnn_W', 'L0_gnn_a', 'L0_ffn_clip_x', 'L0_ffn_clip_down', 'L0_ffn_w_gate',
        'L0_ffn_w_up', 'L0_ffn_w_down', 'L1_gnn_W1', 'L1_gnn_b1', 'L1_gnn_Wg', 'L1_gnn_bg',
        'L1_ffn_gate_w', 'L1_ffn_w1', 'L1_ffn_w2']


def build(nc, args):
    n, d = args[0].shape
    out = nc.dram_tensor("out_0_dram", (n, d), F32, kind="ExternalOutput").ap()
    x_rows = nc.dram_tensor("x_rows", (n, d), F32).ap()
    gnn_moe_kernel(nc, *args, out, x_rows)


def kernel(**inputs):
    import numpy as np
    from concourse import bacc
    from concourse.bass_utils import run_bass_kernel_spmd

    nc = bacc.Bacc("TRN2", target_bir_lowering=False, num_devices=1, dynamic_dma_scratch_size=4096)
    arrays, args = {}, []
    for name in _INS:
        a = np.ascontiguousarray(inputs[name])
        arrays[f"in_{name}_dram"] = a
        args.append(nc.dram_tensor(f"in_{name}_dram", a.shape, mybir.dt.from_np(a.dtype), kind="ExternalInput").ap())
    build(nc, args)
    r = run_bass_kernel_spmd(nc, [arrays], core_ids=[0])
    return r.results[0]["out_0_dram"]
```
